# Optimizing a Trainium2 kernel written in Bass

```python
import numpy as np
import jax
import jax.numpy as jnp

def _softmax(x, axis=-1):
    return jax.nn.softmax(x, axis=axis)

def _gelu(x):
    return jax.nn.gelu(x, approximate=True)

def _silu(x):
    return jax.nn.silu(x)

def _sigmoid(x):
    return jax.nn.sigmoid(x)

def _layernorm(x, axis=-1, eps=1e-05):
    m = jnp.mean(x, axis=axis, keepdims=True)
    v = jnp.var(x, axis=axis, keepdims=True)
    return (x - m) / jnp.sqrt(v + eps)

def _scatter_add(tgt, idx, src, axis=0):
    return tgt.at[idx].add(src)

def _segment_sum(src, seg, n):
    return jax.ops.segment_sum(src, seg, n)
kernel_name = 'mk_gnn_preln_d2_gnn_r32_57a91c'

def setup_inputs(seed: int=0):
    np.random.seed(seed)
    _w = jnp.asarray

    def _rec_inputs():
        import jax
        import jax.numpy as jnp
        _gk = jax.random.key(seed)
        x = -0.000202 + 1 * jax.random.normal(jax.random.fold_in(_gk, 1), (50000, 128), jnp.float32)
        src = jax.random.randint(jax.random.fold_in(_gk, 2), (50000,), 0, 50000, jnp.int32)
        dst = jnp.minimum((50000 * jax.random.uniform(jax.random.fold_in(_gk, 3), (50000,)) ** 2.0).astype(jnp.int32), 49999)
        _o = jnp.argsort(dst, stable=True)
        src = src[_o]
        dst = dst[_o]
        edge_attr_4 = 0.000714719 + 1.00021 * jax.random.normal(jax.random.fold_in(_gk, 11), (50000, 4), jnp.float32)
        edge_weight = jax.random.uniform(jax.random.fold_in(_gk, 13), (50000,), jnp.float32, 0.0, 0.999998)
        return (x, src, dst, edge_attr_4, edge_weight)
    x, src, dst, edge_attr_4, edge_weight = _rec_inputs()

    def _L0_gnn_setup():
        import jax, jax.numpy as jnp
        import numpy as np
        N = 50000
        E = 25000
        HID = 128
        H = 4
        C = HID // H
        ED = 4

        def layer_norm(x, g, b, eps=1e-05):
            mu = jnp.mean(x, axis=-1, keepdims=True)
            var = jnp.mean(jnp.square(x - mu), axis=-1, keepdims=True)
            return (x - mu) * jax.lax.rsqrt(var + eps) * g + b

        def transformer_conv(h, edge_index, edge_attr, Wq, bq, Wk, bk, Wv, bv, We, Wskip, bskip, Wbeta):
            src, dst = (edge_index[0], edge_index[1])
            n = h.shape[0]
            q = (h @ Wq.T + bq).reshape(n, H, C)
            k = (h @ Wk.T + bk).reshape(n, H, C)
            v = (h @ Wv.T + bv).reshape(n, H, C)
            e = (edge_attr @ We.T).reshape(-1, H, C)
            k_j = k[src] + e
            v_j = v[src] + e
            alpha = jnp.einsum('ehc,ehc->eh', q[dst], k_j) / np.sqrt(C)
            m = jax.ops.segment_max(alpha, dst, num_segments=n)
            a = jnp.exp(alpha - m[dst])
            denom = jax.ops.segment_sum(a, dst, num_segments=n) + 1e-16
            a = a / denom[dst]
            out = jax.ops.segment_sum(a[:, :, None] * v_j, dst, num_segments=n)
            out = out.reshape(n, H * C)
            skip = h @ Wskip.T + bskip
            beta = jax.nn.sigmoid(jnp.concatenate([out, skip, out - skip], axis=-1) @ Wbeta.T)
            return beta * skip + (1.0 - beta) * out
        key = jax.random.key(seed)
        ks = jax.random.split(key, 16)
        s = 0.05
        rn = lambda k, shape: jax.random.normal(k, shape, jnp.float32) * s
        z = lambda n: jnp.zeros((n,), jnp.float32)
        return {'x': jax.random.normal(ks[0], (N, HID), jnp.float32), 'edge_index': jax.random.randint(ks[1], (2, E), 0, N, dtype=jnp.int32), 'edge_attr': jax.random.normal(ks[2], (E, ED), jnp.float32), 'ln1_g': jnp.ones((HID,), jnp.float32), 'ln1_b': z(HID), 'Wq': rn(ks[3], (HID, HID)), 'bq': z(HID), 'Wk': rn(ks[4], (HID, HID)), 'bk': z(HID), 'Wv': rn(ks[5], (HID, HID)), 'bv': z(HID), 'We': rn(ks[6], (HID, ED)), 'Wskip': rn(ks[7], (HID, HID)), 'bskip': z(HID), 'Wbeta': rn(ks[8], (1, 3 * HID)), 'ln2_g': jnp.ones((HID,), jnp.float32), 'ln2_b': z(HID), 'W1': rn(ks[9], (4 * HID, HID)), 'b1': z(4 * HID), 'W2': rn(ks[10], (HID, 4 * HID)), 'b2': z(HID)}
    _L0_gnn_all = _L0_gnn_setup()
    _L0_gnn_in = {k: v for k, v in _L0_gnn_all.items() if k in ('ln1_g', 'ln1_b', 'Wq', 'bq', 'Wk', 'bk', 'Wv', 'bv', 'We', 'Wskip', 'bskip', 'Wbeta', 'ln2_g', 'ln2_b', 'W1', 'b1', 'W2', 'b2')}
    del _L0_gnn_all

    def _L1_gnn_setup():
        import jax, jax.numpy as jnp
        import numpy as np
        N_NODES = 3125
        N_EDGES = 31250
        EMB_DIM = 128
        NEG_SLOPE = 0.01
        key = jax.random.key(seed)
        k1, k2, k3, k4 = jax.random.split(key, 4)
        x = jax.random.normal(k1, (N_NODES, EMB_DIM), dtype=jnp.float32)
        edge_index = jax.random.randint(k2, (2, N_EDGES), 0, N_NODES, dtype=jnp.int64)
        edge_attrs = jax.random.uniform(k3, (N_EDGES,), dtype=jnp.float32)
        limit = float(np.sqrt(6.0 / (EMB_DIM + EMB_DIM)))
        W1_w = jax.random.uniform(k4, (EMB_DIM, EMB_DIM), dtype=jnp.float32, minval=-limit, maxval=limit)
        W1_b = jnp.zeros((EMB_DIM,), dtype=jnp.float32)
        return {'x': x, 'edge_index': edge_index, 'edge_attrs': edge_attrs, 'W1_w': W1_w, 'W1_b': W1_b}
    _L1_gnn_all = _L1_gnn_setup()
    _L1_gnn_in = {k: v for k, v in _L1_gnn_all.items() if k in ('W1_w', 'W1_b')}
    del _L1_gnn_all
    return {'x': x, 'src': src, 'dst': dst, 'edge_attr_4': edge_attr_4, 'edge_weight': edge_weight, 'L0_gnn_ln1_g': _L0_gnn_in['ln1_g'], 'L0_gnn_ln1_b': _L0_gnn_in['ln1_b'], 'L0_gnn_Wq': _L0_gnn_in['Wq'], 'L0_gnn_bq': _L0_gnn_in['bq'], 'L0_gnn_Wk': _L0_gnn_in['Wk'], 'L0_gnn_bk': _L0_gnn_in['bk'], 'L0_gnn_Wv': _L0_gnn_in['Wv'], 'L0_gnn_bv': _L0_gnn_in['bv'], 'L0_gnn_We': _L0_gnn_in['We'], 'L0_gnn_Wskip': _L0_gnn_in['Wskip'], 'L0_gnn_bskip': _L0_gnn_in['bskip'], 'L0_gnn_Wbeta': _L0_gnn_in['Wbeta'], 'L0_gnn_ln2_g': _L0_gnn_in['ln2_g'], 'L0_gnn_ln2_b': _L0_gnn_in['ln2_b'], 'L0_gnn_W1': _L0_gnn_in['W1'], 'L0_gnn_b1': _L0_gnn_in['b1'], 'L0_gnn_W2': _L0_gnn_in['W2'], 'L0_gnn_b2': _L0_gnn_in['b2'], 'L1_gnn_W1_w': _L1_gnn_in['W1_w'], 'L1_gnn_W1_b': _L1_gnn_in['W1_b']}

def reference(x, src, dst, edge_attr_4, edge_weight, L0_gnn_ln1_g, L0_gnn_ln1_b, L0_gnn_Wq, L0_gnn_bq, L0_gnn_Wk, L0_gnn_bk, L0_gnn_Wv, L0_gnn_bv, L0_gnn_We, L0_gnn_Wskip, L0_gnn_bskip, L0_gnn_Wbeta, L0_gnn_ln2_g, L0_gnn_ln2_b, L0_gnn_W1, L0_gnn_b1, L0_gnn_W2, L0_gnn_b2, L1_gnn_W1_w, L1_gnn_W1_b):
    import jax
    import jax.numpy as jnp

    def _L0_gnn_ref(x, edge_index, edge_attr, ln1_g, ln1_b, Wq, bq, Wk, bk, Wv, bv, We, Wskip, bskip, Wbeta, ln2_g, ln2_b, W1, b1, W2, b2):
        import jax, jax.numpy as jnp
        import numpy as np
        N = 50000
        E = 25000
        HID = 128
        H = 4
        C = HID // H
        ED = 4

        def layer_norm(x, g, b, eps=1e-05):
            mu = jnp.mean(x, axis=-1, keepdims=True)
            var = jnp.mean(jnp.square(x - mu), axis=-1, keepdims=True)
            return (x - mu) * jax.lax.rsqrt(var + eps) * g + b

        def transformer_conv(h, edge_index, edge_attr, Wq, bq, Wk, bk, Wv, bv, We, Wskip, bskip, Wbeta):
            src, dst = (edge_index[0], edge_index[1])
            n = h.shape[0]
            q = (h @ Wq.T + bq).reshape(n, H, C)
            k = (h @ Wk.T + bk).reshape(n, H, C)
            v = (h @ Wv.T + bv).reshape(n, H, C)
            e = (edge_attr @ We.T).reshape(-1, H, C)
            k_j = k[src] + e
            v_j = v[src] + e
            alpha = jnp.einsum('ehc,ehc->eh', q[dst], k_j) / np.sqrt(C)
            m = jax.ops.segment_max(alpha, dst, num_segments=n)
            a = jnp.exp(alpha - m[dst])
            denom = jax.ops.segment_sum(a, dst, num_segments=n) + 1e-16
            a = a / denom[dst]
            out = jax.ops.segment_sum(a[:, :, None] * v_j, dst, num_segments=n)
            out = out.reshape(n, H * C)
            skip = h @ Wskip.T + bskip
            beta = jax.nn.sigmoid(jnp.concatenate([out, skip, out - skip], axis=-1) @ Wbeta.T)
            return beta * skip + (1.0 - beta) * out
        h = transformer_conv(layer_norm(x, ln1_g, ln1_b), edge_index, edge_attr, Wq, bq, Wk, bk, Wv, bv, We, Wskip, bskip, Wbeta)
        x = x + h
        h2 = layer_norm(x, ln2_g, ln2_b)
        h2 = jax.nn.relu(h2 @ W1.T + b1) @ W2.T + b2
        return x + h2

    def _L1_gnn_ref(x, edge_index, edge_attrs, W1_w, W1_b):
        import jax, jax.numpy as jnp
        import numpy as np
        N_NODES = 3125
        N_EDGES = 31250
        EMB_DIM = 128
        NEG_SLOPE = 0.01
        n = x.shape[0]
        from_, to_ = (edge_index[0], edge_index[1])
        deg = jax.ops.segment_sum(jnp.ones((to_.shape[0],), dtype=x.dtype), to_, num_segments=n)
        deg_inv = jnp.where(deg > 0, 1.0 / jnp.sqrt(deg), 0.0)
        norm = deg_inv[from_] * deg_inv[to_]
        x_i = x[from_]
        x_j = x[to_]
        m_j = norm[:, None] * (x_j + x_j * x_i @ W1_w.T + W1_b)
        out = jax.ops.segment_sum(m_j, to_, num_segments=n)
        out = jnp.where(out >= 0, out, NEG_SLOPE * out)
        return out
    edge_index = jnp.stack([src, dst])
    h = jnp.maximum(_layernorm(x, axis=-1), 0.0)
    x = x + _L0_gnn_ref(h, edge_index, edge_attr_4, L0_gnn_ln1_g, L0_gnn_ln1_b, L0_gnn_Wq, L0_gnn_bq, L0_gnn_Wk, L0_gnn_bk, L0_gnn_Wv, L0_gnn_bv, L0_gnn_We, L0_gnn_Wskip, L0_gnn_bskip, L0_gnn_Wbeta, L0_gnn_ln2_g, L0_gnn_ln2_b, L0_gnn_W1, L0_gnn_b1, L0_gnn_W2, L0_gnn_b2)
    h = jnp.maximum(_layernorm(x, axis=-1), 0.0)
    x = x + _L1_gnn_ref(h, edge_index, edge_weight, L1_gnn_W1_w, L1_gnn_W1_b)
    return x

_drawn_inputs = setup_inputs


def setup_inputs(seed=0):
    import zlib

    import numpy as np

    out = dict(_drawn_inputs(seed))
    spreads = {'L0_gnn_ln1_g': (1.0, 0.2),
     'L0_gnn_ln1_b': (0.0, 0.279),
     'L0_gnn_bq': (0.0, 2.0),
     'L0_gnn_bk': (0.0, 2.0),
     'L0_gnn_bv': (0.0, 0.317),
     'L0_gnn_bskip': (0.0, 0.1),
     'L0_gnn_ln2_g': (1.0, 0.2),
     'L0_gnn_ln2_b': (0.0, 0.299),
     'L0_gnn_b1': (0.0, 0.1),
     'L0_gnn_b2': (0.0, 0.1),
     'L1_gnn_W1_b': (0.0, 0.38)}
    factors = {'L0_gnn_Wq': 3.326, 'L0_gnn_Wk': 3.336}
    for name, (base, spread) in spreads.items():
        noise = np.random.default_rng([zlib.crc32(name.encode()), seed]).standard_normal(out[name].shape)
        drawn = base * np.exp(spread * noise) if base else spread * noise
        out[name] = jnp.asarray(drawn.astype(out[name].dtype))
    for name, factor in factors.items():
        out[name] = (out[name] * factor).astype(out[name].dtype)
    return out
```

```python
from contextlib import ExitStack, contextmanager

import numpy as np

import concourse.bass as bass
from concourse import mybir

F32 = mybir.dt.float32
I32 = mybir.dt.int32
U16 = mybir.dt.uint16
BF16 = mybir.dt.bfloat16
ALU = mybir.AluOpType
ACT = mybir.ActivationFunctionType
AX = mybir.AxisListType

P = 128
D = 128
H = 4
C = D // H
ED = 4
FF = 4 * D
G = 8
GR = G * P
META = ED + 2
MSG = D + H
ROW0 = MSG + H
ROW1 = D + 1
EPS = 1e-5
NEG = -3.0e38
FAR = 1.0e6
SCALE = float(C) ** -0.5


def at_least(eng, sem, value):
    if isinstance(value, int) and value <= 0:
        return
    eng.wait_ge(sem, value)


def hold(eng, sem):
    eng.sem_inc(sem, 1)


def pipeline(eng, n, depth, half):
    def at(g):
        return (g, g % 2, g // 2) if 0 <= g < n else None

    start, end = depth // 2 + 1, (n - 1) // 2
    assert end > start
    for step in range(2 * start):
        half(*[at(step - d) for d in range(depth)])
    with eng.Fori(start, end) as i:
        for odd in range(2):
            half(*[(2 * i + (odd - d), (odd - d) % 2, i + (odd - d) // 2) for d in range(depth)])
    for step in range(2 * end, n + depth - 1):
        half(*[at(step - d) for d in range(depth)])


class Chain:

    def __init__(self, eng, sem, base=0):
        self.eng, self.sem, self.base, self.k = eng, sem, base, 0

    def mark(self, ins):
        ins.then_inc(self.sem, 1)
        self.k += 1

    def wait(self):
        self.eng.wait_ge(self.sem, self.base + self.k)

    def step(self, ins):
        self.mark(ins)
        self.wait()


def build(nc, x, src, dst, ea, ln1g, ln1b, wq, bq, wk, bk, wv, bv, we, wskip, bskip, wbeta,
          ln2g, ln2b, w1, b1, w2, b2, wl, bl, out):
    N, E = x.shape[0], src.shape[0]
    NGN = -(-N // GR)
    NGE = -(-E // (2 * GR)) * 2
    TE, EP = NGE * G, NGE * GR
    HI = N // P + 1
    RB = max(r for r in range(16, P + 1, 16) if TE % r == 0)
    NB = TE // RB
    HB = -(-HI // P)
    assert N >= 3 * GR and NGE >= 4 and E % 16 == 0 and N < 65536 and TE <= 512 and HI <= 512

    def first_row(g):
        return N - GR if isinstance(g, int) and g == NGN - 1 else g * GR

    def dram(name, shape, dt=F32):
        return nc.dram_tensor(name, shape, dt, kind="Internal").ap()

    dst_pad = dram("dst_pad", [EP + 2], I32)
    src_pad = dram("src_pad", [EP], I32)
    ea_pad = dram("ea_pad", [EP, ED])
    dst16 = dram("dst16", [EP], U16)
    pen_f = dram("pen_f", [EP])
    pen_b = dram("pen_b", [EP])
    through_d = dram("through_d", [TE])
    z_table = dram("z_table", [N + 1, D])
    rows0 = dram("rows0", [EP + 1, ROW0])
    rows1 = dram("rows1", [EP + 1, ROW1])
    x1_table = dram("x1_table", [N, D])
    h2_table = dram("h2_table", [N, ROW1])
    node_row_d = dram("node_row_d", [HI * P], I32)
    dinv_d = dram("dinv_d", [HI * P])

    with ExitStack() as top:
        def sb(name, shape, dt=F32, ctx=top):
            return ctx.enter_context(nc.sbuf_tensor(name, shape, dt))

        def sem(name, ctx=top):
            return ctx.enter_context(nc.semaphore(name))

        @contextmanager
        def phase():
            made = []

            def sem_of_phase(name):
                made.append(nc.alloc_semaphore(name))
                return made[-1]

            with ExitStack() as ctx:
                yield ctx, lambda name, shape, dt=F32: sb(name, shape, dt, ctx), sem_of_phase
            nc.clear_and_free_semaphores(made)
            nc.all_engine_barrier()

        held = sem("held")
        ident = sb("ident", [P, P])
        tri = sb("tri", [P, P])
        ones = sb("ones", [P, P])
        src_col = sb("src_col", [P, TE], I32)
        dst_col = sb("dst_col", [P, TE], I32)
        lohi = sb("lohi", [P, TE, 2])
        meta = sb("meta", [P, TE, META])
        iota16 = sb("iota16", [P, 512], U16)
        stats = sb("stats", [P, NGN, 4, G])
        stats2 = sb("stats2", [P, NGN, 2, G])
        deg = sb("deg", [P, HI])
        wq_t = sb("wq_t", [P, D])
        wkv_t = sb("wkv_t", [P, 2 * D])
        wsk_t = sb("wsk_t", [P, D + 1])
        w1_t = sb("w1_t", [P, FF])
        w2_t = sb("w2_t", [P, 4, D])
        wl_t = sb("wl_t", [P, D])
        wea = sb("wea", [G * META, G, 2 * D])
        bq_row = sb("bq_row", [P, D])
        bsk_row = sb("bsk_row", [P, D + 1])
        b1_col = sb("b1_col", [P, 4])
        b2_row = sb("b2_row", [P, D])
        bl_row = sb("bl_row", [P, D])
        wa_row = sb("wa_row", [P, D])
        half_neg = sb("half_neg", [P, 512])
        headmap = sb("headmap", [H, D])
        fix_at = sb("fix_at", [RB, NB], I32)
        through = sb("through", [P, TE])
        node_row = sb("node_row", [P, NGN, G], I32)
        dinv = sb("dinv", [P, NGN, G])

        with phase() as (ctx, t, s):
            pad_i = t("pad_i", [16, (EP - E + 16) // 16 + 1], I32)
            pad_z = t("pad_z", [16, (EP - E) * ED // 16])
            front = t("front", [1, 1], I32)
            dstw = t("dstw", [RB, NB, P + 2], I32)
            srcw = t("srcw", [RB, NB, P], I32)
            eaw = t("eaw", [RB, NB, P * ED])
            dstf = t("dstf", [RB, NB, P + 2])
            srcf = t("srcf", [RB, NB, P])
            d16 = t("d16", [RB, NB, P], U16)
            pf = t("pf", [RB, NB, P])
            pb = t("pb", [RB, NB, P])
            eq = t("eq", [RB, NB, P])
            cont = t("cont", [RB, NB])
            count = t("count", [RB, NB])
            thr = t("thr", [RB, NB])
            at0 = t("at0", [RB, NB])
            at1 = t("at1", [RB, NB])
            lohi_i = t("lohi_i", [P, TE, 2], I32)
            iota32 = t("iota32", [P, 512], I32)
            zrow = t("zrow", [1, ROW0])
            raw = t("raw", [P, 9, D])
            raw2 = t("raw2", [P, FF])
            rawe = t("rawe", [P, ED])
            gcol = t("gcol", [P, 2])
            bcol = t("bcol", [P, 2])
            b1raw = t("b1raw", [P, 4])
            bcast = t("bcast", [P, 2, D])
            brow = t("brow", [P, 6, D])
            wb = t("wb", [P, 3, D])
            plain = t("plain", [P, 8, D])
            tmp = t("tmp", [P, D])
            wb_row = t("wb_row", [P, D])
            bkv = t("bkv", [P, 2, D])
            wea1 = t("wea1", [META, 2 * D])
            we_sb = t("we_sb", [ED, D])
            pbank = [ctx.enter_context(nc.psum_tensor(f"pset{n}", [P, 512], F32)) for n in range(8)]

            pads_set, padded, edges_in, weights_in = s("pads_set"), s("padded"), s("edges_in"), s("weights_in")
            consts_set, pool_step, dve_step, cols_t = s("consts_set"), s("pool_step"), s("dve_step"), s("cols_t")
            rows_out, thr_out, thr_in, ea_t, w_t = s("rows_out"), s("thr_out"), s("thr_in"), s("ea_t"), s("w_t")
            floats_set, cols_copied, weights_copied, bias_t = s("floats_set"), s("cols_copied"), s("weights_copied"), s("bias_t")
            thr_set, rows_set, wea1_set, wea1_done, wea_done = s("thr_set"), s("rows_set"), s("wea1_set"), s("wea1_done"), s("wea_done")
            ea_copied, we_t = s("ea_copied"), s("we_t")
            loads = [(raw[:, n, :], w) for n, w in enumerate((wq, wk, wv, wskip))]
            loads += [(raw[:, 4:8, :], w1.rearrange("(c p) k -> p c k", p=P)), (raw[:, 8, :], wl), (raw2[:], w2), (rawe[:], we)]
            loads += [(gcol[:, n:n + 1], v.unsqueeze(1)) for n, v in enumerate((ln1g, ln2g))]
            loads += [(bcol[:, n:n + 1], v.unsqueeze(1)) for n, v in enumerate((ln1b, ln2b))]
            loads += [(b1raw[:, n:n + 1], b1[n * P:(n + 1) * P].unsqueeze(1)) for n in range(4)]
            loads += [(brow[:, n, :], v.unsqueeze(0).broadcast_to([P, D])) for n, v in enumerate((bq, bk, bv, bskip, b2, bl))]
            loads += [(wb[:].rearrange("p a b -> p (a b)"), wbeta.broadcast_to([P, 3 * D]))]
            LOADS = 16 * len(loads)
            block = nc.Block()
            with block:
                @block.sync
                def _(sp):
                    sp.dma_start(src_pad[0:E].rearrange("(a b) -> a b", a=16), src.rearrange("(a b) -> a b", a=16)).then_inc(padded, 16)
                    sp.dma_start(dst_pad[1:E + 1].rearrange("(a b) -> a b", a=16), dst.rearrange("(a b) -> a b", a=16)).then_inc(padded, 16)
                    sp.dma_start(ea_pad[0:E, :].rearrange("(a b) j -> a (b j)", a=16), ea.rearrange("(a b) j -> a (b j)", a=16)).then_inc(padded, 16)
                    sp.wait_ge(pads_set, 4)
                    n = (EP - E) // 16
                    sp.dma_start(dst_pad[0:1].unsqueeze(0), front[:]).then_inc(padded, 16)
                    sp.dma_start(dst_pad[E + 1:EP + 1].rearrange("(a b) -> a b", a=16), pad_i[:, 0:n]).then_inc(padded, 16)
                    sp.dma_start(dst_pad[EP + 1:EP + 2].unsqueeze(0), pad_i[0:1, 0:1]).then_inc(padded, 16)
                    sp.dma_start(ea_pad[E:EP, :].rearrange("(a b) j -> a (b j)", a=16), pad_z[:]).then_inc(padded, 16)
                    sp.dma_start(src_pad[E:EP].rearrange("(a b) -> a b", a=16), pad_z[:, 0:n].bitcast(I32)).then_inc(padded, 16)
                    sp.dma_start(z_table[N:N + 1, :], zrow[:, 0:D]).then_inc(padded, 16)
                    sp.dma_start(rows0[EP:EP + 1, :], zrow[:]).then_inc(padded, 16)
                    sp.dma_start(rows1[EP:EP + 1, :], zrow[:, 0:ROW1]).then_inc(padded, 16)
                    sp.wait_ge(padded, 11 * 16)
                    for b in range(NB):
                        window = bass.AP(dst_pad.tensor, b * RB * P, [[P, RB], [1, P + 2]])
                        sp.dma_start(dstw[:, b, :], window).then_inc(edges_in, 16)
                    sp.dma_start(srcw[:], src_pad.rearrange("(b r e) -> r b e", b=NB, r=RB)).then_inc(edges_in, 16)
                    sp.dma_start(eaw[:], ea_pad.rearrange("(b r e) j -> r b (e j)", b=NB, r=RB)).then_inc(edges_in, 16)
                    sp.wait_ge(rows_set, 3)
                    for table, rows in ((dst16, d16), (pen_f, pf), (pen_b, pb)):
                        sp.dma_start(table.rearrange("(b r e) -> r b e", b=NB, r=RB), rows[:]).then_inc(rows_out, 16)
                    sp.wait_ge(thr_set, 1)
                    for b in range(NB):
                        sp.dma_start(through_d[b * RB:(b + 1) * RB].unsqueeze(1), thr[:, b:b + 1]).then_inc(thr_out, 16)
                    sp.wait_ge(thr_out, 16 * NB)
                    sp.dma_start(through[:], through_d.unsqueeze(0).broadcast_to([P, TE])).then_inc(thr_in, 16)
                    sp.wait_ge(wea1_set, 3)
                    for n in range(2):
                        sp.dma_start(wea1[0:ED, n * D:(n + 1) * D], we_sb[:]).then_inc(wea1_done, 16)
                        sp.dma_start(wea1[ED:ED + 1, n * D:(n + 1) * D], bkv[0:1, n, :]).then_inc(wea1_done, 16)
                    sp.wait_ge(wea1_done, 64)
                    for j in range(G):
                        sp.dma_start(wea[j * META:(j + 1) * META, j, :], wea1[:]).then_inc(wea_done, 16)
                    sp.wait_ge(wea_done, 16 * G)
                    sp.wait_ge(thr_in, 16)
                    sp.wait_ge(rows_out, 48)

                @block.scalar
                def _(act):
                    for to, of in loads:
                        act.dma_start(to, of).then_inc(weights_in, 16)
                    act.wait_ge(weights_in, LOADS)

                @block.gpsimd
                def _(pool):
                    chain = Chain(pool, pool_step)
                    g = nc.gpsimd
                    chain.mark(g.memset(ident[:], 0.0))
                    chain.mark(g.memset(tri[:], 1.0))
                    chain.mark(g.memset(headmap[:], 1.0))
                    chain.mark(g.memset(half_neg[:], -0.5))
                    chain.step(g.iota(iota32[:], pattern=[[1, 512]], base=0, channel_multiplier=0))
                    chain.mark(g.affine_select(out=ident[:], in_=ident[:], compare_op=ALU.not_equal, fill=1.0, base=0,
                                               pattern=[[-1, P]], channel_multiplier=1))
                    chain.mark(g.affine_select(out=tri[:], in_=tri[:], compare_op=ALU.is_ge, fill=0.0, base=0,
                                               pattern=[[1, P]], channel_multiplier=-1))
                    chain.step(g.affine_select(out=headmap[:], in_=headmap[:], compare_op=ALU.is_ge, fill=0.0, base=0,
                                               pattern=[[1, D]], channel_multiplier=-C))
                    g.affine_select(out=headmap[:], in_=headmap[:], compare_op=ALU.is_ge, fill=0.0, base=C - 1,
                                    pattern=[[-1, D]], channel_multiplier=C).then_inc(consts_set, 1)
                    g.tensor_copy(iota16[:], iota32[:]).then_inc(consts_set, 1)

                @block.vector
                def _(dve):
                    v = nc.vector
                    chain = Chain(dve, dve_step)
                    v.memset(pad_i[:], N).then_inc(pads_set, 1)
                    v.memset(pad_z[:], 0.0).then_inc(pads_set, 1)
                    v.memset(front[:], -1).then_inc(pads_set, 1)
                    v.memset(zrow[:], 0.0).then_inc(pads_set, 1)
                    chain.mark(v.memset(ones[:], 1.0))
                    chain.mark(v.memset(meta[:], 1.0))
                    chain.mark(v.memset(wea[:], 0.0))
                    v.memset(wea1[:], 0.0).then_inc(wea1_set, 1)
                    dve.wait_ge(edges_in, 16 * (NB + 2))
                    v.tensor_copy(srcf[:], srcw[:]).then_inc(floats_set, 1)
                    v.tensor_copy(dstf[:], dstw[:]).then_inc(floats_set, 1)
                    dve.wait_ge(floats_set, 2)
                    v.tensor_copy(d16[:], dstf[:, :, 1:P + 1]).then_inc(rows_set, 1)
                    chain.mark(v.tensor_tensor(pf[:], dstf[:, :, 1:P + 1], dstf[:, :, 0:P], ALU.not_equal))
                    chain.mark(v.tensor_tensor(pb[:], dstf[:, :, 1:P + 1], dstf[:, :, 2:P + 2], ALU.not_equal))
                    chain.mark(v.tensor_tensor(cont[:], dstf[:, :, 1], dstf[:, :, 0], ALU.is_equal))
                    first = dstf[:, :, 1:2].broadcast_to([RB, NB, P])
                    chain.step(v.tensor_tensor(eq[:], dstf[:, :, 1:P + 1], first, ALU.is_equal))
                    v.tensor_scalar(pf[:], pf[:], NEG, None, ALU.mult).then_inc(rows_set, 1)
                    v.tensor_scalar(pb[:], pb[:], NEG, None, ALU.mult).then_inc(rows_set, 1)
                    chain.step(v.tensor_reduce(count[:], eq[:], AX.X, ALU.add))
                    chain.step(v.tensor_scalar(at0[:], count[:], float(P), None, ALU.is_equal))
                    v.tensor_tensor(thr[:], at0[:], cont[:], ALU.mult).then_inc(thr_set, 1)
                    chain.mark(v.tensor_scalar(at1[:], cont[:], -FAR, FAR, ALU.mult, ALU.add))
                    dve.wait_ge(consts_set, 2)
                    for b in range(NB):
                        dve.wait_ge(cols_t, b + 1)
                        cols = slice(b * RB, (b + 1) * RB)
                        chain.mark(v.tensor_copy(src_col[:, cols], pbank[b % 2][:, 0:RB]))
                        chain.mark(v.tensor_copy(meta[:, cols, META - 1], pbank[b % 2][:, P:P + RB]))
                        v.tensor_copy(dst_col[:, cols], pbank[b % 2][:, P:P + RB]).then_inc(cols_copied, 1)
                    for b in range(NB):
                        dve.wait_ge(ea_t, b + 1)
                        cols = slice(b * RB, (b + 1) * RB)
                        v.tensor_copy(meta[:, cols, 0:ED].rearrange("p r j -> p j r"),
                                      pbank[2 + b % 2][:, :].rearrange("p (j r) -> p j r", j=ED)[:, :, 0:RB]).then_inc(ea_copied, 1)
                    dve.wait_ge(cols_copied, NB)
                    chain.mark(v.tensor_scalar(lohi_i[:, :, 0], dst_col[:], P - 1, None, ALU.bitwise_and))
                    chain.step(v.tensor_scalar(lohi_i[:, :, 1], dst_col[:], 7, None, ALU.logical_shift_right))
                    chain.mark(v.tensor_copy(lohi[:], lohi_i[:]))
                    chain.step(v.tensor_scalar(at0[:], iota16[0:RB, 0:NB], float(RB * P), float(-1 - P), ALU.mult, ALU.add))
                    chain.step(v.tensor_tensor(at0[:], at0[:], at1[:], ALU.add))
                    chain.step(v.tensor_tensor(at0[:], at0[:], count[:], ALU.add))
                    dve.wait_ge(we_t, 2)
                    chain.mark(v.scalar_tensor_tensor(fix_at[:], pbank[6][0:RB, 0:NB], float(P), at0[:], ALU.mult, ALU.add))
                    v.tensor_copy(we_sb[:], pbank[7][0:ED, 0:D]).then_inc(wea1_set, 1)
                    dve.wait_ge(weights_in, LOADS)
                    dve.wait_ge(w_t, 1)
                    chain.mark(v.tensor_copy(plain[:, 0:4, :], pbank[4][:, :].rearrange("p (a b) -> p a b", a=4)))
                    dve.wait_ge(w_t, 2)
                    chain.mark(v.tensor_copy(plain[:, 4:8, :], pbank[5][:, :].rearrange("p (a b) -> p a b", a=4)))
                    dve.wait_ge(w_t, 3)
                    chain.mark(v.tensor_copy(w2_t[:], pbank[0][:, :].rearrange("p (a b) -> p a b", a=4)))
                    dve.wait_ge(w_t, 4)
                    chain.mark(v.tensor_copy(wl_t[:], pbank[1][:, 0:D]))
                    chain.mark(v.tensor_copy(bcast[:, 0, :], bcol[:, 0:1].broadcast_to([P, D])))
                    chain.step(v.tensor_copy(bcast[:, 1, :], bcol[:, 1:2].broadcast_to([P, D])))
                    v.tensor_scalar(wq_t[:], plain[:, 0, :], gcol[:, 0:1], None, ALU.mult).then_inc(weights_copied, 1)
                    chain.mark(v.tensor_scalar(wkv_t[:, 0:D], plain[:, 1, :], gcol[:, 0:1], None, ALU.mult))
                    chain.mark(v.tensor_scalar(wkv_t[:, D:2 * D], plain[:, 2, :], gcol[:, 0:1], None, ALU.mult))
                    chain.mark(v.tensor_scalar(wsk_t[:, 0:D], plain[:, 3, :], gcol[:, 0:1], None, ALU.mult))
                    chain.mark(v.tensor_scalar(w1_t[:], plain[:, 4:8, :].rearrange("p a b -> p (a b)"), gcol[:, 1:2], None, ALU.mult))
                    chain.mark(v.tensor_tensor(wa_row[:], wb[:, 0, :], wb[:, 2, :], ALU.add))
                    chain.step(v.tensor_tensor(wb_row[:], wb[:, 1, :], wb[:, 2, :], ALU.subtract))
                    chain.step(v.tensor_tensor(tmp[:], wsk_t[:, 0:D], wb_row[:], ALU.mult))
                    chain.step(v.tensor_reduce(wsk_t[:, D:D + 1], tmp[:], AX.X, ALU.add))
                    dve.wait_ge(bias_t, 2)
                    chain.mark(v.tensor_tensor(bq_row[:], pbank[2][:, 0:D], brow[:, 0, :], ALU.add))
                    chain.mark(v.tensor_tensor(bsk_row[:, 0:D], pbank[2][:, 3 * D:4 * D], brow[:, 3, :], ALU.add))
                    chain.mark(v.tensor_copy(b2_row[:], brow[:, 4, :]))
                    chain.mark(v.tensor_copy(bl_row[:], brow[:, 5, :]))
                    chain.mark(v.tensor_tensor(b1_col[:], pbank[3][:, 0:4], b1raw[:], ALU.add))
                    v.tensor_tensor(bkv[:].rearrange("p a b -> p (a b)"), pbank[2][:, D:3 * D],
                                    brow[:, 1:3, :].rearrange("p a b -> p (a b)"), ALU.add).then_inc(wea1_set, 1)
                    chain.wait()
                    chain.step(v.tensor_tensor(tmp[:], bsk_row[:, 0:D], wb_row[:], ALU.mult))
                    chain.step(v.tensor_reduce(bsk_row[:, D:D + 1], tmp[:], AX.X, ALU.add))

                @block.tensor
                def _(pe):
                    t_ = nc.tensor
                    pe.wait_ge(consts_set, 1)
                    pe.wait_ge(floats_set, 2)
                    for b in range(NB):
                        if b >= 2:
                            pe.wait_ge(cols_copied, b - 1)
                        t_.transpose(pbank[b % 2][:, 0:RB], srcf[:, b, :], ident[0:RB, 0:RB])
                        t_.transpose(pbank[b % 2][:, P:P + RB], dstf[:, b, 1:P + 1], ident[0:RB, 0:RB]).then_inc(cols_t, 1)
                    for b in range(NB):
                        if b >= 2:
                            pe.wait_ge(ea_copied, b - 1)
                        for j in range(ED):
                            last = t_.transpose(pbank[2 + b % 2][:, j * P:j * P + RB],
                                                eaw[:, b, :].rearrange("r (e j) -> r e j", j=ED)[:, :, j], ident[0:RB, 0:RB])
                        last.then_inc(ea_t, 1)
                    pe.wait_ge(dve_step, 1)
                    t_.matmul(pbank[6][:, 0:P], tri[:], ones[:], start=True, stop=True).then_inc(we_t, 1)
                    pe.wait_ge(weights_in, LOADS)
                    t_.transpose(pbank[7][0:ED, 0:D], rawe[:], ident[:]).then_inc(we_t, 1)
                    for n in range(8):
                        last = t_.transpose(pbank[4 + n // 4][:, n % 4 * D:(n % 4 + 1) * D], raw[:, n, :], ident[:])
                        if n % 4 == 3:
                            last.then_inc(w_t, 1)
                    pe.wait_ge(cols_copied, NB)
                    for n in range(4):
                        last = t_.transpose(pbank[0][:, n * D:(n + 1) * D], raw2[:, n * D:(n + 1) * D], ident[:])
                    last.then_inc(w_t, 1)
                    t_.transpose(pbank[1][:, 0:D], raw[:, 8, :], ident[:]).then_inc(w_t, 1)
                    pe.wait_ge(weights_copied, 1)
                    pe.wait_ge(ea_copied, NB)
                    t_.matmul(pbank[2][:, :], bcast[:, 0, :], plain[:, 0:4, :].rearrange("p a b -> p (a b)"),
                              start=True, stop=True).then_inc(bias_t, 1)
                    for n in range(4):
                        last = t_.matmul(pbank[3][:, n:n + 1], plain[:, 4 + n, :], bcol[:, 1:2], start=True, stop=True)
                    last.then_inc(bias_t, 1)

        with phase() as (ctx, t, s):
            x_sb, h_sb, z_sb = t("xa", [P, 2, G, D]), t("ha", [P, 2, G, D]), t("za", [P, 2, G, D])
            six = t("six", [P, 2, 2, G, 6])
            mv = t("mva", [P, 2, 2, G, 2])
            var = t("vara", [P, 2, 2, G])
            norm = t("norma", [P, 2, 4, G])
            x_in, z_out = [s(f"xa_in{n}") for n in range(2)], [s(f"za_out{n}") for n in range(2)]
            bn_done, var_ready, rstd_ready, norm_ready = s("a_bn_done"), s("a_var_ready"), s("a_rstd_ready"), s("a_norm_ready")
            a_aggr = s("a_aggr")
            h_ready, z_ready, stats_kept = s("a_h_ready"), s("a_z_ready"), s("a_stats_kept")
            block = nc.Block()
            with block:
                @block.sync
                def _(sp):
                    def load(g, slot, use):
                        at_least(sp, h_ready, G * (g - 1))
                        hold(sp, held)
                        rows = x[bass.ds(first_row(g), GR), :].rearrange("(p t) d -> p t d", t=G)
                        sp.dma_start(x_sb[:, slot], rows).then_inc(x_in[slot], 16)
                    pipeline(sp, NGN, 1, lambda new: load(*new))

                @block.vector
                def _(dve):
                    v = nc.vector

                    def half(new, old):
                        if new:
                            g, slot, use = new
                            dve.wait_ge(x_in[slot], 16 * (use + 1))
                            for k in range(G):
                                last = v.bn_stats(six[:, slot, 0, k], x_sb[:, slot, k])
                            last.then_inc(bn_done, 1)
                        if old:
                            go, so, _ = old
                            for k in range(G):
                                dve.wait_ge(h_ready, G * go + k + 1)
                                last = v.bn_stats(six[:, so, 1, k], h_sb[:, so, k])
                            last.then_inc(bn_done, 1)
                        todo = ([(new[1], 0)] if new else []) + ([(old[1], 1)] if old else [])
                        before = 0 if old is None else 2 * old[0] + 1
                        n = len(todo)
                        dve.wait_ge(bn_done, before + n)
                        hold(dve, held)
                        for slot, which in todo:
                            for k in range(G):
                                last = v.bn_aggr(mv[:, slot, which, k], six[:, slot, which, k])
                            last.then_inc(a_aggr, 1)
                        dve.wait_ge(a_aggr, before + n)
                        for slot, which in todo:
                            v.tensor_scalar(var[:, slot, which], mv[:, slot, which, :, 1], EPS, None, ALU.add).then_inc(var_ready, 1)
                        for j, (slot, which) in enumerate(todo):
                            dve.wait_ge(rstd_ready, before + j + 1)
                            v.scalar_tensor_tensor(norm[:, slot, 2 * which + 1], mv[:, slot, which, :, 0], -1.0,
                                                   norm[:, slot, 2 * which], ALU.mult, ALU.mult).then_inc(norm_ready, 1)
                        if old:
                            dve.wait_ge(norm_ready, before + n)
                            v.tensor_copy(stats[:, bass.ds(old[0], 1)].rearrange("p a b c -> p (a b) c"), norm[:, old[1]]).then_inc(stats_kept, 1)
                    pipeline(dve, NGN, 2, half)

                @block.gpsimd
                def _(pool):
                    def half(new, old):
                        todo = ([(new[1], 0, new[0])] if new else []) + ([(old[1], 1, old[0])] if old else [])
                        before = 0 if old is None else 2 * old[0] + 1
                        for j, (slot, which, g) in enumerate(todo):
                            pool.wait_ge(var_ready, before + j + 1)
                            if which == 0:
                                at_least(pool, stats_kept, g - 1)
                            nc.gpsimd.tensor_tensor(norm[:, slot, 2 * which], var[:, slot, which], half_neg[:, 0:G], ALU.pow).then_inc(rstd_ready, 1)
                        if old:
                            g, slot, use = old
                            pool.wait_ge(z_ready, g + 1)
                            if isinstance(g, int) and g == NGN - 1:
                                pool.wait_ge(z_out[1 - slot], 16 * ((g - 1) // 2 + 1))
                            rows = z_table[bass.ds(first_row(g), GR), :].rearrange("(p t) d -> p t d", t=G)
                            pool.dma_start(rows, z_sb[:, slot]).then_inc(z_out[slot], 16)
                    pipeline(pool, NGN, 2, half)
                    for n in range(2):
                        pool.wait_ge(z_out[n], 16 * ((NGN - n + 1) // 2))

                @block.scalar
                def _(act):
                    def half(new, old):
                        before = 0 if old is None else 2 * old[0] + 1
                        if new:
                            g, slot, use = new
                            act.wait_ge(norm_ready, before + 1)
                            for k in range(G):
                                nc.scalar.activation(h_sb[:, slot, k], x_sb[:, slot, k], ACT.Relu, bias=norm[:, slot, 1, k:k + 1],
                                                     scale=norm[:, slot, 0, k:k + 1]).then_inc(h_ready, 1)
                        if old:
                            g, slot, use = old
                            act.wait_ge(norm_ready, before + (2 if new else 1))
                            at_least(act, z_out[slot], 16 * use)
                            for k in range(G):
                                last = nc.scalar.activation(z_sb[:, slot, k], h_sb[:, slot, k], ACT.Identity, bias=norm[:, slot, 3, k:k + 1],
                                                            scale=norm[:, slot, 2, k:k + 1])
                            last.then_inc(z_ready, 1)
                    pipeline(act, NGN, 2, half)

        with phase() as (ctx, t, s):
            ps = lambda name: ctx.enter_context(nc.psum_tensor(name, [P, 512], F32))
            zs, zd = t("zs", [P, 2, G, D]), t("zd", [P, 2, G, D])
            at_s, at_d = t("at_s", [P, 2, G], I32), t("at_d", [P, 2, G], I32)
            z_t = t("z_t", [P, 2, 4, P])
            metag = t("metag", [P, 2, G, META])
            lohig = t("lohig", [P, 2, G, 2])
            ea_tr = t("ea_tr", [G * META, 2, P])
            q_sb, prod = t("q_sb", [P, 2, D]), t("prod", [P, 2, D])
            alpha = t("alpha", [P, 2, G, H])
            v_sb = t("v_sb", [P, 2, G, D])
            penf_sb, penb_sb = t("penf_sb", [G * H, 2, P]), t("penb_sb", [G * H, 2, P])
            dst_sb = t("dst_sb", [P, 2, GR], U16)
            run_max, seg_max = t("run_max", [G * H, P]), t("seg_max", [G * H, P])
            below, weight = t("below", [G * H, P]), t("weight", [G * H, P])
            msgs = t("msgs", [P, 2, G, MSG])
            same = t("same", [P, 2, G, P])
            is_lo, is_hi = t("is_lo", [P, 2, G, P], BF16), t("is_hi", [P, 2, G, HI], BF16)
            rows_sb = t("rows_sb", [P, 2, G, ROW0])
            p_tr = [ps("p_tr0"), ps("p_tr1")]
            p_qk = [ps("p_qk0"), ps("p_qk1")]
            p_v, p_small, p_sum, p_deg = ps("p_v"), ps("p_small"), ps("p_sum"), ps("p_deg")
            p_alpha, p_back, p_ea = p_small[0:G * H, 0:P], p_small[:, P:P + 2 * G * H], p_small[0:G * META, 256:256 + P]

            gathered = [[s(f"gathered{a}{b}") for b in range(4)] for a in range(2)]
            dst_in, pen_in, stored = ([s(f"{n}{a}") for a in range(2)] for n in ("e0_dst_in", "e0_pen_in", "e0_stored"))
            turned, z_copied, projected, valued, q_ready, scored, v_copied = (s(n) for n in ("turned", "z_copied", "projected", "valued", "q_ready", "scored", "v_copied"))
            meta_ready, ea_turned, ea_ready, alpha_ready, alpha_turned = (s(n) for n in ("meta_ready", "ea_turned", "ea_ready", "alpha_ready", "alpha_turned"))
            scanned, weighted, back_turned, weights_ready = (s(n) for n in ("scanned", "weighted", "back_turned", "weights_ready"))
            same_ready, msg_ready, summed, sums_copied, prod_ready, counted = (s(n) for n in ("same_ready", "msg_ready", "summed", "sums_copied", "prod_ready", "counted"))
            spun, at_ready, deg_done = s("spun"), s("at_ready"), s("deg_done")
            block = nc.Block()
            with block:
                @block.gpsimd
                def _(pool):
                    def gather(g, slot, use):
                        for u in range(4):
                            at_least(pool, gathered[slot][u], 64 * use)
                        nc.gpsimd.tensor_copy(at_s[:, slot], src_col[:, bass.ds(g * G, G)]).then_inc(at_ready, 1)
                        nc.gpsimd.tensor_copy(at_d[:, slot], dst_col[:, bass.ds(g * G, G)]).then_inc(at_ready, 1)
                        for u in range(4):
                            at_least(pool, turned, 4 * g + u - 7)
                            pool.wait_ge(at_ready, 2 * g + 2)
                            hold(pool, held)
                            for k in (2 * u, 2 * u + 1):
                                for to, at in ((zs, at_s), (zd, at_d)):
                                    pool.indirect_dma_start(out=to[:, slot, k], out_offset=None, in_=z_table,
                                                            in_offset=bass.IndirectOffsetOnAxis(ap=at[:, slot, k:k + 1], axis=0)
                                                            ).then_inc(gathered[slot][u], 16)
                    pipeline(pool, NGE, 1, lambda new: gather(*new))

                @block.sync
                def _(sp):
                    def half(new, old):
                        if new:
                            g, slot, use = new
                            at_least(sp, same_ready, 4 * (g - 1))
                            hold(sp, held)
                            sp.dma_start(dst_sb[:, slot], dst16[bass.ds(g * GR, GR)].unsqueeze(0).broadcast_to([P, GR])).then_inc(dst_in[slot], 16)
                            at_least(sp, scanned, 3 * (g - 1))
                            hold(sp, held)
                            for to, of in ((penf_sb, pen_f), (penb_sb, pen_b)):
                                rows = of[bass.ds(g * GR, GR)].rearrange("(t e) -> t e", t=G).unsqueeze(1).broadcast_to([G, H, P])
                                sp.dma_start(to[:, slot], rows).then_inc(pen_in[slot], 16)
                        if old:
                            g, slot, use = old
                            sp.wait_ge(sums_copied, 4 * g + 4)
                            hold(sp, held)
                            rows = rows0[bass.ds(g * GR, GR), :].rearrange("(t p) c -> p t c", p=P)
                            sp.dma_start(rows, rows_sb[:, slot]).then_inc(stored[slot], 16)
                    pipeline(sp, NGE, 2, half)
                    for n in range(2):
                        sp.wait_ge(stored[n], 16 * (NGE // 2))

                @block.tensor
                def _(pe):
                    t_ = nc.tensor

                    def turn_ea(g, slot, use):
                        pe.wait_ge(meta_ready, 2 * g + 2)
                        at_least(pe, weights_ready, 2 * g - 2)
                        hold(pe, held)
                        t_.transpose(p_ea, metag[:, slot].rearrange("p t j -> p (t j)"), ident[:]).then_inc(ea_turned, 1)

                    def turn(g, slot, use, u):
                        pe.wait_ge(gathered[slot][u], 64 * (use + 1))
                        at_least(pe, z_copied, 4 * g + u - 1)
                        for j, z in enumerate((zs, zd)):
                            for k in range(2):
                                last = t_.transpose(p_tr[u % 2][:, (2 * j + k) * P:(2 * j + k + 1) * P], z[:, slot, 2 * u + k], ident[:])
                        last.then_inc(turned, 1)

                    def project(g, slot, use, u):
                        pe.wait_ge(z_copied, 4 * g + u + 1)
                        pe.wait_ge(ea_ready, g + 1)
                        at_least(pe, scored, 4 * g + u - 1)
                        for k in range(2):
                            q, key = (p_qk[u % 2][:, (2 * k + j) * D:(2 * k + j + 1) * D] for j in range(2))
                            t_.matmul(q, z_t[:, u % 2, 2 + k], wq_t[:], start=True, stop=True)
                            t_.matmul(key, z_t[:, u % 2, k], wkv_t[:, 0:D], start=True, stop=False)
                            last = t_.matmul(key, ea_tr[:, slot], wea[:, 2 * u + k, 0:D], start=False, stop=True)
                        last.then_inc(projected, 1)
                        at_least(pe, v_copied, 4 * g + u)
                        for k in range(2):
                            val = p_v[:, k * D:(k + 1) * D]
                            t_.matmul(val, z_t[:, u % 2, k], wkv_t[:, D:2 * D], start=True, stop=False)
                            last = t_.matmul(val, ea_tr[:, slot], wea[:, 2 * u + k, D:2 * D], start=False, stop=True)
                        last.then_inc(valued, 1)

                    def count(g, slot, use, u):
                        pe.wait_ge(counted, 4 * g + u + 1)
                        for k in (2 * u, 2 * u + 1):
                            first = isinstance(g, int) and g == 0 and k == 0
                            final = isinstance(g, int) and g == NGE - 1 and k == G - 1
                            last = t_.matmul(p_deg[:, 0:HI], is_lo[:, slot, k], is_hi[:, slot, k], start=first, stop=final)
                        last.then_inc(deg_done, 1)

                    def add_up(g, slot, use, u):
                        pe.wait_ge(msg_ready, 4 * g + u + 1)
                        at_least(pe, sums_copied, 4 * g + u)
                        for k in (2 * u, 2 * u + 1):
                            last = t_.matmul(p_sum[:, k % 2 * MSG:(k % 2 + 1) * MSG], same[:, slot, k], msgs[:, slot, k], start=True, stop=True)
                        last.then_inc(summed, 1)

                    def half(new, old):
                        if new:
                            turn_ea(*new)
                            turn(*new, 0)
                        if old:
                            pe.wait_ge(alpha_ready, old[0] + 1)
                            pe.wait_ge(ea_ready, old[0] + (2 if new else 1))
                            t_.transpose(p_alpha, alpha[:, old[1]].rearrange("p t h -> p (t h)"), ident[:]).then_inc(alpha_turned, 1)
                        if new:
                            turn(*new, 1)
                            project(*new, 0)
                        if old:
                            count(*old, 0)
                            pe.wait_ge(weighted, old[0] + 1)
                            hold(pe, held)
                            t_.transpose(p_back[:, 0:G * H], weight[:], ident[0:G * H, 0:G * H])
                            t_.transpose(p_back[:, G * H:2 * G * H], seg_max[:], ident[0:G * H, 0:G * H]).then_inc(back_turned, 1)
                        if new:
                            turn(*new, 2)
                            project(*new, 1)
                        if old:
                            count(*old, 1)
                            add_up(*old, 0)
                        if new:
                            turn(*new, 3)
                            project(*new, 2)
                        if old:
                            count(*old, 2)
                            add_up(*old, 1)
                        if new:
                            project(*new, 3)
                        if old:
                            count(*old, 3)
                            add_up(*old, 2)
                            add_up(*old, 3)
                    pipeline(pe, NGE, 2, half)

                @block.scalar
                def _(act):
                    a = nc.scalar

                    def copy_z(g, slot, use, u):
                        act.wait_ge(turned, 4 * g + u + 1)
                        at_least(act, valued, 4 * g + u - 1)
                        a.activation(z_t[:, u % 2].rearrange("p a b -> p (a b)"), p_tr[u % 2][:, :], ACT.Copy).then_inc(z_copied, 1)

                    def copy_v(g, slot, use, u):
                        act.wait_ge(valued, 4 * g + u + 1)
                        at_least(act, msg_ready, 4 * g + u - 7)
                        a.activation(v_sb[:, slot, 2 * u:2 * u + 2], p_v[:, 0:2 * D].rearrange("p (t c) -> p t c", t=2), ACT.Copy).then_inc(v_copied, 1)

                    def copy_sums(g, slot, use, u):
                        act.wait_ge(summed, 4 * g + u + 1)
                        a.activation(rows_sb[:, slot, 2 * u:2 * u + 2, 0:MSG], p_sum[:, 0:2 * MSG].rearrange("p (t c) -> p t c", t=2), ACT.Copy).then_inc(sums_copied, 1)

                    def half(new, old):
                        if new:
                            g, slot, use = new
                            act.wait_ge(ea_turned, g + 1)
                            a.activation(ea_tr[:, slot], p_ea, ACT.Copy).then_inc(ea_ready, 1)
                            copy_z(*new, 0)
                        if old:
                            g, slot, use = old
                            act.wait_ge(scanned, 3 * g + 3)
                            at_least(act, back_turned, g)
                            a.activation(weight[:], below[:], ACT.Exp, scale=SCALE).then_inc(weighted, 1)
                        if new:
                            copy_z(*new, 1)
                            copy_v(*new, 0)
                        if old:
                            act.wait_ge(back_turned, g + 1)
                            at_least(act, summed, 4 * (g - 1))
                            a.activation(msgs[:, slot, :, D:MSG], p_back[:, 0:G * H].rearrange("p (t h) -> p t h", t=G), ACT.Copy).then_inc(weights_ready, 1)
                            at_least(act, stored[slot], 16 * use)
                            a.activation(rows_sb[:, slot, :, MSG:ROW0], p_back[:, G * H:2 * G * H].rearrange("p (t h) -> p t h", t=G), ACT.Copy).then_inc(weights_ready, 1)
                        for u in (0, 1, 2):
                            if new and u < 2:
                                copy_z(*new, u + 2)
                            if new:
                                copy_v(*new, u + 1)
                            if old:
                                copy_sums(*old, u)
                        if old:
                            copy_sums(*old, 3)
                    pipeline(act, NGE, 2, half)

                @block.vector
                def _(dve):
                    v = nc.vector

                    def score(g, slot, use, u):
                        dve.wait_ge(projected, 4 * g + u + 1)
                        qk = p_qk[u % 2][:, :].rearrange("p (t a c) -> p t a c", t=2, a=2)
                        q, k = qk[:, :, 0], qk[:, :, 1]
                        v.tensor_tensor(q_sb[:], q, bq_row[:].unsqueeze(1).broadcast_to([P, 2, D]), ALU.add).then_inc(q_ready, 1)
                        dve.wait_ge(q_ready, 4 * g + u + 1)
                        v.tensor_tensor(prod[:], q_sb[:], k, ALU.mult).then_inc(scored, 1)
                        dve.wait_ge(scored, 4 * g + u + 1)
                        last = v.tensor_reduce(alpha[:, slot, 2 * u:2 * u + 2].rearrange("p t h -> p (t h)"),
                                               prod[:].rearrange("p t (h c) -> p (t h) c", h=H), AX.X, ALU.add)
                        last.then_inc(alpha_ready if u == 3 else prod_ready, 1)

                    def compare(g, slot, use, u):
                        if u == 0:
                            dve.wait_ge(dst_in[slot], 16 * (use + 1))
                            at_least(dve, summed, 4 * (g - 1))
                            at_least(dve, deg_done, 4 * (g - 1))
                        for k in (2 * u, 2 * u + 1):
                            last = v.tensor_scalar(same[:, slot, k], dst_sb[:, slot, k * P:(k + 1) * P], metag[:, slot, k, META - 1:META], None, ALU.is_equal)
                        last.then_inc(same_ready, 1)
                        for k in (2 * u, 2 * u + 1):
                            v.tensor_scalar(is_lo[:, slot, k], iota16[:, 0:P], lohig[:, slot, k, 0:1], None, ALU.is_equal)
                            last = v.tensor_scalar(is_hi[:, slot, k], iota16[:, 0:HI], lohig[:, slot, k, 1:2], None, ALU.is_equal)
                        last.then_inc(counted, 1)

                    def message(g, slot, use, u):
                        if u == 0:
                            dve.wait_ge(weights_ready, 2 * g + 1)
                        dve.wait_ge(v_copied, 4 * g + u + 1)
                        w = msgs[:, slot, 2 * u:2 * u + 2, D:MSG].unsqueeze(3).broadcast_to([P, 2, H, C])
                        v.tensor_tensor(msgs[:, slot, 2 * u:2 * u + 2, 0:D].rearrange("p t (h c) -> p t h c", h=H),
                                        v_sb[:, slot, 2 * u:2 * u + 2].rearrange("p t (h c) -> p t h c", h=H), w, ALU.mult).then_inc(msg_ready, 1)

                    def scan(g, slot, use):
                        dve.wait_ge(alpha_turned, g + 1)
                        dve.wait_ge(pen_in[slot], 32 * (use + 1))
                        at_least(dve, weighted, g)
                        at_least(dve, back_turned, g)
                        v.tensor_tensor_scan(run_max[:], penf_sb[:, slot], p_alpha, NEG, ALU.add, ALU.max).then_inc(scanned, 1)
                        dve.wait_ge(scanned, 3 * g + 1)
                        v.tensor_tensor_scan(seg_max[:, ::-1], penb_sb[:, slot, ::-1], run_max[:, ::-1], NEG, ALU.add, ALU.max).then_inc(scanned, 1)
                        dve.wait_ge(scanned, 3 * g + 2)
                        v.tensor_tensor(below[:], p_alpha, seg_max[:], ALU.subtract).then_inc(scanned, 1)

                    def half(new, old):
                        if new:
                            g, slot, use = new
                            at_least(dve, ea_turned, g - 1)
                            v.tensor_copy(metag[:, slot], meta[:, bass.ds(g * G, G)]).then_inc(meta_ready, 1)
                            v.tensor_copy(lohig[:, slot], lohi[:, bass.ds(g * G, G)]).then_inc(meta_ready, 1)
                        if old:
                            scan(*old)
                            dve.wait_ge(meta_ready, 2 * old[0] + 2)
                            compare(*old, 0)
                        for u in range(4):
                            if new:
                                score(*new, u)
                            if old:
                                message(*old, u)
                                if u < 3:
                                    compare(*old, u + 1)
                    pipeline(dve, NGE, 2, half)
                    dve.wait_ge(deg_done, 4 * NGE)
                    v.tensor_copy(deg[:], p_deg[:, 0:HI]).then_inc(prod_ready, 1)
                    dve.wait_ge(prod_ready, 3 * NGE + 1)

        with phase() as (ctx, t, s):
            pbank = [ctx.enter_context(nc.psum_tensor(f"pm{n}", [P, 512], F32)) for n in range(8)]
            first_r, last_r = t("first_r", [RB, NB, ROW0]), t("last_r", [RB, NB, ROW0])
            before_r, joined = t("before_r", [RB, NB, ROW0]), t("joined", [RB, NB, ROW0])
            cum, tot = t("cum", [P, HI]), t("tot", [P, HI])
            none, row_f, dinv_f = t("none", [P, HI]), t("row_f", [P, HI]), t("dinv_f", [P, HI])
            deg1, some = t("deg1", [P, HI]), t("some", [P, HI])
            row_i, dinv_r = t("row_i", [P, HB, P], I32), t("dinv_r", [P, HB, P])
            msg_t, den_t, max_t = t("msg_t", [D, TE]), t("den_t", [H, TE]), t("max_t", [H, TE])
            stop4, decay, gain = t("stop4", [H, TE]), t("decay", [H, TE]), t("gain", [H, TE])
            msg_c, den_c, max_c = t("msg_c", [D, TE + 1]), t("den_c", [H, TE + 1]), t("max_c", [H, TE + 1])
            top_m, wf, wb_ = t("top_m", [RB, NB, H]), t("wf", [RB, NB, H]), t("wb_", [RB, NB, H])
            part = t("part", [RB, NB, MSG])
            ends_in, tables_out, tables_in, fixed = s("m_ends_in"), s("m_tables_out"), s("m_tables_in"), s("m_fixed")
            pe_t, act_x, dve_s, powed = s("m_pe"), s("m_act"), s("m_dve"), s("m_powed")
            deg_ready, cum_ready, rows_t, rows_set = s("deg_ready"), s("cum_ready"), s("rows_t"), s("m_rows_set")
            turned, copied, exps_in, expanded, back, joined_s = s("m_turned"), s("m_copied"), s("exps_in"), s("expanded"), s("m_back"), s("m_joined")
            chained, floats = s("chained"), s("m_floats")
            block = nc.Block()
            with block:
                @block.sync
                def _(sp):
                    ends = rows0[0:EP, :].rearrange("(b r e) c -> r b e c", b=NB, r=RB)
                    sp.dma_start(first_r[:], ends[:, :, 0, :]).then_inc(ends_in, 16)
                    sp.dma_start(last_r[:], ends[:, :, P - 1, :]).then_inc(ends_in, 16)
                    sp.wait_ge(rows_set, HB)
                    for b in range(HB):
                        n = min(P, HI - b * P)
                        for table, rows in ((node_row_d, row_i), (dinv_d, dinv_r)):
                            sp.dma_start(table[b * P * P:(b * P + n) * P].rearrange("(h l) -> h l", l=P), rows[0:n, b, :]).then_inc(tables_out, 16)
                    sp.wait_ge(tables_out, 32 * HB)
                    for g in range(NGN):
                        for table, cols in ((node_row_d, node_row), (dinv_d, dinv)):
                            r0 = first_row(g)
                            sp.dma_start(cols[:, g, :], table[r0:r0 + GR].rearrange("(p t) -> p t", t=G)).then_inc(tables_in, 16)
                    sp.wait_ge(tables_in, 32 * NGN)

                @block.gpsimd
                def _(pool):
                    pool.wait_ge(deg_ready, 1)
                    nc.gpsimd.tensor_tensor(row_f[:], deg1[:], half_neg[:, 0:HI], ALU.pow).then_inc(powed, 1)
                    pool.wait_ge(joined_s, 1)
                    for b in range(NB):
                        pool.indirect_dma_start(out=rows0, out_offset=bass.IndirectOffsetOnAxis(ap=fix_at[:, b:b + 1], axis=0),
                                                in_=joined[:, b, :], in_offset=None, bounds_check=EP - 1, oob_is_err=False).then_inc(fixed, 16)
                    pool.wait_ge(fixed, 16 * NB)

                @block.tensor
                def _(pe):
                    t_ = nc.tensor
                    t_.matmul(pbank[0][:, 0:HI], tri[:], deg[:], start=True, stop=True)
                    t_.matmul(pbank[1][:, 0:HI], ones[:], deg[:], start=True, stop=True).then_inc(pe_t, 1)
                    pe.wait_ge(ends_in, 32)
                    for b in range(NB):
                        cols = slice(b * RB, (b + 1) * RB)
                        t_.transpose(pbank[2][:, cols], last_r[:, b, 0:D], ident[0:RB, 0:RB])
                        t_.transpose(pbank[3][0:H, cols], last_r[:, b, D:MSG], ident[0:RB, 0:RB])
                        last = t_.transpose(pbank[4][0:H, cols], last_r[:, b, MSG:ROW0], ident[0:RB, 0:RB])
                    last.then_inc(turned, 1)
                    for b in range(HB):
                        n = min(P, HI - b * P)
                        pe.wait_ge(floats, 2)
                        if b:
                            pe.wait_ge(rows_set, b)
                        t_.transpose(pbank[5][0:n, 0:P], cum[:, b * P:b * P + n], ident[:])
                        t_.transpose(pbank[5][0:n, P:2 * P], dinv_f[:, b * P:b * P + n], ident[:]).then_inc(rows_t, 1)
                    pe.wait_ge(exps_in, 2)
                    t_.matmul(pbank[6][:, 0:TE], headmap[:], decay[:], start=True, stop=True)
                    t_.matmul(pbank[7][:, 0:TE], headmap[:], gain[:], start=True, stop=True).then_inc(expanded, 1)
                    pe.wait_ge(chained, 2)
                    for b in range(NB):
                        cols = slice(b * RB, (b + 1) * RB)
                        at = b % 3 * ROW0
                        o = pbank[b // 3][0:RB, :]
                        t_.transpose(o[:, at:at + D], msg_c[:, cols], ident[:])
                        t_.transpose(o[:, at + D:at + MSG], den_c[:, cols], ident[0:H, 0:H])
                        last = t_.transpose(o[:, at + MSG:at + ROW0], max_c[:, cols], ident[0:H, 0:H])
                    last.then_inc(back, 1)

                @block.scalar
                def _(act):
                    a = nc.scalar
                    act.wait_ge(copied, 2)
                    a.activation(decay[:], decay[:], ACT.Exp, scale=SCALE).then_inc(act_x, 1)
                    a.activation(gain[:], gain[:], ACT.Exp, scale=SCALE).then_inc(act_x, 1)
                    act.wait_ge(copied, 4)
                    a.activation(wf[:], wf[:], ACT.Exp, scale=SCALE).then_inc(act_x, 1)
                    a.activation(wb_[:], wb_[:], ACT.Exp, scale=SCALE).then_inc(act_x, 1)

                @block.vector
                def _(dve):
                    v = nc.vector
                    chain = Chain(dve, dve_s)
                    v.tensor_scalar(deg1[:], deg[:], 1.0, None, ALU.max).then_inc(deg_ready, 1)
                    chain.mark(v.tensor_scalar(some[:], deg[:], 0.5, None, ALU.is_gt))
                    chain.mark(v.tensor_scalar(none[:], deg[:], 0.5, float(EP), ALU.is_lt, ALU.mult))
                    dve.wait_ge(pe_t, 1)
                    chain.step(v.memset(dinv_f[:], 0.0))
                    chain.step(v.tensor_tensor_scan(tot[:], dinv_f[:], pbank[1][:, 0:HI], 0.0, ALU.add, ALU.add))
                    chain.step(v.tensor_tensor(tot[:], tot[:], pbank[1][:, 0:HI], ALU.subtract))
                    chain.step(v.tensor_tensor(cum[:], tot[:], pbank[0][:, 0:HI], ALU.add))
                    chain.step(v.scalar_tensor_tensor(cum[:], cum[:], -1.0, some[:], ALU.add, ALU.mult))
                    v.tensor_tensor(cum[:], cum[:], none[:], ALU.add).then_inc(floats, 1)
                    dve.wait_ge(powed, 1)
                    v.tensor_tensor(dinv_f[:], row_f[:], some[:], ALU.mult).then_inc(floats, 1)
                    for b in range(HB):
                        n = min(P, HI - b * P)
                        dve.wait_ge(rows_t, b + 1)
                        v.tensor_copy(row_i[0:n, b, :], pbank[5][0:n, 0:P])
                        v.tensor_copy(dinv_r[0:n, b, :], pbank[5][0:n, P:2 * P]).then_inc(rows_set, 1)
                    dve.wait_ge(turned, 1)
                    chain.mark(v.tensor_copy(msg_t[:], pbank[2][:, 0:TE]))
                    chain.mark(v.tensor_copy(den_t[:], pbank[3][0:H, 0:TE]))
                    chain.mark(v.tensor_copy(max_t[:], pbank[4][0:H, 0:TE]))
                    chain.mark(v.memset(msg_c[:, 0:1], 0.0))
                    chain.mark(v.memset(den_c[:, 0:1], 0.0))
                    chain.mark(v.memset(max_c[:, 0:1], 0.0))
                    chain.step(v.tensor_scalar(stop4[:], through[0:H, :], -1.0, -NEG, ALU.add, ALU.mult))
                    chain.step(v.tensor_tensor_scan(max_c[:, 1:TE + 1], stop4[:], max_t[:], NEG, ALU.add, ALU.max))
                    chain.mark(v.tensor_tensor(gain[:], max_t[:], max_c[:, 1:TE + 1], ALU.subtract))
                    chain.step(v.tensor_tensor(decay[:], max_c[:, 0:TE], max_c[:, 1:TE + 1], ALU.subtract))
                    v.tensor_scalar(decay[:], decay[:], 0.0, None, ALU.min).then_inc(copied, 1)
                    v.tensor_scalar(gain[:], gain[:], 0.0, None, ALU.min).then_inc(copied, 1)
                    dve.wait_ge(act_x, 2)
                    chain.mark(v.tensor_tensor(den_t[:], den_t[:], gain[:], ALU.mult))
                    v.tensor_tensor(decay[:], decay[:], through[0:H, :], ALU.mult).then_inc(exps_in, 2)
                    dve.wait_ge(exps_in, 2)
                    chain.wait()
                    v.tensor_tensor_scan(den_c[:, 1:TE + 1], decay[:], den_t[:], 0.0, ALU.mult, ALU.add).then_inc(chained, 1)
                    dve.wait_ge(expanded, 1)
                    chain.step(v.tensor_tensor(msg_t[:], msg_t[:], pbank[7][:, 0:TE], ALU.mult))
                    v.tensor_tensor_scan(msg_c[:, 1:TE + 1], pbank[6][:, 0:TE], msg_t[:], 0.0, ALU.mult, ALU.add).then_inc(chained, 1)
                    dve.wait_ge(back, 1)
                    for b in range(NB):
                        at = b % 3 * ROW0
                        chain.mark(v.tensor_copy(before_r[:, b, :], pbank[b // 3][0:RB, at:at + ROW0]))
                    chain.wait()
                    chain.step(v.tensor_tensor(top_m[:], first_r[:, :, MSG:ROW0], before_r[:, :, MSG:ROW0], ALU.max))
                    chain.mark(v.tensor_copy(joined[:, :, MSG:ROW0], top_m[:]))
                    v.tensor_tensor(wf[:], first_r[:, :, MSG:ROW0], top_m[:], ALU.subtract).then_inc(copied, 1)
                    v.tensor_tensor(wb_[:], before_r[:, :, MSG:ROW0], top_m[:], ALU.subtract).then_inc(copied, 1)
                    dve.wait_ge(act_x, 4)
                    for o, rows, w in ((joined, first_r, wf), (part, before_r, wb_)):
                        chain.mark(v.tensor_tensor(o[:, :, D:MSG], rows[:, :, D:MSG], w[:], ALU.mult))
                        for b in range(NB):
                            chain.mark(v.tensor_tensor(o[:, b, 0:D].rearrange("r (h c) -> r h c", h=H), rows[:, b, 0:D].rearrange("r (h c) -> r h c", h=H),
                                                       w[:, b, :].unsqueeze(2).broadcast_to([RB, H, C]), ALU.mult))
                    chain.wait()
                    v.tensor_tensor(joined[:, :, 0:MSG], joined[:, :, 0:MSG], part[:], ALU.add).then_inc(joined_s, 1)

        with phase() as (ctx, t, s):
            ps = lambda name: ctx.enter_context(nc.psum_tensor(name, [P, 512], F32))
            x_sb = t("xb", [P, 2, G, D])
            agg = t("agg", [P, 2, G, ROW0])
            at_n = t("at_n", [P, 2, G], I32)
            norm = t("normb", [P, 2, 4, G])
            h_sb, z_sb = t("hb", [P, 2, G, D]), t("zb", [P, G, D])
            z_t = t("ztb", [P, 2, 4, P])
            den, recip, wa_sum = t("den", [P, G, H]), t("recip", [P, G, H]), t("wa_sum", [P, 2, G])
            attn, hat, wa_prod = t("attn", [P, 2, G, D]), t("hat", [P, 2, G, D]), t("wa_prod", [P, G, D])
            diff, skip = t("diff", [P, G, D]), t("skip", [P, G, D + 1])
            logit, gate_e, gate_1, gate = t("logit", [P, G]), t("gate_e", [P, G]), t("gate_1", [P, G]), t("gate", [P, G])
            x_l = t("x_l", [P, 2, G, D])
            six2, mv2, var2 = t("six2", [P, G, 6]), t("mv2", [P, G, 2]), t("var2", [P, G])
            six3, mv3, var3 = t("six3", [P, G, 6]), t("mv3", [P, G, 2]), t("var3", [P, G])
            norm2 = t("norm2", [P, 2, 2, G])
            norm3 = t("norm3", [P, 2, 5, G])
            z2, z2_t = t("z2", [P, G, D]), t("z2_t", [P, 2, 4, P])
            act1 = t("act1", [P, 2, 4, 4 * P])
            xb2 = t("xb2", [P, 2, G, D])
            x1_sb, h2_sb = t("x1b", [P, 2, G, D]), t("h2b", [P, 2, G, ROW1])
            p_zt, p_z2t = ps("p_zt"), ps("p_z2t")
            p_skip = [ps("p_skip0"), ps("p_skip1")]
            p_f1 = [ps("p_f10"), ps("p_f11")]
            p_f2 = [ps("p_f20"), ps("p_f21")]
            S = {n: s("b_" + n) for n in (
                "at_ready tab_ready h_ready z_ready zt_turned zt_copied skipped skip_ready recips attn_ready "
                "wa_ready logit_ready gate_exp diff_ready hat_ready xb2_ready xl_ready bn2 var2 rstd2 norm2_ready "
                "gates norm3s z2_ready z2_turned z2_copied f1_done f1_copied f2_done y_ready x1_ready bn3 var3 rstd3 norm3_ready h2_ready").split()}
            x_in, agg_in, x1_out, h2_out = ([s(f"b_{n}{a}") for a in range(2)] for n in ("x_in", "agg_in", "x1_out", "h2_out"))
            block = nc.Block()

            with block:
                @block.sync
                def _(sp):
                    def half(load, prep, gating, mlp, ending, last):
                        if load:
                            g, slot, use = load
                            at_least(sp, S["xb2_ready"], g - 1)
                            hold(sp, held)
                            at_least(sp, S["h_ready"], 2 * (g - 1))
                            hold(sp, held)
                            rows = x[bass.ds(first_row(g), GR), :].rearrange("(p t) d -> p t d", t=G)
                            sp.dma_start(x_sb[:, slot], rows).then_inc(x_in[slot], 16)
                        if ending:
                            g, slot, use = ending
                            if isinstance(g, int) and g == NGN - 1:
                                sp.wait_ge(x1_out[1 - slot], 16 * ((g - 1) // 2 + 1))
                            sp.wait_ge(S["x1_ready"], g + 1)
                            hold(sp, held)
                            rows = bass.ds(first_row(g), GR)
                            sp.dma_start(x1_table[rows, :].rearrange("(p t) d -> p t d", t=G), x1_sb[:, slot]).then_inc(x1_out[slot], 16)
                    pipeline(sp, NGN, 6, half)
                    for n in range(2):
                        sp.wait_ge(x1_out[n], 16 * ((NGN - n + 1) // 2))

                @block.gpsimd
                def _(pool):
                    def gather(g, slot, tiles):
                        for k in tiles:
                            pool.indirect_dma_start(out=agg[:, slot, k], out_offset=None, in_=rows0,
                                                    in_offset=bass.IndirectOffsetOnAxis(ap=at_n[:, slot, k:k + 1], axis=0)).then_inc(agg_in[slot], 16)

                    def half(load, prep, gating, mlp, ending, last):
                        if load:
                            g, slot, use = load
                            at_least(pool, agg_in[slot], 16 * G * use)
                            nc.gpsimd.tensor_copy(at_n[:, slot], node_row[:, bass.ds(g, 1), :].rearrange("p a t -> p (a t)")).then_inc(S["at_ready"], 1)
                            at_least(pool, S["attn_ready"], g - 1)
                            pool.wait_ge(S["at_ready"], g + 1)
                            hold(pool, held)
                            gather(g, slot, range(G))
                        if gating:
                            g, slot, use = gating
                            pool.wait_ge(x_in[slot], 16 * (use + 1))
                            at_least(pool, S["x1_ready"], g - 1)
                            nc.gpsimd.tensor_tensor(xb2[:, slot], x_sb[:, slot], b2_row[:].unsqueeze(1).broadcast_to([P, G, D]), ALU.add).then_inc(S["xb2_ready"], 1)
                        if prep:
                            g, slot, use = prep
                            pool.wait_ge(S["attn_ready"], g + 1)
                            pool.wait_ge(S["h_ready"], 2 * g + 2)
                            at_least(pool, S["xl_ready"], g - 1)
                            nc.gpsimd.tensor_tensor(hat[:, slot], attn[:, slot], h_sb[:, slot], ALU.add).then_inc(S["hat_ready"], 1)
                        if gating:
                            g, slot, use = gating
                            pool.wait_ge(S["var2"], g + 1)
                            at_least(pool, S["z2_ready"], 2 * (g - 1))
                            nc.gpsimd.tensor_tensor(norm2[:, slot, 0], var2[:], half_neg[:, 0:G], ALU.pow).then_inc(S["rstd2"], 1)
                        if ending:
                            g, slot, use = ending
                            pool.wait_ge(S["var3"], g + 1)
                            at_least(pool, S["h2_ready"], g - 1)
                            nc.gpsimd.tensor_tensor(norm3[:, slot, 0], var3[:], half_neg[:, 0:G], ALU.pow).then_inc(S["rstd3"], 1)
                    pipeline(pool, NGN, 6, half)

                @block.tensor
                def _(pe):
                    t_ = nc.tensor

                    def turn_z2(g, slot, q):
                        pe.wait_ge(S["z2_ready"], 2 * g + q + 1)
                        at_least(pe, S["z2_copied"], 2 * g + q)
                        for k in range(4):
                            last = t_.transpose(p_z2t[:, k * P:(k + 1) * P], z2[:, 4 * q + k], ident[:])
                        last.then_inc(S["z2_turned"], 1)

                    def turn_z(g, slot, q):
                        pe.wait_ge(S["z_ready"], 2 * g + q + 1)
                        at_least(pe, S["zt_copied"], 2 * g + q)
                        for k in range(4):
                            last = t_.transpose(p_zt[:, k * P:(k + 1) * P], z_sb[:, 4 * q + k], ident[:])
                        last.then_inc(S["zt_turned"], 1)

                    def skips(g, u):
                        pe.wait_ge(S["zt_copied"], 2 * g + u // 2 + 1)
                        at_least(pe, S["skip_ready"], 4 * g + u - 1)
                        for k in range(2):
                            last = t_.matmul(p_skip[u % 2][:, k * (D + 1):(k + 1) * (D + 1)], z_t[:, u // 2, 2 * (u % 2) + k], wsk_t[:], start=True, stop=True)
                        last.then_inc(S["skipped"], 1)

                    def up(g, q, chunks):
                        pe.wait_ge(S["z2_copied"], 2 * g + q + 1)
                        for c in chunks:
                            at_least(pe, S["f1_copied"], 8 * g + 4 * q + c - 1)
                            t_.matmul(p_f1[c % 2][:, :], w1_t[:, c * P:(c + 1) * P], z2_t[:, q].rearrange("p a b -> p (a b)"),
                                      start=True, stop=True).then_inc(S["f1_done"], 1)

                    def down(g, q):
                        at_least(pe, S["y_ready"], 2 * (g - 1) + q + 1)
                        pe.wait_ge(S["f1_copied"], 8 * g + 4 * q + 4)
                        for k in range(4):
                            for c in range(4):
                                last = t_.matmul(p_f2[q][:, k * D:(k + 1) * D], act1[:, q, c, k * P:(k + 1) * P], w2_t[:, c], start=(c == 0), stop=(c == 3))
                        last.then_inc(S["f2_done"], 1)

                    def half(load, prep, gating, mlp, ending, last):
                        if gating:
                            turn_z(gating[0], gating[1], 0)
                            turn_z(gating[0], gating[1], 1)
                            skips(gating[0], 0)
                            skips(gating[0], 1)
                        if mlp:
                            turn_z2(mlp[0], mlp[1], 0)
                        if gating:
                            skips(gating[0], 2)
                            skips(gating[0], 3)
                        if mlp:
                            up(mlp[0], 0, (0, 1))
                            turn_z2(mlp[0], mlp[1], 1)
                            up(mlp[0], 0, (2, 3))
                            up(mlp[0], 1, range(4))
                            down(mlp[0], 0)
                            down(mlp[0], 1)
                    pipeline(pe, NGN, 6, half)

                @block.scalar
                def _(act):
                    a = nc.scalar

                    def h_of(g, slot, use, q):
                        if q == 0:
                            act.wait_ge(x_in[slot], 16 * (use + 1))
                            act.wait_ge(S["tab_ready"], g + 1)
                            at_least(act, S["hat_ready"], g - 1)
                            at_least(act, S["z_ready"], 2 * (g - 1))
                        for k in range(4 * q, 4 * q + 4):
                            last = a.activation(h_sb[:, slot, k], x_sb[:, slot, k], ACT.Relu, bias=norm[:, slot, 1, k:k + 1], scale=norm[:, slot, 0, k:k + 1])
                        last.then_inc(S["h_ready"], 1)

                    def z2_of(g, slot, use, q):
                        act.wait_ge(S["norm2_ready"], g + 1)
                        at_least(act, S["z2_turned"], 2 * (g - 1) + q + 1)
                        for k in range(4 * q, 4 * q + 4):
                            last = a.activation(z2[:, k], x_l[:, slot, k], ACT.Identity, bias=norm2[:, slot, 1, k:k + 1], scale=norm2[:, slot, 0, k:k + 1])
                        last.then_inc(S["z2_ready"], 1)

                    def copy_z2(g, q):
                        act.wait_ge(S["z2_turned"], 2 * g + q + 1)
                        at_least(act, S["f1_done"], 8 * (g - 1) + 4 * q + 4)
                        a.activation(z2_t[:, q].rearrange("p a b -> p (a b)"), p_z2t[:, :], ACT.Copy).then_inc(S["z2_copied"], 1)

                    def copy_z(g, q):
                        act.wait_ge(S["zt_turned"], 2 * g + q + 1)
                        at_least(act, S["skipped"], 4 * (g - 1) + 2 * q + 2)
                        a.activation(z_t[:, q].rearrange("p a b -> p (a b)"), p_zt[:, :], ACT.Copy).then_inc(S["zt_copied"], 1)

                    def relus(g, q, chunks):
                        at_least(act, S["f2_done"], 2 * (g - 1) + q + 1)
                        for c in chunks:
                            act.wait_ge(S["f1_done"], 8 * g + 4 * q + c + 1)
                            a.activation(act1[:, q, c], p_f1[c % 2][:, :], ACT.Relu, bias=b1_col[:, c:c + 1]).then_inc(S["f1_copied"], 1)

                    def half(load, prep, gating, mlp, ending, last):
                        if mlp:
                            z2_of(*mlp, 0)
                        if gating:
                            copy_z(gating[0], 0)
                            copy_z(gating[0], 1)
                        if mlp:
                            copy_z2(mlp[0], 0)
                            z2_of(*mlp, 1)
                            relus(mlp[0], 0, (0, 1))
                            copy_z2(mlp[0], 1)
                            relus(mlp[0], 0, (2, 3))
                        if gating:
                            act.wait_ge(S["logit_ready"], gating[0] + 1)
                            a.activation(gate_e[:], logit[:], ACT.Exp, scale=-1.0).then_inc(S["gate_exp"], 1)
                        if mlp:
                            relus(mlp[0], 1, range(4))
                        if last:
                            g, slot, use = last
                            act.wait_ge(S["norm3_ready"], g + 1)
                            at_least(act, h2_out[slot], 16 * use)
                            if isinstance(g, int) and g == NGN - 1:
                                act.wait_ge(h2_out[1 - slot], 16 * ((g - 1) // 2 + 1))
                            for k in range(G):
                                a.activation(h2_sb[:, slot, k, 0:D], x1_sb[:, slot, k], ACT.Relu, bias=norm3[:, slot, 3, k:k + 1], scale=norm3[:, slot, 2, k:k + 1])
                            a.activation(h2_sb[:, slot, :, D], norm3[:, slot, 4], ACT.Copy).then_inc(S["h2_ready"], 1)
                            act.wait_ge(S["h2_ready"], g + 1)
                            act.dma_start(h2_table[bass.ds(first_row(g), GR), :].rearrange("(p t) d -> p t d", t=G), h2_sb[:, slot]).then_inc(h2_out[slot], 16)
                        if load:
                            h_of(*load, 0)
                            h_of(*load, 1)
                    pipeline(act, NGN, 6, half)
                    for n in range(2):
                        act.wait_ge(h2_out[n], 16 * ((NGN - n + 1) // 2))

                @block.vector
                def _(dve):
                    v = nc.vector

                    def half(load, prep, gating, mlp, ending, last):
                        if load:
                            g, slot, use = load
                            v.tensor_copy(norm[:, slot], stats[:, bass.ds(g, 1)].rearrange("p a b c -> p (a b) c")).then_inc(S["tab_ready"], 1)
                        if ending:
                            g, slot, use = ending
                            at_least(dve, x1_out[slot], 16 * use)
                            at_least(dve, S["h2_ready"], g - 1)
                            for q in range(2):
                                dve.wait_ge(S["f2_done"], 2 * g + q + 1)
                                v.tensor_tensor(x1_sb[:, slot, 4 * q:4 * q + 4].rearrange("p a b -> p (a b)"), p_f2[q][:, :],
                                                x_l[:, slot, 4 * q:4 * q + 4].rearrange("p a b -> p (a b)"), ALU.add).then_inc(S["y_ready"], 1)
                        if gating:
                            g, slot, use = gating
                            for u in range(4):
                                dve.wait_ge(S["skipped"], 4 * g + u + 1)
                                v.tensor_tensor(skip[:, 2 * u:2 * u + 2], p_skip[u % 2][:, 0:2 * (D + 1)].rearrange("p (t c) -> p t c", t=2),
                                                bsk_row[:].unsqueeze(1).broadcast_to([P, 2, D + 1]), ALU.add).then_inc(S["skip_ready"], 1)
                            dve.wait_ge(S["skip_ready"], 4 * g + 4)
                            v.tensor_tensor(logit[:], wa_sum[:, slot], skip[:, :, D], ALU.add).then_inc(S["logit_ready"], 1)
                            v.tensor_tensor(diff[:], skip[:, :, 0:D], attn[:, slot], ALU.subtract).then_inc(S["diff_ready"], 1)
                        if ending:
                            g, slot, use = ending
                            dve.wait_ge(S["y_ready"], 2 * g + 2)
                            dve.wait_ge(S["xb2_ready"], g + 1)
                            v.tensor_tensor(x1_sb[:, slot], x1_sb[:, slot], xb2[:, slot], ALU.add).then_inc(S["x1_ready"], 1)
                        if prep:
                            g, slot, use = prep
                            dve.wait_ge(agg_in[slot], 16 * G * (use + 1))
                            v.tensor_scalar(den[:], agg[:, slot, :, D:MSG], 1e-16, None, ALU.add).then_inc(S["recips"], 1)
                            dve.wait_ge(S["recips"], 2 * g + 1)
                            v.reciprocal(recip[:], den[:]).then_inc(S["recips"], 1)
                            dve.wait_ge(S["recips"], 2 * g + 2)
                            v.tensor_tensor(attn[:, slot].rearrange("p t (h c) -> p t h c", h=H), agg[:, slot, :, 0:D].rearrange("p t (h c) -> p t h c", h=H),
                                            recip[:].unsqueeze(3).broadcast_to([P, G, H, C]), ALU.mult).then_inc(S["attn_ready"], 1)
                        if gating:
                            g, slot, use = gating
                            dve.wait_ge(S["gate_exp"], g + 1)
                            v.tensor_scalar(gate_1[:], gate_e[:], 1.0, None, ALU.add).then_inc(S["gates"], 1)
                            dve.wait_ge(S["gates"], 2 * g + 1)
                            v.reciprocal(gate[:], gate_1[:]).then_inc(S["gates"], 1)
                            dve.wait_ge(S["gates"], 2 * g + 2)
                            dve.wait_ge(S["diff_ready"], g + 1)
                            dve.wait_ge(S["hat_ready"], g + 1)
                            for k in range(G):
                                last = v.scalar_tensor_tensor(x_l[:, slot, k], diff[:, k], gate[:, k:k + 1], hat[:, slot, k], ALU.mult, ALU.add)
                            last.then_inc(S["xl_ready"], 1)
                            dve.wait_ge(S["xl_ready"], g + 1)
                            for k in range(G):
                                last = v.bn_stats(six2[:, k], x_l[:, slot, k])
                            last.then_inc(S["bn2"], 1)
                            dve.wait_ge(S["bn2"], 2 * g + 1)
                            hold(dve, held)
                            for k in range(G):
                                last = v.bn_aggr(mv2[:, k], six2[:, k])
                            last.then_inc(S["bn2"], 1)
                            dve.wait_ge(S["bn2"], 2 * g + 2)
                            at_least(dve, S["rstd2"], g)
                            v.tensor_scalar(var2[:], mv2[:, :, 1], EPS, None, ALU.add).then_inc(S["var2"], 1)
                        if ending:
                            g, slot, use = ending
                            dve.wait_ge(S["x1_ready"], g + 1)
                            for k in range(G):
                                last = v.bn_stats(six3[:, k], x1_sb[:, slot, k])
                            last.then_inc(S["bn3"], 1)
                            dve.wait_ge(S["bn3"], 2 * g + 1)
                            hold(dve, held)
                            for k in range(G):
                                last = v.bn_aggr(mv3[:, k], six3[:, k])
                            last.then_inc(S["bn3"], 1)
                            dve.wait_ge(S["bn3"], 2 * g + 2)
                            at_least(dve, S["rstd3"], g)
                            v.tensor_scalar(var3[:], mv3[:, :, 1], EPS, None, ALU.add).then_inc(S["var3"], 1)
                        if gating:
                            g, slot, use = gating
                            dve.wait_ge(S["rstd2"], g + 1)
                            v.scalar_tensor_tensor(norm2[:, slot, 1], mv2[:, :, 0], -1.0, norm2[:, slot, 0], ALU.mult, ALU.mult).then_inc(S["norm2_ready"], 1)
                        if prep:
                            g, slot, use = prep
                            dve.wait_ge(S["tab_ready"], g + 1)
                            for q in range(2):
                                dve.wait_ge(S["h_ready"], 2 * g + q + 1)
                                at_least(dve, S["zt_turned"], 2 * (g - 1) + q + 1)
                                for k in range(4 * q, 4 * q + 4):
                                    last = v.tensor_scalar(z_sb[:, k], h_sb[:, slot, k], norm[:, slot, 2, k:k + 1], norm[:, slot, 3, k:k + 1], ALU.mult, ALU.add)
                                last.then_inc(S["z_ready"], 1)
                            dve.wait_ge(S["attn_ready"], g + 1)
                            v.tensor_tensor(wa_prod[:], attn[:, slot], wa_row[:].unsqueeze(1).broadcast_to([P, G, D]), ALU.mult).then_inc(S["wa_ready"], 1)
                            dve.wait_ge(S["wa_ready"], 2 * g + 1)
                            v.tensor_reduce(wa_sum[:, slot], wa_prod[:], AX.X, ALU.add).then_inc(S["wa_ready"], 1)
                        if ending:
                            g, slot, use = ending
                            dve.wait_ge(S["rstd3"], g + 1)
                            at_least(dve, S["h2_ready"], g - 1)
                            v.scalar_tensor_tensor(norm3[:, slot, 1], mv3[:, :, 0], -1.0, norm3[:, slot, 0], ALU.mult, ALU.mult).then_inc(S["norm3s"], 1)
                            v.tensor_copy(norm3[:, slot, 4], dinv[:, bass.ds(g, 1)].rearrange("p a t -> p (a t)")).then_inc(S["norm3s"], 1)
                            dve.wait_ge(S["norm3s"], 2 * g + 2)
                            v.tensor_copy(stats2[:, bass.ds(g, 1)].rearrange("p a b c -> p (a b) c"), norm3[:, slot, 0:2])
                            v.tensor_tensor(norm3[:, slot, 2:4], norm3[:, slot, 0:2], norm3[:, slot, 4].unsqueeze(1).broadcast_to([P, 2, G]), ALU.mult).then_inc(S["norm3_ready"], 1)
                    pipeline(dve, NGN, 6, half)

        with phase() as (ctx, t, s):
            h2s = t("h2s", [P, 2, G, ROW1])
            at_s = t("at_s1", [P, 2, G], I32)
            dst_sb, dst_g = t("dst_sb1", [P, 2, GR], U16), t("dst_g", [P, 2, G])
            same = t("same1", [P, 2, G, P])
            rows_sb = t("rows_sb1", [P, 2, G, ROW1])
            p_sum = [ctx.enter_context(nc.psum_tensor(f"p_sum1{n}", [P, 512], F32)) for n in range(4)]
            gathered = [[s(f"e1_gathered{a}{b}") for b in range(4)] for a in range(2)]
            dst_in, stored = ([s(f"e1_{n}{a}") for a in range(2)] for n in ("dst_in", "stored"))
            at_ready, dst_ready, same_ready, summed, sums_copied = (s("e1_" + n) for n in ("at_ready", "dst_ready", "same_ready", "summed", "sums_copied"))
            block = nc.Block()
            with block:
                @block.gpsimd
                def _(pool):
                    def gather(new):
                        g, slot, use = new
                        for u in range(4):
                            at_least(pool, gathered[slot][u], 32 * use)
                        nc.gpsimd.tensor_copy(at_s[:, slot], src_col[:, bass.ds(g * G, G)]).then_inc(at_ready, 1)
                        for u in range(4):
                            at_least(pool, summed, 4 * g + u - 7)
                            pool.wait_ge(at_ready, g + 1)
                            hold(pool, held)
                            for k in (2 * u, 2 * u + 1):
                                pool.indirect_dma_start(out=h2s[:, slot, k], out_offset=None, in_=h2_table,
                                                        in_offset=bass.IndirectOffsetOnAxis(ap=at_s[:, slot, k:k + 1], axis=0)
                                                        ).then_inc(gathered[slot][u], 16)
                    pipeline(pool, NGE, 1, gather)

                @block.sync
                def _(sp):
                    def half(new, old):
                        if new:
                            g, slot, use = new
                            at_least(sp, same_ready, 4 * (g - 1))
                            hold(sp, held)
                            sp.dma_start(dst_sb[:, slot], dst16[bass.ds(g * GR, GR)].unsqueeze(0).broadcast_to([P, GR])).then_inc(dst_in[slot], 16)
                        if old:
                            g, slot, use = old
                            sp.wait_ge(sums_copied, 4 * g + 4)
                            hold(sp, held)
                            sp.dma_start(rows1[bass.ds(g * GR, GR), :].rearrange("(t p) c -> p t c", p=P), rows_sb[:, slot]).then_inc(stored[slot], 16)
                    pipeline(sp, NGE, 2, half)
                    for n in range(2):
                        sp.wait_ge(stored[n], 16 * (NGE // 2))

                @block.vector
                def _(dve):
                    def half(new):
                        g, slot, use = new
                        nc.vector.tensor_copy(dst_g[:, slot], meta[:, bass.ds(g * G, G), META - 1]).then_inc(dst_ready, 1)
                        dve.wait_ge(dst_ready, g + 1)
                        dve.wait_ge(dst_in[slot], 16 * (use + 1))
                        for u in range(4):
                            at_least(dve, summed, 4 * g + u - 7)
                            for k in (2 * u, 2 * u + 1):
                                last = nc.vector.tensor_scalar(same[:, slot, k], dst_sb[:, slot, k * P:(k + 1) * P], dst_g[:, slot, k:k + 1], None, ALU.is_equal)
                            last.then_inc(same_ready, 1)
                    pipeline(dve, NGE, 1, half)

                @block.tensor
                def _(pe):
                    def half(new):
                        g, slot, use = new
                        for u in range(4):
                            pe.wait_ge(same_ready, 4 * g + u + 1)
                            pe.wait_ge(gathered[slot][u], 32 * (use + 1))
                            at_least(pe, sums_copied, 4 * g + u - 3)
                            for j in range(2):
                                last = nc.tensor.matmul(p_sum[u][:, j * ROW1:(j + 1) * ROW1], same[:, slot, 2 * u + j], h2s[:, slot, 2 * u + j], start=True, stop=True)
                            last.then_inc(summed, 1)
                    pipeline(pe, NGE, 1, half)

                @block.scalar
                def _(act):
                    def half(new):
                        g, slot, use = new
                        at_least(act, stored[slot], 16 * use)
                        for u in range(4):
                            act.wait_ge(summed, 4 * g + u + 1)
                            nc.scalar.activation(rows_sb[:, slot, 2 * u:2 * u + 2], p_sum[u][:, 0:2 * ROW1].rearrange("p (t c) -> p t c", t=2), ACT.Copy).then_inc(sums_copied, 1)
                    pipeline(act, NGE, 1, half)

        with phase() as (ctx, t, s):
            pbank = [ctx.enter_context(nc.psum_tensor(f"pn{n}", [P, 512], F32)) for n in range(4)]
            first_r, last_r, joined = t("first1", [RB, NB, ROW1]), t("last1", [RB, NB, ROW1]), t("joined1", [RB, NB, ROW1])
            sum_t, one_t = t("sum_t", [D, TE]), t("one_t", [1, TE])
            sum_c, one_c = t("sum_c", [D, TE + 1]), t("one_c", [1, TE + 1])
            ends_in, turned, copied, chained, back, joined_s, fixed = (s("n_" + n) for n in ("ends_in", "turned", "copied", "chained", "back", "joined", "fixed"))
            block = nc.Block()
            with block:
                @block.sync
                def _(sp):
                    ends = rows1[0:EP, :].rearrange("(b r e) c -> r b e c", b=NB, r=RB)
                    sp.dma_start(first_r[:], ends[:, :, 0, :]).then_inc(ends_in, 16)
                    sp.dma_start(last_r[:], ends[:, :, P - 1, :]).then_inc(ends_in, 16)

                @block.tensor
                def _(pe):
                    t_ = nc.tensor
                    pe.wait_ge(ends_in, 32)
                    for b in range(NB):
                        cols = slice(b * RB, (b + 1) * RB)
                        t_.transpose(pbank[0][:, cols], last_r[:, b, 0:D], ident[0:RB, 0:RB])
                        last = t_.transpose(pbank[1][0:1, cols], last_r[:, b, D:ROW1], ident[0:RB, 0:RB])
                    last.then_inc(turned, 1)
                    pe.wait_ge(chained, 2)
                    for b in range(NB):
                        cols, at = slice(b * RB, (b + 1) * RB), b % 3 * ROW1
                        t_.transpose(pbank[2 + b // 3][0:RB, at:at + D], sum_c[:, cols], ident[:])
                        last = t_.transpose(pbank[2 + b // 3][0:RB, at + D:at + ROW1], one_c[:, cols], ident[0:1, 0:1])
                    last.then_inc(back, 1)

                @block.vector
                def _(dve):
                    v = nc.vector
                    dve.wait_ge(turned, 1)
                    v.memset(sum_c[:, 0:1], 0.0)
                    v.memset(one_c[:, 0:1], 0.0)
                    v.tensor_copy(sum_t[:], pbank[0][:, 0:TE])
                    v.tensor_copy(one_t[:], pbank[1][0:1, 0:TE]).then_inc(copied, 1)
                    dve.wait_ge(copied, 1)
                    v.tensor_tensor_scan(sum_c[:, 1:TE + 1], through[:], sum_t[:], 0.0, ALU.mult, ALU.add).then_inc(chained, 1)
                    v.tensor_tensor_scan(one_c[:, 1:TE + 1], through[0:1, :], one_t[:], 0.0, ALU.mult, ALU.add).then_inc(chained, 1)
                    dve.wait_ge(back, 1)
                    for b in range(NB):
                        at = b % 3 * ROW1
                        last = v.tensor_tensor(joined[:, b, :], pbank[2 + b // 3][0:RB, at:at + ROW1], first_r[:, b, :], ALU.add)
                    last.then_inc(joined_s, 1)

                @block.gpsimd
                def _(pool):
                    pool.wait_ge(joined_s, 1)
                    for b in range(NB):
                        pool.indirect_dma_start(out=rows1, out_offset=bass.IndirectOffsetOnAxis(ap=fix_at[:, b:b + 1], axis=0),
                                                in_=joined[:, b, :], in_offset=None, bounds_check=EP - 1, oob_is_err=False).then_inc(fixed, 16)
                    pool.wait_ge(fixed, 16 * NB)

        with phase() as (ctx, t, s):
            x1_sb, agg = t("x1c", [P, 2, G, D]), t("aggc", [P, 2, G, ROW1])
            at_n = t("at_nc", [P, 2, G], I32)
            norm, dinv_g = t("normc", [P, 2, 2, G]), t("dinv_g", [P, 2, G])
            h2 = t("h2c", [P, G, D])
            mixed, base = t("mixed", [P, G, D]), t("basec", [P, 2, G, D])
            m_t = t("m_t", [P, 2, 4, P])
            total, leaky = t("total", [P, G, D]), t("leaky", [P, G, D])
            out_sb = t("out_sb", [P, 2, G, D])
            p_mt = [ctx.enter_context(nc.psum_tensor(f"p_mt{n}", [P, 512], F32)) for n in range(2)]
            p_w = [ctx.enter_context(nc.psum_tensor(f"p_w{n}", [P, 512], F32)) for n in range(2)]
            S = {n: s("c_" + n) for n in (
                "at_ready tab_ready h2_ready mixed_ready hb_ready base_ready turned copied multiplied total_ready leaky_ready out_ready").split()}
            x1_in, agg_in, out_out = ([s(f"c_{n}{a}") for a in range(2)] for n in ("x1_in", "agg_in", "out_out"))
            block = nc.Block()
            with block:
                @block.sync
                def _(sp):
                    def half(new, mid, old):
                        if new:
                            g, slot, use = new
                            at_least(sp, S["out_ready"], g - 1)
                            hold(sp, held)
                            sp.dma_start(x1_sb[:, slot], x1_table[bass.ds(first_row(g), GR), :].rearrange("(p t) d -> p t d", t=G)).then_inc(x1_in[slot], 16)
                        if old:
                            g, slot, use = old
                            if isinstance(g, int) and g == NGN - 1:
                                sp.wait_ge(out_out[1 - slot], 16 * ((g - 1) // 2 + 1))
                            sp.wait_ge(S["out_ready"], g + 1)
                            hold(sp, held)
                            sp.dma_start(out[bass.ds(first_row(g), GR), :].rearrange("(p t) d -> p t d", t=G), out_sb[:, slot]).then_inc(out_out[slot], 16)
                    pipeline(sp, NGN, 3, half)
                    for n in range(2):
                        sp.wait_ge(out_out[n], 16 * ((NGN - n + 1) // 2))

                @block.gpsimd
                def _(pool):
                    def gather(new):
                        g, slot, use = new
                        at_least(pool, agg_in[slot], 16 * G * use)
                        nc.gpsimd.tensor_copy(at_n[:, slot], node_row[:, bass.ds(g, 1), :].rearrange("p a t -> p (a t)")).then_inc(S["at_ready"], 1)
                        at_least(pool, S["base_ready"], g - 1)
                        at_least(pool, S["mixed_ready"], g - 1)
                        pool.wait_ge(S["at_ready"], g + 1)
                        hold(pool, held)
                        for k in range(G):
                            pool.indirect_dma_start(out=agg[:, slot, k], out_offset=None, in_=rows1,
                                                    in_offset=bass.IndirectOffsetOnAxis(ap=at_n[:, slot, k:k + 1], axis=0)).then_inc(agg_in[slot], 16)
                    pipeline(pool, NGN, 1, gather)

                @block.scalar
                def _(act):
                    a = nc.scalar

                    def half(new, old):
                        if new:
                            g, slot, use = new
                            act.wait_ge(S["tab_ready"], 2 * g + 2)
                            act.wait_ge(x1_in[slot], 16 * (use + 1))
                            at_least(act, S["hb_ready"], g)
                            at_least(act, S["mixed_ready"], g)
                            for k in range(G):
                                last = a.activation(h2[:, k], x1_sb[:, slot, k], ACT.Relu, bias=norm[:, slot, 1, k:k + 1], scale=norm[:, slot, 0, k:k + 1])
                            last.then_inc(S["h2_ready"], 1)
                            for q in range(2):
                                act.wait_ge(S["turned"], 2 * g + q + 1)
                                at_least(act, S["multiplied"], 2 * (g - 1) + q + 1)
                                a.activation(m_t[:, q].rearrange("p a b -> p (a b)"), p_mt[q][:, :], ACT.Copy).then_inc(S["copied"], 1)
                    pipeline(act, NGN, 2, half)

                @block.tensor
                def _(pe):
                    t_ = nc.tensor

                    def half(new):
                        g, slot, use = new
                        pe.wait_ge(S["mixed_ready"], g + 1)
                        for q in range(2):
                            at_least(pe, S["copied"], 2 * (g - 1) + q + 1)
                            for k in range(4):
                                last = t_.transpose(p_mt[q][:, k * P:(k + 1) * P], mixed[:, 4 * q + k], ident[:])
                            last.then_inc(S["turned"], 1)
                        for q in range(2):
                            pe.wait_ge(S["copied"], 2 * g + q + 1)
                            at_least(pe, S["total_ready"], 2 * (g - 1) + q + 1)
                            for k in range(4):
                                last = t_.matmul(p_w[q][:, k * D:(k + 1) * D], m_t[:, q, k], wl_t[:], start=True, stop=True)
                            last.then_inc(S["multiplied"], 1)
                    pipeline(pe, NGN, 1, half)

                @block.vector
                def _(dve):
                    v = nc.vector

                    def half(new, old):
                        if new:
                            g, slot, use = new
                            v.tensor_copy(norm[:, slot], stats2[:, bass.ds(g, 1)].rearrange("p a b c -> p (a b) c")).then_inc(S["tab_ready"], 1)
                            v.tensor_copy(dinv_g[:, slot], dinv[:, bass.ds(g, 1)].rearrange("p a t -> p (a t)")).then_inc(S["tab_ready"], 1)
                        if old:
                            g, slot, use = old
                            dve.wait_ge(S["base_ready"], g + 1)
                            for q in range(2):
                                dve.wait_ge(S["multiplied"], 2 * g + q + 1)
                                v.tensor_tensor(total[:, 4 * q:4 * q + 4].rearrange("p a b -> p (a b)"), p_w[q][:, :],
                                                base[:, slot, 4 * q:4 * q + 4].rearrange("p a b -> p (a b)"), ALU.add).then_inc(S["total_ready"], 1)
                            dve.wait_ge(S["total_ready"], 2 * g + 2)
                            v.scalar_tensor_tensor(leaky[:], total[:], 0.01, total[:], ALU.mult, ALU.max).then_inc(S["leaky_ready"], 1)
                            dve.wait_ge(S["leaky_ready"], g + 1)
                            at_least(dve, out_out[slot], 16 * use)
                            for k in range(G):
                                last = v.scalar_tensor_tensor(out_sb[:, slot, k], leaky[:, k], dinv_g[:, slot, k:k + 1], x1_sb[:, slot, k], ALU.mult, ALU.add)
                            last.then_inc(S["out_ready"], 1)
                        if new:
                            g, slot, use = new
                            dve.wait_ge(S["h2_ready"], g + 1)
                            dve.wait_ge(agg_in[slot], 16 * G * (use + 1))
                            at_least(dve, S["turned"], 2 * g)
                            v.tensor_tensor(mixed[:], h2[:], agg[:, slot, :, 0:D], ALU.mult).then_inc(S["mixed_ready"], 1)
                            v.tensor_tensor(base[:, slot], h2[:], bl_row[:].unsqueeze(1).broadcast_to([P, G, D]), ALU.add).then_inc(S["hb_ready"], 1)
                            dve.wait_ge(S["hb_ready"], g + 1)
                            v.tensor_tensor(base[:, slot], base[:, slot], agg[:, slot, :, D:ROW1].broadcast_to([P, G, D]), ALU.mult).then_inc(S["base_ready"], 1)
                    pipeline(dve, NGN, 2, half)


_INS = ["x", "src", "dst", "edge_attr_4", "L0_gnn_ln1_g", "L0_gnn_ln1_b", "L0_gnn_Wq", "L0_gnn_bq", "L0_gnn_Wk", "L0_gnn_bk",
        "L0_gnn_Wv", "L0_gnn_bv", "L0_gnn_We", "L0_gnn_Wskip", "L0_gnn_bskip", "L0_gnn_Wbeta", "L0_gnn_ln2_g", "L0_gnn_ln2_b",
        "L0_gnn_W1", "L0_gnn_b1", "L0_gnn_W2", "L0_gnn_b2", "L1_gnn_W1_w", "L1_gnn_W1_b"]


def kernel(**inputs):
    import numpy as _np
    import concourse.bacc as _bacc
    from concourse import mybir as _mybir
    from concourse.bass_utils import run_bass_kernel_spmd as _run

    nc = _bacc.Bacc("TRN2", target_bir_lowering=False, num_devices=1)
    arrays, args = {}, []
    for name in _INS:
        a = _np.ascontiguousarray(inputs[name])
        arrays[f"in_{name}_dram"] = a
        args.append(nc.dram_tensor(f"in_{name}_dram", a.shape, _mybir.dt.from_np(a.dtype), kind="ExternalInput").ap())
    shape = arrays["in_x_dram"].shape
    args.append(nc.dram_tensor("out_0_dram", shape, _mybir.dt.float32, kind="ExternalOutput").ap())
    build(nc, *args)
    r = _run(nc, [arrays], core_ids=[0])
    return r.results[0]["out_0_dram"]
```

```python
from contextlib import ExitStack, contextmanager

import numpy as np

import concourse.bass as bass
from concourse import mybir

F32 = mybir.dt.float32
I32 = mybir.dt.int32
U16 = mybir.dt.uint16
BF16 = mybir.dt.bfloat16
ALU = mybir.AluOpType
ACT = mybir.ActivationFunctionType
AX = mybir.AxisListType

P = 128
D = 128
H = 4
C = D // H
ED = 4
FF = 4 * D
G = 8
GR = G * P
META = ED + 2
MSG = D + H
ROW0 = MSG + H
ROW1 = D + 1
EPS = 1e-5
NEG = -3.0e38
FAR = 1.0e6
SCALE = float(C) ** -0.5


def at_least(eng, sem, value):
    if isinstance(value, int) and value <= 0:
        return
    eng.wait_ge(sem, value)


def hold(eng, sem):
    eng.sem_inc(sem, 1)


def pipeline(eng, n, depth, half, ways=2):
    def at(g):
        return (g, g % ways, g // ways) if 0 <= g < n else None

    start, end = -(-(depth - 1) // ways) + 1, (n - 1) // ways
    assert end > start
    for step in range(ways * start):
        half(*[at(step - d) for d in range(depth)])
    with eng.Fori(start, end) as i:
        for odd in range(ways):
            half(*[(ways * i + (odd - d), (odd - d) % ways, i + (odd - d) // ways) for d in range(depth)])
    for step in range(ways * end, n + depth - 1):
        half(*[at(step - d) for d in range(depth)])


class Chain:

    def __init__(self, eng, sem, base=0):
        self.eng, self.sem, self.base, self.k = eng, sem, base, 0

    def mark(self, ins):
        ins.then_inc(self.sem, 1)
        self.k += 1

    def wait(self):
        self.eng.wait_ge(self.sem, self.base + self.k)

    def step(self, ins):
        self.mark(ins)
        self.wait()


def build(nc, x, src, dst, ea, ln1g, ln1b, wq, bq, wk, bk, wv, bv, we, wskip, bskip, wbeta,
          ln2g, ln2b, w1, b1, w2, b2, wl, bl, out):
    N, E = x.shape[0], src.shape[0]
    NGN = -(-N // GR)
    NGE = -(-E // GR)
    TE, EP = NGE * G, NGE * GR
    HI = N // P + 1
    RB = max(r for r in range(1, P + 1) if TE % r == 0)
    NB = TE // RB
    HB = -(-HI // P)
    assert N >= 3 * GR and NGE >= 4 and E % 16 == 0 and N < 65536 and TE <= 512 and HI <= 512

    def first_row(g):
        return N - GR if isinstance(g, int) and g == NGN - 1 else g * GR

    def dram(name, shape, dt=F32):
        return nc.dram_tensor(name, shape, dt, kind="Internal").ap()

    dst_pad = dram("dst_pad", [EP + 2], I32)
    src_pad = dram("src_pad", [EP], I32)
    ea_pad = dram("ea_pad", [EP, ED])
    dst16 = dram("dst16", [EP], U16)
    pen_f = dram("pen_f", [EP])
    pen_b = dram("pen_b", [EP])
    through_d = dram("through_d", [TE])
    z_table = dram("z_table", [N + 1, D])
    rows0 = dram("rows0", [EP + 1, ROW0])
    rows1 = dram("rows1", [EP + 1, ROW1])
    x1_table = dram("x1_table", [N, D])
    h2_table = dram("h2_table", [N, ROW1])
    node_row_d = dram("node_row_d", [HI * P], I32)
    dinv_d = dram("dinv_d", [HI * P])

    with ExitStack() as top:
        def sb(name, shape, dt=F32, ctx=top):
            return ctx.enter_context(nc.sbuf_tensor(name, shape, dt))

        def sem(name, ctx=top):
            return ctx.enter_context(nc.semaphore(name))

        @contextmanager
        def phase():
            made = []

            def sem_of_phase(name):
                made.append(nc.alloc_semaphore(name))
                return made[-1]

            with ExitStack() as ctx:
                yield ctx, lambda name, shape, dt=F32: sb(name, shape, dt, ctx), sem_of_phase
            nc.clear_and_free_semaphores(made)
            nc.all_engine_barrier()

        held = sem("held")
        ident = sb("ident", [P, P])
        tri = sb("tri", [P, P])
        ones = sb("ones", [P, P])
        src_col = sb("src_col", [P, TE], I32)
        dst_col = sb("dst_col", [P, TE], I32)
        lohi = sb("lohi", [P, TE, 2])
        meta = sb("meta", [P, TE, META])
        iota16 = sb("iota16", [P, 512], U16)
        stats = sb("stats", [P, NGN, 4, G])
        stats2 = sb("stats2", [P, NGN, 2, G])
        deg = sb("deg", [P, HI])
        wq_t = sb("wq_t", [P, D])
        wkv_t = sb("wkv_t", [P, 2 * D])
        wsk_t = sb("wsk_t", [P, D + 1])
        w1_t = sb("w1_t", [P, FF])
        w2_t = sb("w2_t", [P, 4, D])
        wl_t = sb("wl_t", [P, D])
        wea = sb("wea", [G * META, G, 2 * D])
        bq_row = sb("bq_row", [P, D])
        bsk_row = sb("bsk_row", [P, D + 1])
        b2_row = sb("b2_row", [3, D])
        bkv = sb("bkv", [P, 2, D])
        we_sb = sb("we_sb", [ED, D])
        b1_col = sb("b1_col", [P, 4])
        ones3 = sb("ones3", [3, P], BF16)
        b2_parts = sb("b2_parts", [3, 4 * D], BF16)
        bsk_parts = sb("bsk_parts", [3, 2 * (D + 1)], BF16)
        bl_row = sb("bl_row", [P, D])
        wa_row = sb("wa_row", [P, D])
        half_neg = sb("half_neg", [P, 512])
        headmap = sb("headmap", [H, D])
        fix_at = sb("fix_at", [RB, NB], I32)
        through = sb("through", [P, TE])
        node_row = sb("node_row", [P, NGN, G], I32)
        dinv = sb("dinv", [P, NGN, G])

        with phase() as (ctx, t, s):
            pad_i = t("pad_i", [16, (EP - E + 16) // 16 + 1], I32)
            pad_z = t("pad_z", [16, (EP - E) * ED // 16])
            front = t("front", [1, 1], I32)
            dstw = t("dstw", [RB, NB, P + 2], I32)
            srcw = t("srcw", [RB, NB, P], I32)
            eaw = t("eaw", [RB, NB, P * ED])
            dstf = t("dstf", [RB, NB, P + 2])
            srcf = t("srcf", [RB, NB, P])
            d16 = t("d16", [RB, NB, P], U16)
            pf = t("pf", [RB, NB, P])
            pb = t("pb", [RB, NB, P])
            eq = t("eq", [RB, NB, P])
            cont = t("cont", [RB, NB])
            count = t("count", [RB, NB])
            thr = t("thr", [RB, NB])
            at0 = t("at0", [RB, NB])
            at1 = t("at1", [RB, NB])
            lohi_i = t("lohi_i", [P, TE, 2], I32)
            iota32 = t("iota32", [P, 512], I32)
            zrow = t("zrow", [1, ROW0])
            raw = t("raw", [P, 9, D])
            raw2 = t("raw2", [P, FF])
            rawe = t("rawe", [P, ED])
            gcol = t("gcol", [P, 2])
            bcol = t("bcol", [P, 2])
            b1raw = t("b1raw", [P, 4])
            bcast = t("bcast", [P, 2, D])
            brow = t("brow", [P, 6, D])
            wb = t("wb", [P, 3, D])
            plain = t("plain", [P, 8, D])
            tmp = t("tmp", [P, D])
            wb_row = t("wb_row", [P, D])
            pbank = [ctx.enter_context(nc.psum_tensor(f"pset{n}", [P, 512], F32)) for n in range(8)]

            pads_set, padded, edges_in, weights_in = s("pads_set"), s("padded"), s("edges_in"), s("weights_in")
            consts_set, pool_step, dve_step, cols_t = s("consts_set"), s("pool_step"), s("dve_step"), s("cols_t")
            rows_out, thr_out, thr_in, ea_t, w_t = s("rows_out"), s("thr_out"), s("thr_in"), s("ea_t"), s("w_t")
            floats_set, cols_copied, weights_copied, bias_t = s("floats_set"), s("cols_copied"), s("weights_copied"), s("bias_t")
            thr_set, rows_set = s("thr_set"), s("rows_set")
            ea_copied, we_t = s("ea_copied"), s("we_t")
            loads = [(raw[:, n, :], w) for n, w in enumerate((wq, wk, wv, wskip))]
            loads += [(raw[:, 4:8, :], w1.rearrange("(c p) k -> p c k", p=P)), (raw[:, 8, :], wl), (raw2[:], w2), (rawe[:], we)]
            loads += [(gcol[:, n:n + 1], v.unsqueeze(1)) for n, v in enumerate((ln1g, ln2g))]
            loads += [(bcol[:, n:n + 1], v.unsqueeze(1)) for n, v in enumerate((ln1b, ln2b))]
            loads += [(b1raw[:, n:n + 1], b1[n * P:(n + 1) * P].unsqueeze(1)) for n in range(4)]
            loads += [(brow[:, n, :], v.unsqueeze(0).broadcast_to([P, D])) for n, v in enumerate((bq, bk, bv, bskip, b2, bl))]
            loads += [(wb[:].rearrange("p a b -> p (a b)"), wbeta.broadcast_to([P, 3 * D]))]
            LOADS = 16 * len(loads)
            assert len(loads) <= 4 * 8
            WAYS, ZA = 4, 7
            x_sb, h_sb, z_sb = t("xa", [P, WAYS, G, D]), t("ha", [P, 2, G, D]), t("za", [P, 2, G, D])
            six = t("six", [P, 2, 2, G, 6])
            mv = t("mva", [P, 2, 2, G, 2])
            var = t("vara", [P, 2, 2, G])
            norm = t("norma", [P, 4, 4, G])
            x_in, z_out = [s(f"xa_in{n}") for n in range(WAYS)], [s(f"za_out{n}") for n in range(2)]
            bn_done, aggr_done, var_ready, rstd_ready, norm_ready = (
                [s(f"a_{name}{n}") for n in range(2)] for name in ("bn_done", "aggr_done", "var_ready", "rstd_ready", "norm_ready"))
            h_ready, za_ready, zd_ready, stats_kept = s("a_h_ready"), s("a_za_ready"), s("a_zd_ready"), s("a_stats_kept")

            def nodes_a_sync(sp):
                def half(load, old):
                    if load:
                        g, slot, use = load
                        at_least(sp, h_ready, 2 * (g - WAYS + 1))
                        hold(sp, held)
                        rows = x[bass.ds(first_row(g), GR), :].rearrange("(p t) d -> p t d", t=G)
                        sp.dma_start(x_sb[:, slot], rows).then_inc(x_in[slot], 16)
                        if isinstance(g, int):
                            for to, of in loads[4 * g:4 * g + 4]:
                                sp.dma_start(to, of).then_inc(weights_in, 16)
                    if old:
                        g, slot, use = old
                        if isinstance(g, int) and g == NGN - 1:
                            sp.wait_ge(z_out[(g - 1) % 2], 16 * ((g - 1) // 2 + 1))
                        sp.wait_ge(za_ready, g + 1)
                        hold(sp, held)
                        sp.wait_ge(zd_ready, g + 1)
                        hold(sp, held)
                        rows = z_table[bass.ds(first_row(g), GR), :].rearrange("(p t) d -> p t d", t=G)
                        sp.dma_start(rows, z_sb[:, slot % 2]).then_inc(z_out[slot % 2], 16)
                pipeline(sp, NGN, 5, lambda load, a, b, c, old: half(load, old), WAYS)
                for n in range(2):
                    sp.wait_ge(z_out[n], 16 * ((NGN - n + 1) // 2))

            def nodes_a_vector(dve):
                v = nc.vector

                def moments(g, slot, which, rows, ready):
                    par = slot % 2
                    for k in range(G):
                        ready(k)
                        last = v.bn_stats(six[:, which, par, k], rows[:, k])
                    last.then_inc(bn_done[which], 1)
                    dve.wait_ge(bn_done[which], g + 1)
                    hold(dve, held)
                    for k in range(G):
                        last = v.bn_aggr(mv[:, which, par, k], six[:, which, par, k])
                    last.then_inc(aggr_done[which], 1)
                    dve.wait_ge(aggr_done[which], g + 1)
                    at_least(dve, rstd_ready[which], g - 1)
                    v.tensor_scalar(var[:, which, par], mv[:, which, par, :, 1], EPS, None, ALU.add).then_inc(var_ready[which], 1)

                def offset(g, slot, which):
                    dve.wait_ge(rstd_ready[which], g + 1)
                    v.scalar_tensor_tensor(norm[:, slot, 2 * which + 1], mv[:, which, slot % 2, :, 0], -1.0,
                                           norm[:, slot, 2 * which], ALU.mult, ALU.mult).then_inc(norm_ready[which], 1)

                def half(new, mid, old):
                    if new:
                        g, slot, use = new
                        dve.wait_ge(x_in[slot], 16 * (use + 1))
                        moments(g, slot, 0, x_sb[:, slot], lambda k: None)
                    if old:
                        g, slot, use = old
                        offset(g, slot, 1)
                        dve.wait_ge(norm_ready[1], g + 1)
                        at_least(dve, z_out[slot % 2], 16 * (2 * use + slot // 2))
                        for k in range(ZA, G):
                            last = v.tensor_scalar(z_sb[:, slot % 2, k], h_sb[:, slot % 2, k], norm[:, slot, 2, k:k + 1],
                                                   norm[:, slot, 3, k:k + 1], ALU.mult, ALU.add)
                        last.then_inc(zd_ready, 1)
                        v.tensor_copy(stats[:, bass.ds(g, 1)].rearrange("p a b c -> p (a b) c"), norm[:, slot]).then_inc(stats_kept, 1)
                    if mid:
                        g, slot, use = mid
                        moments(g, slot, 1, h_sb[:, slot % 2], lambda k: dve.wait_ge(h_ready, 2 * g + k // 4 + 1) if k % 4 == 0 else None)
                    if new:
                        offset(new[0], new[1], 0)
                pipeline(dve, NGN, 3, half, WAYS)

            def nodes_a_gpsimd(pool):
                def power(g, slot, which):
                    pool.wait_ge(var_ready[which], g + 1)
                    at_least(pool, stats_kept, g - 3)
                    nc.gpsimd.tensor_tensor(norm[:, slot, 2 * which], var[:, which, slot % 2], half_neg[:, 0:G], ALU.pow).then_inc(rstd_ready[which], 1)

                def half(new, mid):
                    if new:
                        power(new[0], new[1], 0)
                        if isinstance(new[0], int) and new[0] == 3:
                            pool.wait_ge(padded, 11 * 16)
                            for b in range(NB):
                                window = bass.AP(dst_pad.tensor, b * RB * P, [[P, RB], [1, P + 2]])
                                pool.dma_start(dstw[:, b, :], window).then_inc(edges_in, 16)
                            pool.dma_start(srcw[:], src_pad.rearrange("(b r e) -> r b e", b=NB, r=RB)).then_inc(edges_in, 16)
                            pool.dma_start(eaw[:], ea_pad.rearrange("(b r e) j -> r b (e j)", b=NB, r=RB)).then_inc(edges_in, 16)
                    if mid:
                        power(mid[0], mid[1], 1)
                pipeline(pool, NGN, 2, half, WAYS)

            def nodes_a_scalar(act):
                def half(mid, old):
                    if mid:
                        g, slot, use = mid
                        act.wait_ge(norm_ready[0], g + 1)
                        at_least(act, zd_ready, g - 1)
                        at_least(act, za_ready, g - 1)
                        for k in range(G):
                            last = nc.scalar.activation(h_sb[:, slot % 2, k], x_sb[:, slot, k], ACT.Relu, bias=norm[:, slot, 1, k:k + 1],
                                                        scale=norm[:, slot, 0, k:k + 1])
                            if k % 4 == 3:
                                last.then_inc(h_ready, 1)
                    if old:
                        g, slot, use = old
                        act.wait_ge(norm_ready[1], g + 1)
                        at_least(act, z_out[slot % 2], 16 * (2 * use + slot // 2))
                        for k in range(ZA):
                            last = nc.scalar.activation(z_sb[:, slot % 2, k], h_sb[:, slot % 2, k], ACT.Identity, bias=norm[:, slot, 3, k:k + 1],
                                                        scale=norm[:, slot, 2, k:k + 1])
                        last.then_inc(za_ready, 1)
                pipeline(act, NGN, 2, half, WAYS)

            block = nc.Block()
            with block:
                @block.sync
                def _(sp):
                    nodes_a_sync(sp)
                    sp.wait_ge(rows_set, 3)
                    for table, rows in ((dst16, d16), (pen_f, pf), (pen_b, pb)):
                        sp.dma_start(table.rearrange("(b r e) -> r b e", b=NB, r=RB), rows[:]).then_inc(rows_out, 16)
                    sp.wait_ge(thr_set, 1)
                    for b in range(NB):
                        sp.dma_start(through_d[b * RB:(b + 1) * RB].unsqueeze(1), thr[:, b:b + 1]).then_inc(thr_out, 16)
                    sp.wait_ge(thr_out, 16 * NB)
                    sp.dma_start(through[:], through_d.unsqueeze(0).broadcast_to([P, TE])).then_inc(thr_in, 16)
                    sp.wait_ge(thr_in, 16)
                    sp.wait_ge(rows_out, 48)

                @block.scalar
                def _(act):
                    act.dma_start(src_pad[0:E].rearrange("(a b) -> a b", a=16), src.rearrange("(a b) -> a b", a=16)).then_inc(padded, 16)
                    act.dma_start(dst_pad[1:E + 1].rearrange("(a b) -> a b", a=16), dst.rearrange("(a b) -> a b", a=16)).then_inc(padded, 16)
                    act.dma_start(ea_pad[0:E, :].rearrange("(a b) j -> a (b j)", a=16), ea.rearrange("(a b) j -> a (b j)", a=16)).then_inc(padded, 16)
                    act.wait_ge(pads_set, 4)
                    n = (EP - E) // 16
                    act.dma_start(dst_pad[0:1].unsqueeze(0), front[:]).then_inc(padded, 16)
                    act.dma_start(dst_pad[E + 1:EP + 1].rearrange("(a b) -> a b", a=16), pad_i[:, 0:n]).then_inc(padded, 16)
                    act.dma_start(dst_pad[EP + 1:EP + 2].unsqueeze(0), pad_i[0:1, 0:1]).then_inc(padded, 16)
                    act.dma_start(ea_pad[E:EP, :].rearrange("(a b) j -> a (b j)", a=16), pad_z[:]).then_inc(padded, 16)
                    act.dma_start(src_pad[E:EP].rearrange("(a b) -> a b", a=16), pad_z[:, 0:n].bitcast(I32)).then_inc(padded, 16)
                    act.dma_start(z_table[N:N + 1, :], zrow[:, 0:D]).then_inc(padded, 16)
                    act.dma_start(rows0[EP:EP + 1, :], zrow[:]).then_inc(padded, 16)
                    act.dma_start(rows1[EP:EP + 1, :], zrow[:, 0:ROW1]).then_inc(padded, 16)
                    nodes_a_scalar(act)

                @block.gpsimd
                def _(pool):
                    chain = Chain(pool, pool_step)
                    g = nc.gpsimd
                    chain.mark(g.memset(ident[:], 0.0))
                    chain.mark(g.memset(tri[:], 1.0))
                    chain.mark(g.memset(headmap[:], 1.0))
                    chain.mark(g.memset(half_neg[:], -0.5))
                    chain.step(g.iota(iota32[:], pattern=[[1, 512]], base=0, channel_multiplier=0))
                    chain.mark(g.affine_select(out=ident[:], in_=ident[:], compare_op=ALU.not_equal, fill=1.0, base=0,
                                               pattern=[[-1, P]], channel_multiplier=1))
                    chain.mark(g.affine_select(out=tri[:], in_=tri[:], compare_op=ALU.is_ge, fill=0.0, base=0,
                                               pattern=[[1, P]], channel_multiplier=-1))
                    chain.step(g.affine_select(out=headmap[:], in_=headmap[:], compare_op=ALU.is_ge, fill=0.0, base=0,
                                               pattern=[[1, D]], channel_multiplier=-C))
                    g.affine_select(out=headmap[:], in_=headmap[:], compare_op=ALU.is_ge, fill=0.0, base=C - 1,
                                    pattern=[[-1, D]], channel_multiplier=C).then_inc(consts_set, 1)
                    g.tensor_copy(iota16[:], iota32[:]).then_inc(consts_set, 1)
                    nodes_a_gpsimd(pool)

                @block.vector
                def _(dve):
                    v = nc.vector
                    chain = Chain(dve, dve_step)
                    v.memset(pad_i[:], N).then_inc(pads_set, 1)
                    v.memset(pad_z[:], 0.0).then_inc(pads_set, 1)
                    v.memset(front[:], -1).then_inc(pads_set, 1)
                    v.memset(zrow[:], 0.0).then_inc(pads_set, 1)
                    nodes_a_vector(dve)
                    chain.mark(v.memset(ones[:], 1.0))
                    chain.mark(v.memset(meta[:], 1.0))
                    dve.wait_ge(edges_in, 16 * (NB + 2))
                    v.tensor_copy(srcf[:], srcw[:]).then_inc(floats_set, 1)
                    v.tensor_copy(dstf[:], dstw[:]).then_inc(floats_set, 1)
                    dve.wait_ge(floats_set, 2)
                    v.tensor_copy(d16[:], dstf[:, :, 1:P + 1]).then_inc(rows_set, 1)
                    chain.mark(v.tensor_tensor(pf[:], dstf[:, :, 1:P + 1], dstf[:, :, 0:P], ALU.not_equal))
                    chain.mark(v.tensor_tensor(pb[:], dstf[:, :, 1:P + 1], dstf[:, :, 2:P + 2], ALU.not_equal))
                    chain.mark(v.tensor_tensor(cont[:], dstf[:, :, 1], dstf[:, :, 0], ALU.is_equal))
                    first = dstf[:, :, 1:2].broadcast_to([RB, NB, P])
                    chain.step(v.tensor_tensor(eq[:], dstf[:, :, 1:P + 1], first, ALU.is_equal))
                    v.tensor_scalar(pf[:], pf[:], NEG, None, ALU.mult).then_inc(rows_set, 1)
                    v.tensor_scalar(pb[:], pb[:], NEG, None, ALU.mult).then_inc(rows_set, 1)
                    chain.step(v.tensor_reduce(count[:], eq[:], AX.X, ALU.add))
                    chain.step(v.tensor_scalar(at0[:], count[:], float(P), None, ALU.is_equal))
                    v.tensor_tensor(thr[:], at0[:], cont[:], ALU.mult).then_inc(thr_set, 1)
                    chain.mark(v.tensor_scalar(at1[:], cont[:], -FAR, FAR, ALU.mult, ALU.add))
                    dve.wait_ge(consts_set, 2)
                    for b in range(NB):
                        dve.wait_ge(cols_t, b + 1)
                        cols = slice(b * RB, (b + 1) * RB)
                        chain.mark(v.tensor_copy(src_col[:, cols], pbank[b % 2][:, 0:RB]))
                        chain.mark(v.tensor_copy(meta[:, cols, META - 1], pbank[b % 2][:, P:P + RB]))
                        v.tensor_copy(dst_col[:, cols], pbank[b % 2][:, P:P + RB]).then_inc(cols_copied, 1)
                    for b in range(NB):
                        dve.wait_ge(ea_t, b + 1)
                        cols = slice(b * RB, (b + 1) * RB)
                        v.tensor_copy(meta[:, cols, 0:ED].rearrange("p r j -> p j r"),
                                      pbank[2 + b % 2][:, :].rearrange("p (j r) -> p j r", j=ED)[:, :, 0:RB]).then_inc(ea_copied, 1)
                    dve.wait_ge(cols_copied, NB)
                    chain.mark(v.tensor_scalar(lohi_i[:, :, 0], dst_col[:], P - 1, None, ALU.bitwise_and))
                    chain.step(v.tensor_scalar(lohi_i[:, :, 1], dst_col[:], 7, None, ALU.logical_shift_right))
                    chain.mark(v.tensor_copy(lohi[:], lohi_i[:]))
                    chain.step(v.tensor_scalar(at0[:], iota16[0:RB, 0:NB], float(RB * P), float(-1 - P), ALU.mult, ALU.add))
                    chain.step(v.tensor_tensor(at0[:], at0[:], at1[:], ALU.add))
                    chain.step(v.tensor_tensor(at0[:], at0[:], count[:], ALU.add))
                    dve.wait_ge(we_t, 2)
                    chain.mark(v.scalar_tensor_tensor(fix_at[:], pbank[6][0:RB, 0:NB], float(P), at0[:], ALU.mult, ALU.add))
                    chain.mark(v.tensor_copy(we_sb[:], pbank[7][0:ED, 0:D]))
                    dve.wait_ge(weights_in, LOADS)
                    dve.wait_ge(w_t, 1)
                    chain.mark(v.tensor_copy(plain[:, 0:4, :], pbank[4][:, :].rearrange("p (a b) -> p a b", a=4)))
                    dve.wait_ge(w_t, 2)
                    chain.mark(v.tensor_copy(plain[:, 4:8, :], pbank[5][:, :].rearrange("p (a b) -> p a b", a=4)))
                    dve.wait_ge(w_t, 3)
                    chain.mark(v.tensor_copy(w2_t[:], pbank[0][:, :].rearrange("p (a b) -> p a b", a=4)))
                    dve.wait_ge(w_t, 4)
                    chain.mark(v.tensor_copy(wl_t[:], pbank[1][:, 0:D]))
                    chain.mark(v.tensor_copy(bcast[:, 0, :], bcol[:, 0:1].broadcast_to([P, D])))
                    chain.step(v.tensor_copy(bcast[:, 1, :], bcol[:, 1:2].broadcast_to([P, D])))
                    v.tensor_scalar(wq_t[:], plain[:, 0, :], gcol[:, 0:1], None, ALU.mult).then_inc(weights_copied, 1)
                    chain.mark(v.tensor_scalar(wkv_t[:, 0:D], plain[:, 1, :], gcol[:, 0:1], None, ALU.mult))
                    chain.mark(v.tensor_scalar(wkv_t[:, D:2 * D], plain[:, 2, :], gcol[:, 0:1], None, ALU.mult))
                    chain.mark(v.tensor_scalar(wsk_t[:, 0:D], plain[:, 3, :], gcol[:, 0:1], None, ALU.mult))
                    chain.mark(v.tensor_scalar(w1_t[:], plain[:, 4:8, :].rearrange("p a b -> p (a b)"), gcol[:, 1:2], None, ALU.mult))
                    chain.mark(v.tensor_tensor(wa_row[:], wb[:, 0, :], wb[:, 2, :], ALU.add))
                    chain.step(v.tensor_tensor(wb_row[:], wb[:, 1, :], wb[:, 2, :], ALU.subtract))
                    chain.step(v.tensor_tensor(tmp[:], wsk_t[:, 0:D], wb_row[:], ALU.mult))
                    chain.step(v.tensor_reduce(wsk_t[:, D:D + 1], tmp[:], AX.X, ALU.add))
                    dve.wait_ge(bias_t, 2)
                    chain.mark(v.tensor_tensor(bq_row[:], pbank[2][:, 0:D], brow[:, 0, :], ALU.add))
                    chain.mark(v.tensor_tensor(bsk_row[:, 0:D], pbank[2][:, 3 * D:4 * D], brow[:, 3, :], ALU.add))
                    chain.mark(v.tensor_copy(bl_row[:], brow[:, 5, :]))
                    chain.mark(v.tensor_tensor(b1_col[:], pbank[3][:, 0:4], b1raw[:], ALU.add))
                    chain.mark(v.tensor_copy(b2_row[:], brow[0:3, 4, :]))
                    chain.mark(v.tensor_tensor(bkv[:].rearrange("p a b -> p (a b)"), pbank[2][:, D:3 * D],
                                               brow[:, 1:3, :].rearrange("p a b -> p (a b)"), ALU.add))
                    chain.wait()
                    chain.step(v.tensor_tensor(tmp[:], bsk_row[:, 0:D], wb_row[:], ALU.mult))
                    chain.step(v.tensor_reduce(bsk_row[:, D:D + 1], tmp[:], AX.X, ALU.add))

                @block.tensor
                def _(pe):
                    t_ = nc.tensor
                    pe.wait_ge(consts_set, 1)
                    pe.wait_ge(floats_set, 2)
                    for b in range(NB):
                        if b >= 2:
                            pe.wait_ge(cols_copied, b - 1)
                        t_.transpose(pbank[b % 2][:, 0:RB], srcf[:, b, :], ident[0:RB, 0:RB])
                        t_.transpose(pbank[b % 2][:, P:P + RB], dstf[:, b, 1:P + 1], ident[0:RB, 0:RB]).then_inc(cols_t, 1)
                    for b in range(NB):
                        if b >= 2:
                            pe.wait_ge(ea_copied, b - 1)
                        for j in range(ED):
                            last = t_.transpose(pbank[2 + b % 2][:, j * P:j * P + RB],
                                                eaw[:, b, :].rearrange("r (e j) -> r e j", j=ED)[:, :, j], ident[0:RB, 0:RB])
                        last.then_inc(ea_t, 1)
                    pe.wait_ge(dve_step, 1)
                    t_.matmul(pbank[6][:, 0:P], tri[:], ones[:], start=True, stop=True).then_inc(we_t, 1)
                    pe.wait_ge(weights_in, LOADS)
                    t_.transpose(pbank[7][0:ED, 0:D], rawe[:], ident[:]).then_inc(we_t, 1)
                    for n in range(8):
                        last = t_.transpose(pbank[4 + n // 4][:, n % 4 * D:(n % 4 + 1) * D], raw[:, n, :], ident[:])
                        if n % 4 == 3:
                            last.then_inc(w_t, 1)
                    pe.wait_ge(cols_copied, NB)
                    for n in range(4):
                        last = t_.transpose(pbank[0][:, n * D:(n + 1) * D], raw2[:, n * D:(n + 1) * D], ident[:])
                    last.then_inc(w_t, 1)
                    t_.transpose(pbank[1][:, 0:D], raw[:, 8, :], ident[:]).then_inc(w_t, 1)
                    pe.wait_ge(weights_copied, 1)
                    pe.wait_ge(ea_copied, NB)
                    t_.matmul(pbank[2][:, :], bcast[:, 0, :], plain[:, 0:4, :].rearrange("p a b -> p (a b)"),
                              start=True, stop=True).then_inc(bias_t, 1)
                    for n in range(4):
                        last = t_.matmul(pbank[3][:, n:n + 1], plain[:, 4 + n, :], bcol[:, 1:2], start=True, stop=True)
                    last.then_inc(bias_t, 1)


        with phase() as (ctx, t, s):
            ps = lambda name: ctx.enter_context(nc.psum_tensor(name, [P, 512], F32))
            zs, zd = t("zs", [P, 2, G, D]), t("zd", [P, 2, G, D])
            at_s, at_d = t("at_s", [P, 2, G], I32), t("at_d", [P, 2, G], I32)
            z_t = t("z_t", [P, 2, 4, P])
            metag = t("metag", [P, 2, G, META])
            lohig = t("lohig", [P, 2, G, 2])
            ea_tr = t("ea_tr", [G * META, 2, P])
            q_sb, prod = t("q_sb", [P, 2, D]), t("prod", [P, 2, D])
            alpha = t("alpha", [P, 2, G, H])
            v_sb = t("v_sb", [P, 2, G, D])
            penf_sb, penb_sb = t("penf_sb", [G * H, 2, P]), t("penb_sb", [G * H, 2, P])
            dst_sb = t("dst_sb", [P, 2, GR], U16)
            run_max, seg_max = t("run_max", [G * H, P]), t("seg_max", [G * H, P])
            below, weight = t("below", [G * H, P]), t("weight", [G * H, P])
            msgs = t("msgs", [P, 2, G, MSG])
            same = t("same", [P, 2, G, P])
            is_lo, is_hi = t("is_lo", [P, 2, G, P], BF16), t("is_hi", [P, 2, G, HI], BF16)
            rows_sb = t("rows_sb", [P, 2, G, ROW0])
            p_tr = [ps("p_tr0"), ps("p_tr1")]
            p_qk = [ps("p_qk0"), ps("p_qk1")]
            p_v, p_small, p_sum, p_deg = ps("p_v"), ps("p_small"), ps("p_sum"), ps("p_deg")
            p_alpha, p_back, p_ea = p_small[0:G * H, 0:P], p_small[:, P:P + 2 * G * H], p_small[0:G * META, 256:256 + P]

            gathered = [[s(f"gathered{a}{b}") for b in range(4)] for a in range(2)]
            dst_in, pen_in, stored = ([s(f"{n}{a}") for a in range(2)] for n in ("e0_dst_in", "e0_pen_in", "e0_stored"))
            turned, z_copied, projected, valued, q_ready, scored, v_copied = (s(n) for n in ("turned", "z_copied", "projected", "valued", "q_ready", "scored", "v_copied"))
            meta_ready, ea_turned, ea_ready, alpha_ready, alpha_turned = (s(n) for n in ("meta_ready", "ea_turned", "ea_ready", "alpha_ready", "alpha_turned"))
            scanned, weighted, back_turned, weights_ready = (s(n) for n in ("scanned", "weighted", "back_turned", "weights_ready"))
            same_ready, msg_ready, summed, sums_copied, prod_ready, counted = (s(n) for n in ("same_ready", "msg_ready", "summed", "sums_copied", "prod_ready", "counted"))
            at_ready, deg_done = s("at_ready"), s("deg_done")
            wea1 = t("wea1", [META, 2 * D])
            part1, part2, part3 = (t(f"bias_part{n}", [3, D + 1], BF16) for n in range(3))
            rest, mixed3 = t("bias_rest", [3, D + 1]), t("mixed3", [3, D + 1])
            zeroed, wea1_done, wea_done, e0_step = s("zeroed"), s("wea1_done"), s("wea_done"), s("e0_step")
            block = nc.Block()
            with block:
                @block.gpsimd
                def _(pool):
                    def gather(g, slot, use):
                        for u in range(4):
                            at_least(pool, gathered[slot][u], 64 * use)
                        nc.gpsimd.tensor_copy(at_s[:, slot], src_col[:, bass.ds(g * G, G)]).then_inc(at_ready, 1)
                        nc.gpsimd.tensor_copy(at_d[:, slot], dst_col[:, bass.ds(g * G, G)]).then_inc(at_ready, 1)
                        for u in range(4):
                            at_least(pool, turned, 4 * g + u - 7)
                            pool.wait_ge(at_ready, 2 * g + 2)
                            hold(pool, held)
                            for k in (2 * u, 2 * u + 1):
                                for to, at in ((zs, at_s), (zd, at_d)):
                                    pool.indirect_dma_start(out=to[:, slot, k], out_offset=None, in_=z_table,
                                                            in_offset=bass.IndirectOffsetOnAxis(ap=at[:, slot, k:k + 1], axis=0)
                                                            ).then_inc(gathered[slot][u], 16)
                    pipeline(pool, NGE, 1, lambda new: gather(*new))

                @block.sync
                def _(sp):
                    def half(new, old):
                        if new:
                            g, slot, use = new
                            at_least(sp, same_ready, 4 * (g - 1))
                            hold(sp, held)
                            sp.dma_start(dst_sb[:, slot], dst16[bass.ds(g * GR, GR)].unsqueeze(0).broadcast_to([P, GR])).then_inc(dst_in[slot], 16)
                            at_least(sp, scanned, 3 * (g - 1))
                            hold(sp, held)
                            for to, of in ((penf_sb, pen_f), (penb_sb, pen_b)):
                                rows = of[bass.ds(g * GR, GR)].rearrange("(t e) -> t e", t=G).unsqueeze(1).broadcast_to([G, H, P])
                                sp.dma_start(to[:, slot], rows).then_inc(pen_in[slot], 16)
                        if old:
                            g, slot, use = old
                            sp.wait_ge(sums_copied, 4 * g + 4)
                            hold(sp, held)
                            rows = rows0[bass.ds(g * GR, GR), :].rearrange("(t p) c -> p t c", p=P)
                            sp.dma_start(rows, rows_sb[:, slot]).then_inc(stored[slot], 16)
                    pipeline(sp, NGE, 2, half)
                    for n in range(2):
                        sp.wait_ge(stored[n], 16 * ((NGE - n + 1) // 2))

                @block.tensor
                def _(pe):
                    t_ = nc.tensor

                    def turn_ea(g, slot, use):
                        pe.wait_ge(meta_ready, 2 * g + 2)
                        at_least(pe, weights_ready, 2 * g - 2)
                        hold(pe, held)
                        t_.transpose(p_ea, metag[:, slot].rearrange("p t j -> p (t j)"), ident[:]).then_inc(ea_turned, 1)

                    def turn(g, slot, use, u):
                        pe.wait_ge(gathered[slot][u], 64 * (use + 1))
                        at_least(pe, z_copied, 4 * g + u - 1)
                        for j, z in enumerate((zs, zd)):
                            for k in range(2):
                                last = t_.transpose(p_tr[u % 2][:, (2 * j + k) * P:(2 * j + k + 1) * P], z[:, slot, 2 * u + k], ident[:])
                        last.then_inc(turned, 1)

                    def project(g, slot, use, u):
                        pe.wait_ge(z_copied, 4 * g + u + 1)
                        pe.wait_ge(ea_ready, g + 1)
                        at_least(pe, scored, 4 * g + u - 1)
                        for k in range(2):
                            q, key = (p_qk[u % 2][:, (2 * k + j) * D:(2 * k + j + 1) * D] for j in range(2))
                            t_.matmul(q, z_t[:, u % 2, 2 + k], wq_t[:], start=True, stop=True)
                            t_.matmul(key, z_t[:, u % 2, k], wkv_t[:, 0:D], start=True, stop=False)
                            last = t_.matmul(key, ea_tr[:, slot], wea[:, 2 * u + k, 0:D], start=False, stop=True)
                        last.then_inc(projected, 1)
                        at_least(pe, v_copied, 4 * g + u)
                        for k in range(2):
                            val = p_v[:, k * D:(k + 1) * D]
                            t_.matmul(val, z_t[:, u % 2, k], wkv_t[:, D:2 * D], start=True, stop=False)
                            last = t_.matmul(val, ea_tr[:, slot], wea[:, 2 * u + k, D:2 * D], start=False, stop=True)
                        last.then_inc(valued, 1)

                    def count(g, slot, use, u):
                        pe.wait_ge(counted, 4 * g + u + 1)
                        for k in (2 * u, 2 * u + 1):
                            first = isinstance(g, int) and g == 0 and k == 0
                            final = isinstance(g, int) and g == NGE - 1 and k == G - 1
                            last = t_.matmul(p_deg[:, 0:HI], is_lo[:, slot, k], is_hi[:, slot, k], start=first, stop=final)
                        last.then_inc(deg_done, 1)

                    def add_up(g, slot, use, u):
                        pe.wait_ge(msg_ready, 4 * g + u + 1)
                        at_least(pe, sums_copied, 4 * g + u)
                        for k in (2 * u, 2 * u + 1):
                            last = t_.matmul(p_sum[:, k % 2 * MSG:(k % 2 + 1) * MSG], same[:, slot, k], msgs[:, slot, k], start=True, stop=True)
                        last.then_inc(summed, 1)

                    def half(new, old):
                        if new:
                            turn_ea(*new)
                            turn(*new, 0)
                        if old:
                            pe.wait_ge(alpha_ready, old[0] + 1)
                            pe.wait_ge(ea_ready, old[0] + (2 if new else 1))
                            t_.transpose(p_alpha, alpha[:, old[1]].rearrange("p t h -> p (t h)"), ident[:]).then_inc(alpha_turned, 1)
                        if new:
                            turn(*new, 1)
                            project(*new, 0)
                        if old:
                            count(*old, 0)
                            pe.wait_ge(weighted, old[0] + 1)
                            hold(pe, held)
                            t_.transpose(p_back[:, 0:G * H], weight[:], ident[0:G * H, 0:G * H])
                            t_.transpose(p_back[:, G * H:2 * G * H], seg_max[:], ident[0:G * H, 0:G * H]).then_inc(back_turned, 1)
                        if new:
                            turn(*new, 2)
                            project(*new, 1)
                        if old:
                            count(*old, 1)
                            add_up(*old, 0)
                        if new:
                            turn(*new, 3)
                            project(*new, 2)
                        if old:
                            count(*old, 2)
                            add_up(*old, 1)
                        if new:
                            project(*new, 3)
                        if old:
                            count(*old, 3)
                            add_up(*old, 2)
                            add_up(*old, 3)
                    pe.wait_ge(wea_done, 16 * G)
                    pipeline(pe, NGE, 2, half)

                @block.scalar
                def _(act):
                    a = nc.scalar

                    def copy_z(g, slot, use, u):
                        act.wait_ge(turned, 4 * g + u + 1)
                        at_least(act, valued, 4 * g + u - 1)
                        a.activation(z_t[:, u % 2].rearrange("p a b -> p (a b)"), p_tr[u % 2][:, :], ACT.Copy).then_inc(z_copied, 1)

                    def copy_v(g, slot, use, u):
                        act.wait_ge(valued, 4 * g + u + 1)
                        at_least(act, msg_ready, 4 * g + u - 7)
                        a.activation(v_sb[:, slot, 2 * u:2 * u + 2], p_v[:, 0:2 * D].rearrange("p (t c) -> p t c", t=2), ACT.Copy).then_inc(v_copied, 1)

                    def copy_sums(g, slot, use, u):
                        act.wait_ge(summed, 4 * g + u + 1)
                        a.activation(rows_sb[:, slot, 2 * u:2 * u + 2, 0:MSG], p_sum[:, 0:2 * MSG].rearrange("p (t c) -> p t c", t=2), ACT.Copy).then_inc(sums_copied, 1)

                    def half(new, old):
                        if new:
                            g, slot, use = new
                            act.wait_ge(ea_turned, g + 1)
                            a.activation(ea_tr[:, slot], p_ea, ACT.Copy).then_inc(ea_ready, 1)
                            copy_z(*new, 0)
                        if old:
                            g, slot, use = old
                            act.wait_ge(scanned, 3 * g + 3)
                            at_least(act, back_turned, g)
                            a.activation(weight[:], below[:], ACT.Exp, scale=SCALE).then_inc(weighted, 1)
                        if new:
                            copy_z(*new, 1)
                            copy_v(*new, 0)
                        if old:
                            act.wait_ge(back_turned, g + 1)
                            at_least(act, summed, 4 * (g - 1))
                            a.activation(msgs[:, slot, :, D:MSG], p_back[:, 0:G * H].rearrange("p (t h) -> p t h", t=G), ACT.Copy).then_inc(weights_ready, 1)
                            at_least(act, stored[slot], 16 * use)
                            a.activation(rows_sb[:, slot, :, MSG:ROW0], p_back[:, G * H:2 * G * H].rearrange("p (t h) -> p t h", t=G), ACT.Copy).then_inc(weights_ready, 1)
                        for u in (0, 1, 2):
                            if new and u < 2:
                                copy_z(*new, u + 2)
                            if new:
                                copy_v(*new, u + 1)
                            if old:
                                copy_sums(*old, u)
                        if old:
                            copy_sums(*old, 3)
                    act.wait_ge(zeroed, 2)
                    for n in range(2):
                        act.dma_start(wea1[0:ED, n * D:(n + 1) * D], we_sb[:]).then_inc(wea1_done, 16)
                        act.dma_start(wea1[ED:ED + 1, n * D:(n + 1) * D], bkv[0:1, n, :]).then_inc(wea1_done, 16)
                    act.wait_ge(wea1_done, 64)
                    for j in range(G):
                        act.dma_start(wea[j * META:(j + 1) * META, j, :], wea1[:]).then_inc(wea_done, 16)
                    pipeline(act, NGE, 2, half)

                @block.vector
                def _(dve):
                    v = nc.vector

                    def score(g, slot, use, u):
                        dve.wait_ge(projected, 4 * g + u + 1)
                        qk = p_qk[u % 2][:, :].rearrange("p (t a c) -> p t a c", t=2, a=2)
                        q, k = qk[:, :, 0], qk[:, :, 1]
                        v.tensor_tensor(q_sb[:], q, bq_row[:].unsqueeze(1).broadcast_to([P, 2, D]), ALU.add).then_inc(q_ready, 1)
                        dve.wait_ge(q_ready, 4 * g + u + 1)
                        v.tensor_tensor(prod[:], q_sb[:], k, ALU.mult).then_inc(scored, 1)
                        dve.wait_ge(scored, 4 * g + u + 1)
                        last = v.tensor_reduce(alpha[:, slot, 2 * u:2 * u + 2].rearrange("p t h -> p (t h)"),
                                               prod[:].rearrange("p t (h c) -> p (t h) c", h=H), AX.X, ALU.add)
                        last.then_inc(alpha_ready if u == 3 else prod_ready, 1)

                    def compare(g, slot, use, u):
                        if u == 0:
                            dve.wait_ge(dst_in[slot], 16 * (use + 1))
                            at_least(dve, summed, 4 * (g - 1))
                            at_least(dve, deg_done, 4 * (g - 1))
                        for k in (2 * u, 2 * u + 1):
                            last = v.tensor_scalar(same[:, slot, k], dst_sb[:, slot, k * P:(k + 1) * P], metag[:, slot, k, META - 1:META], None, ALU.is_equal)
                        last.then_inc(same_ready, 1)
                        for k in (2 * u, 2 * u + 1):
                            v.tensor_scalar(is_lo[:, slot, k], iota16[:, 0:P], lohig[:, slot, k, 0:1], None, ALU.is_equal)
                            last = v.tensor_scalar(is_hi[:, slot, k], iota16[:, 0:HI], lohig[:, slot, k, 1:2], None, ALU.is_equal)
                        last.then_inc(counted, 1)

                    def message(g, slot, use, u):
                        if u == 0:
                            dve.wait_ge(weights_ready, 2 * g + 1)
                        dve.wait_ge(v_copied, 4 * g + u + 1)
                        w = msgs[:, slot, 2 * u:2 * u + 2, D:MSG].unsqueeze(3).broadcast_to([P, 2, H, C])
                        v.tensor_tensor(msgs[:, slot, 2 * u:2 * u + 2, 0:D].rearrange("p t (h c) -> p t h c", h=H),
                                        v_sb[:, slot, 2 * u:2 * u + 2].rearrange("p t (h c) -> p t h c", h=H), w, ALU.mult).then_inc(msg_ready, 1)

                    def scan(g, slot, use):
                        dve.wait_ge(alpha_turned, g + 1)
                        dve.wait_ge(pen_in[slot], 32 * (use + 1))
                        at_least(dve, weighted, g)
                        at_least(dve, back_turned, g)
                        v.tensor_tensor_scan(run_max[:], penf_sb[:, slot], p_alpha, NEG, ALU.add, ALU.max).then_inc(scanned, 1)
                        dve.wait_ge(scanned, 3 * g + 1)
                        v.tensor_tensor_scan(seg_max[:, ::-1], penb_sb[:, slot, ::-1], run_max[:, ::-1], NEG, ALU.add, ALU.max).then_inc(scanned, 1)
                        dve.wait_ge(scanned, 3 * g + 2)
                        v.tensor_tensor(below[:], p_alpha, seg_max[:], ALU.subtract).then_inc(scanned, 1)

                    def half(new, old):
                        if new:
                            g, slot, use = new
                            at_least(dve, ea_turned, g - 1)
                            v.tensor_copy(metag[:, slot], meta[:, bass.ds(g * G, G)]).then_inc(meta_ready, 1)
                            v.tensor_copy(lohig[:, slot], lohi[:, bass.ds(g * G, G)]).then_inc(meta_ready, 1)
                        if old:
                            scan(*old)
                            dve.wait_ge(meta_ready, 2 * old[0] + 2)
                            compare(*old, 0)
                        for u in range(4):
                            if new:
                                score(*new, u)
                            if old:
                                message(*old, u)
                                if u < 3:
                                    compare(*old, u + 1)
                    v.memset(wea1[:], 0.0).then_inc(zeroed, 1)
                    v.memset(wea[:], 0.0).then_inc(zeroed, 1)
                    chain = Chain(dve, e0_step)
                    chain.mark(v.memset(ones3[:], 1.0))
                    for row, n, parts, times in ((b2_row[:], D, b2_parts, 4), (bsk_row[0:3, :], D + 1, bsk_parts, 2)):
                        chain.step(v.tensor_copy(part1[:, 0:n], row))
                        chain.step(v.tensor_tensor(rest[:, 0:n], row, part1[:, 0:n], ALU.subtract))
                        chain.step(v.tensor_copy(part2[:, 0:n], rest[:, 0:n]))
                        chain.step(v.tensor_tensor(rest[:, 0:n], rest[:, 0:n], part2[:, 0:n], ALU.subtract))
                        chain.step(v.tensor_copy(part3[:, 0:n], rest[:, 0:n]))
                        chain.step(v.tensor_scalar(mixed3[:, 0:n], part1[:, 0:n], ident[0:3, 0:1], None, ALU.mult))
                        chain.step(v.scalar_tensor_tensor(mixed3[:, 0:n], part2[:, 0:n], ident[0:3, 1:2], mixed3[:, 0:n], ALU.mult, ALU.add))
                        chain.step(v.scalar_tensor_tensor(mixed3[:, 0:n], part3[:, 0:n], ident[0:3, 2:3], mixed3[:, 0:n], ALU.mult, ALU.add))
                        for j in range(times):
                            chain.mark(v.tensor_copy(parts[:, j * n:(j + 1) * n], mixed3[:, 0:n]))
                        chain.wait()
                    pipeline(dve, NGE, 2, half)
                    dve.wait_ge(deg_done, 4 * NGE)
                    v.tensor_copy(deg[:], p_deg[:, 0:HI]).then_inc(prod_ready, 1)
                    dve.wait_ge(prod_ready, 3 * NGE + 1)

        with phase() as (ctx, t, s):
            pbank = [ctx.enter_context(nc.psum_tensor(f"pm{n}", [P, 512], F32)) for n in range(8)]
            first_r, last_r = t("first_r", [RB, NB, ROW0]), t("last_r", [RB, NB, ROW0])
            before_r, joined = t("before_r", [RB, NB, ROW0]), t("joined", [RB, NB, ROW0])
            cum, tot = t("cum", [P, HI]), t("tot", [P, HI])
            none, row_f, dinv_f = t("none", [P, HI]), t("row_f", [P, HI]), t("dinv_f", [P, HI])
            deg1, root, some = t("deg1", [P, HI]), t("root", [P, HI]), t("some", [P, HI])
            row_i, dinv_r = t("row_i", [P, HB, P], I32), t("dinv_r", [P, HB, P])
            msg_t, den_t, max_t = t("msg_t", [D, TE]), t("den_t", [H, TE]), t("max_t", [H, TE])
            stop4, decay, gain = t("stop4", [H, TE]), t("decay", [H, TE]), t("gain", [H, TE])
            msg_c, den_c, max_c = t("msg_c", [D, TE + 1]), t("den_c", [H, TE + 1]), t("max_c", [H, TE + 1])
            top_m, wf, wb_ = t("top_m", [RB, NB, H]), t("wf", [RB, NB, H]), t("wb_", [RB, NB, H])
            part = t("part", [RB, NB, MSG])
            ends_in, tables_out, tables_in, fixed = s("m_ends_in"), s("m_tables_out"), s("m_tables_in"), s("m_fixed")
            pe_t, act_x, dve_s, powed = s("m_pe"), s("m_act"), s("m_dve"), s("m_powed")
            deg_ready, rows_t, rows_set = s("deg_ready"), s("rows_t"), s("m_rows_set")
            turned, copied, exps_in, expanded, back, joined_s = s("m_turned"), s("m_copied"), s("exps_in"), s("expanded"), s("m_back"), s("m_joined")
            chained, floats = s("chained"), s("m_floats")

            def load_table(eng, table, cols):
                eng.dma_start(cols[:, 0:NGN - 1, :], table[0:(NGN - 1) * GR].rearrange("(g p t) -> p g t", p=P, t=G)).then_inc(tables_in, 16)
                eng.dma_start(cols[:, NGN - 1, :], table[N - GR:N].rearrange("(p t) -> p t", t=G)).then_inc(tables_in, 16)

            def turned_rows(b):
                return pbank[5 if b < 2 else 4][:, b % 2 * 2 * P:(b % 2 + 1) * 2 * P]
            block = nc.Block()
            with block:
                @block.sync
                def _(sp):
                    ends = rows0[0:EP, :].rearrange("(b r e) c -> r b e c", b=NB, r=RB)
                    sp.dma_start(first_r[:], ends[:, :, 0, :]).then_inc(ends_in, 16)
                    sp.dma_start(last_r[:], ends[:, :, P - 1, :]).then_inc(ends_in, 16)
                    sp.wait_ge(rows_set, HB)
                    for b in range(HB):
                        n = min(P, HI - b * P)
                        for table, rows in ((node_row_d, row_i), (dinv_d, dinv_r)):
                            sp.dma_start(table[b * P * P:(b * P + n) * P].rearrange("(h l) -> h l", l=P), rows[0:n, b, :]).then_inc(tables_out, 16)
                    sp.wait_ge(tables_out, 32 * HB)
                    load_table(sp, node_row_d, node_row)
                    sp.wait_ge(tables_in, 64)

                @block.gpsimd
                def _(pool):
                    pool.wait_ge(joined_s, 1)
                    for b in range(NB):
                        pool.indirect_dma_start(out=rows0, out_offset=bass.IndirectOffsetOnAxis(ap=fix_at[:, b:b + 1], axis=0),
                                                in_=joined[:, b, :], in_offset=None, bounds_check=EP - 1, oob_is_err=False).then_inc(fixed, 16)
                    pool.wait_ge(fixed, 16 * NB)

                @block.tensor
                def _(pe):
                    t_ = nc.tensor
                    t_.matmul(pbank[0][:, 0:HI], tri[:], deg[:], start=True, stop=True)
                    t_.matmul(pbank[1][:, 0:HI], ones[:], deg[:], start=True, stop=True).then_inc(pe_t, 1)
                    pe.wait_ge(ends_in, 32)
                    for b in range(NB):
                        cols = slice(b * RB, (b + 1) * RB)
                        t_.transpose(pbank[2][:, cols], last_r[:, b, 0:D], ident[0:RB, 0:RB])
                        t_.transpose(pbank[3][0:H, cols], last_r[:, b, D:MSG], ident[0:RB, 0:RB])
                        last = t_.transpose(pbank[4][0:H, cols], last_r[:, b, MSG:ROW0], ident[0:RB, 0:RB])
                    last.then_inc(turned, 1)
                    pe.wait_ge(exps_in, 2)
                    t_.matmul(pbank[6][:, 0:TE], headmap[:], decay[:], start=True, stop=True)
                    t_.matmul(pbank[7][:, 0:TE], headmap[:], gain[:], start=True, stop=True).then_inc(expanded, 1)
                    pe.wait_ge(floats, 2)
                    for b in range(HB):
                        n = min(P, HI - b * P)
                        t_.transpose(turned_rows(b)[0:n, 0:P], cum[:, b * P:b * P + n], ident[:])
                        last = t_.transpose(turned_rows(b)[0:n, P:2 * P], dinv_f[:, b * P:b * P + n], ident[:])
                    last.then_inc(rows_t, 1)
                    pe.wait_ge(chained, 2)
                    for b in range(NB):
                        cols = slice(b * RB, (b + 1) * RB)
                        at = b % 3 * ROW0
                        o = pbank[b // 3][0:RB, :]
                        t_.transpose(o[:, at:at + D], msg_c[:, cols], ident[:])
                        t_.transpose(o[:, at + D:at + MSG], den_c[:, cols], ident[0:H, 0:H])
                        last = t_.transpose(o[:, at + MSG:at + ROW0], max_c[:, cols], ident[0:H, 0:H])
                    last.then_inc(back, 1)

                @block.scalar
                def _(act):
                    a = nc.scalar
                    act.wait_ge(deg_ready, 1)
                    a.activation(root[:], deg1[:], ACT.Sqrt).then_inc(powed, 1)
                    act.wait_ge(copied, 2)
                    a.activation(decay[:], decay[:], ACT.Exp, scale=SCALE).then_inc(act_x, 1)
                    a.activation(gain[:], gain[:], ACT.Exp, scale=SCALE).then_inc(act_x, 1)
                    act.wait_ge(copied, 4)
                    a.activation(wf[:], wf[:], ACT.Exp, scale=SCALE).then_inc(act_x, 1)
                    a.activation(wb_[:], wb_[:], ACT.Exp, scale=SCALE).then_inc(act_x, 1)
                    act.wait_ge(tables_out, 32 * HB)
                    load_table(act, dinv_d, dinv)

                @block.vector
                def _(dve):
                    v = nc.vector
                    chain = Chain(dve, dve_s)
                    v.tensor_scalar(deg1[:], deg[:], 1.0, None, ALU.max).then_inc(deg_ready, 1)
                    chain.mark(v.tensor_scalar(some[:], deg[:], 0.5, None, ALU.is_gt))
                    chain.mark(v.tensor_scalar(none[:], deg[:], 0.5, float(EP), ALU.is_lt, ALU.mult))
                    dve.wait_ge(turned, 1)
                    chain.mark(v.tensor_copy(msg_t[:], pbank[2][:, 0:TE]))
                    chain.mark(v.tensor_copy(den_t[:], pbank[3][0:H, 0:TE]))
                    chain.mark(v.tensor_copy(max_t[:], pbank[4][0:H, 0:TE]))
                    chain.mark(v.memset(msg_c[:, 0:1], 0.0))
                    chain.mark(v.memset(den_c[:, 0:1], 0.0))
                    chain.mark(v.memset(max_c[:, 0:1], 0.0))
                    chain.step(v.tensor_scalar(stop4[:], through[0:H, :], -1.0, -NEG, ALU.add, ALU.mult))
                    chain.step(v.tensor_tensor_scan(max_c[:, 1:TE + 1], stop4[:], max_t[:], NEG, ALU.add, ALU.max))
                    chain.mark(v.tensor_tensor(gain[:], max_t[:], max_c[:, 1:TE + 1], ALU.subtract))
                    chain.step(v.tensor_tensor(decay[:], max_c[:, 0:TE], max_c[:, 1:TE + 1], ALU.subtract))
                    v.tensor_scalar(decay[:], decay[:], 0.0, None, ALU.min).then_inc(copied, 1)
                    v.tensor_scalar(gain[:], gain[:], 0.0, None, ALU.min).then_inc(copied, 1)
                    dve.wait_ge(pe_t, 1)
                    chain.step(v.memset(dinv_f[:], 0.0))
                    chain.step(v.tensor_tensor_scan(tot[:], dinv_f[:], pbank[1][:, 0:HI], 0.0, ALU.add, ALU.add))
                    chain.step(v.tensor_tensor(tot[:], tot[:], pbank[1][:, 0:HI], ALU.subtract))
                    chain.step(v.tensor_tensor(cum[:], tot[:], pbank[0][:, 0:HI], ALU.add))
                    chain.step(v.scalar_tensor_tensor(cum[:], cum[:], -1.0, some[:], ALU.add, ALU.mult))
                    v.tensor_tensor(cum[:], cum[:], none[:], ALU.add).then_inc(floats, 1)
                    dve.wait_ge(powed, 1)
                    chain.step(v.reciprocal(row_f[:], root[:]))
                    chain.step(v.tensor_tensor(root[:], row_f[:], row_f[:], ALU.mult))
                    chain.step(v.scalar_tensor_tensor(root[:], root[:], -0.5, deg1[:], ALU.mult, ALU.mult))
                    chain.step(v.scalar_tensor_tensor(root[:], root[:], 1.5, row_f[:], ALU.add, ALU.mult))
                    v.tensor_tensor(dinv_f[:], root[:], some[:], ALU.mult).then_inc(floats, 1)
                    dve.wait_ge(act_x, 2)
                    chain.mark(v.tensor_tensor(den_t[:], den_t[:], gain[:], ALU.mult))
                    v.tensor_tensor(decay[:], decay[:], through[0:H, :], ALU.mult).then_inc(exps_in, 2)
                    dve.wait_ge(exps_in, 2)
                    chain.wait()
                    v.tensor_tensor_scan(den_c[:, 1:TE + 1], decay[:], den_t[:], 0.0, ALU.mult, ALU.add).then_inc(chained, 1)
                    dve.wait_ge(expanded, 1)
                    chain.step(v.tensor_tensor(msg_t[:], msg_t[:], pbank[7][:, 0:TE], ALU.mult))
                    v.tensor_tensor_scan(msg_c[:, 1:TE + 1], pbank[6][:, 0:TE], msg_t[:], 0.0, ALU.mult, ALU.add).then_inc(chained, 1)
                    dve.wait_ge(rows_t, 1)
                    for b in range(HB):
                        n = min(P, HI - b * P)
                        v.tensor_copy(row_i[0:n, b, :], turned_rows(b)[0:n, 0:P])
                        v.tensor_copy(dinv_r[0:n, b, :], turned_rows(b)[0:n, P:2 * P]).then_inc(rows_set, 1)
                    dve.wait_ge(back, 1)
                    for b in range(NB):
                        at = b % 3 * ROW0
                        chain.mark(v.tensor_copy(before_r[:, b, :], pbank[b // 3][0:RB, at:at + ROW0]))
                    chain.wait()
                    chain.step(v.tensor_tensor(top_m[:], first_r[:, :, MSG:ROW0], before_r[:, :, MSG:ROW0], ALU.max))
                    chain.mark(v.tensor_copy(joined[:, :, MSG:ROW0], top_m[:]))
                    v.tensor_tensor(wf[:], first_r[:, :, MSG:ROW0], top_m[:], ALU.subtract).then_inc(copied, 1)
                    v.tensor_tensor(wb_[:], before_r[:, :, MSG:ROW0], top_m[:], ALU.subtract).then_inc(copied, 1)
                    dve.wait_ge(act_x, 4)
                    for o, rows, w in ((joined, first_r, wf), (part, before_r, wb_)):
                        chain.mark(v.tensor_tensor(o[:, :, D:MSG], rows[:, :, D:MSG], w[:], ALU.mult))
                        for b in range(NB):
                            chain.mark(v.tensor_tensor(o[:, b, 0:D].rearrange("r (h c) -> r h c", h=H), rows[:, b, 0:D].rearrange("r (h c) -> r h c", h=H),
                                                       w[:, b, :].unsqueeze(2).broadcast_to([RB, H, C]), ALU.mult))
                    chain.wait()
                    v.tensor_tensor(joined[:, :, 0:MSG], joined[:, :, 0:MSG], part[:], ALU.add).then_inc(joined_s, 1)

        with phase() as (ctx, t, s):
            ps = lambda name: ctx.enter_context(nc.psum_tensor(name, [P, 512], F32))
            WAYS = 4
            x_sb = t("xb", [P, WAYS, G, D])
            agg = t("agg", [P, 2, G, ROW0])
            at_n = t("at_n", [P, 2, G], I32)
            norm = t("normb", [P, 2, 4, G])
            h_sb, z_sb = t("hb", [P, 2, G, D]), t("zb", [P, G, D])
            z_t = t("ztb", [P, 2, 4, P])
            den, recip, wa_sum = t("den", [P, G, H]), t("recip", [P, G, H]), t("wa_sum", [P, 2, G])
            attn, hat, wa_prod = t("attn", [P, 2, G, D]), t("hat", [P, 2, G, D]), t("wa_prod", [P, G, D])
            diff = t("diff", [P, G, D])
            logit, gate_e, gate_1, gate = t("logit", [P, G]), t("gate_e", [P, G]), t("gate_1", [P, G]), t("gate", [P, G])
            x_l = t("x_l", [P, 2, G, D])
            six2, mv2, var2 = t("six2", [P, G, 6]), t("mv2", [P, G, 2]), t("var2", [P, G])
            six3, mv3, var3 = t("six3", [P, G, 6]), t("mv3", [P, G, 2]), t("var3", [P, G])
            norm2 = t("norm2", [P, 2, 2, G])
            norm3 = t("norm3", [P, 2, 5, G])
            z2, z2_t = t("z2", [P, G, D]), t("z2_t", [P, 2, 4, P])
            act1 = t("act1", [P, 2, 4, 4 * P])
            x_xl = t("x_xl", [P, 2, G, D])
            x1_sb, h2_sb = t("x1b", [P, 2, G, D]), t("h2b", [P, 2, G, ROW1])
            p_zt, p_z2t = ps("p_zt"), ps("p_z2t")
            p_skip = [ps("p_skip0"), ps("p_skip1")]
            p_f1 = [ps("p_f10"), ps("p_f11")]
            p_f2 = [ps("p_f20"), ps("p_f21")]
            S = {n: s("b_" + n) for n in (
                "at_ready tab_ready h_ready z_ready zt_turned zt_copied skipped skip_ready recips attn_ready "
                "wa_ready gate_exp hat_ready xxl_ready xl_ready bn2 var2 rstd2 norm2_ready "
                "gates norm3s z2_ready z2_turned z2_copied f1_done f1_copied f2_done y_ready bn3 var3 rstd3 norm3_ready h2_ready").split()}
            x_in = [s(f"b_x_in{a}") for a in range(WAYS)]
            agg_in, x1_out, h2_out = ([s(f"b_{n}{a}") for a in range(2)] for n in ("agg_in", "x1_out", "h2_out"))

            def flow(eng, half):
                def split(*groups):
                    half(*[(v[0], v[1] % 2, 2 * v[2] + v[1] // 2, v[1], v[2]) if v else None for v in groups])
                pipeline(eng, NGN, 6, split, WAYS)
            block = nc.Block()

            with block:
                @block.sync
                def _(sp):
                    def half(load, prep, gating, mlp, ending, last):
                        if load:
                            g, slot, use, x_slot, x_use = load
                            at_least(sp, S["xxl_ready"], g - WAYS + 1)
                            hold(sp, held)
                            rows = x[bass.ds(first_row(g), GR), :].rearrange("(p t) d -> p t d", t=G)
                            sp.dma_start(x_sb[:, x_slot], rows).then_inc(x_in[x_slot], 16)
                        if ending:
                            g, slot, use, *_ = ending
                            if isinstance(g, int) and g == NGN - 1:
                                sp.wait_ge(x1_out[1 - slot], 16 * ((g - 1) // 2 + 1))
                            sp.wait_ge(S["y_ready"], 2 * g + 2)
                            hold(sp, held)
                            rows = bass.ds(first_row(g), GR)
                            sp.dma_start(x1_table[rows, :].rearrange("(p t) d -> p t d", t=G), x1_sb[:, slot]).then_inc(x1_out[slot], 16)
                        if last:
                            g, slot, use, *_ = last
                            if isinstance(g, int) and g == NGN - 1:
                                sp.wait_ge(h2_out[1 - slot], 16 * ((g - 1) // 2 + 1))
                            sp.wait_ge(S["h2_ready"], g + 1)
                            hold(sp, held)
                            sp.dma_start(h2_table[bass.ds(first_row(g), GR), :].rearrange("(p t) d -> p t d", t=G), h2_sb[:, slot]).then_inc(h2_out[slot], 16)
                    flow(sp, half)
                    for n in range(2):
                        sp.wait_ge(x1_out[n], 16 * ((NGN - n + 1) // 2))
                        sp.wait_ge(h2_out[n], 16 * ((NGN - n + 1) // 2))

                @block.gpsimd
                def _(pool):
                    def gather(g, slot, tiles):
                        for k in tiles:
                            pool.indirect_dma_start(out=agg[:, slot, k], out_offset=None, in_=rows0,
                                                    in_offset=bass.IndirectOffsetOnAxis(ap=at_n[:, slot, k:k + 1], axis=0)).then_inc(agg_in[slot], 16)

                    def half(load, prep, gating, mlp, ending, last):
                        if load:
                            g, slot, use, x_slot, x_use = load
                            at_least(pool, agg_in[slot], 16 * G * use)
                            nc.gpsimd.tensor_copy(at_n[:, slot], node_row[:, bass.ds(g, 1), :].rearrange("p a t -> p (a t)")).then_inc(S["at_ready"], 1)
                            at_least(pool, S["attn_ready"], g - 1)
                            pool.wait_ge(S["at_ready"], g + 1)
                            hold(pool, held)
                            gather(g, slot, range(G))
                        if mlp:
                            g, slot, use, x_slot, x_use = mlp
                            pool.wait_ge(S["xl_ready"], g + 1)
                            at_least(pool, S["y_ready"], 2 * (g - 1))
                            nc.gpsimd.tensor_tensor(x_xl[:, slot], x_sb[:, x_slot], x_l[:, slot], ALU.add).then_inc(S["xxl_ready"], 1)
                        if prep:
                            g, slot, use, *_ = prep
                            pool.wait_ge(S["attn_ready"], g + 1)
                            pool.wait_ge(S["h_ready"], 2 * g + 2)
                            at_least(pool, S["xl_ready"], g - 1)
                            nc.gpsimd.tensor_tensor(hat[:, slot], attn[:, slot], h_sb[:, slot], ALU.add).then_inc(S["hat_ready"], 1)
                        if gating:
                            g, slot, use, *_ = gating
                            pool.wait_ge(S["var2"], g + 1)
                            at_least(pool, S["z2_ready"], 2 * (g - 1))
                            nc.gpsimd.tensor_tensor(norm2[:, slot, 0], var2[:], half_neg[:, 0:G], ALU.pow).then_inc(S["rstd2"], 1)
                        if ending:
                            g, slot, use, *_ = ending
                            pool.wait_ge(S["var3"], g + 1)
                            at_least(pool, S["h2_ready"], g - 1)
                            nc.gpsimd.tensor_tensor(norm3[:, slot, 0], var3[:], half_neg[:, 0:G], ALU.pow).then_inc(S["rstd3"], 1)
                    flow(pool, half)

                @block.tensor
                def _(pe):
                    t_ = nc.tensor

                    def turn_z2(g, slot, q):
                        pe.wait_ge(S["z2_ready"], 2 * g + q + 1)
                        at_least(pe, S["z2_copied"], 2 * g + q)
                        for k in range(4):
                            last = t_.transpose(p_z2t[:, k * P:(k + 1) * P], z2[:, 4 * q + k], ident[:])
                        last.then_inc(S["z2_turned"], 1)

                    def turn_z(g, slot, q):
                        pe.wait_ge(S["z_ready"], 2 * g + q + 1)
                        at_least(pe, S["zt_copied"], 2 * g + q)
                        for k in range(4):
                            last = t_.transpose(p_zt[:, k * P:(k + 1) * P], z_sb[:, 4 * q + k], ident[:])
                        last.then_inc(S["zt_turned"], 1)

                    def skips(g, u):
                        pe.wait_ge(S["zt_copied"], 2 * g + u // 2 + 1)
                        at_least(pe, S["skip_ready"], 4 * g + u - 1)
                        hold(pe, held)
                        t_.matmul(p_skip[u % 2][:, 0:2 * (D + 1)], ones3[:], bsk_parts[:], start=True, stop=False)
                        for k in range(2):
                            last = t_.matmul(p_skip[u % 2][:, k * (D + 1):(k + 1) * (D + 1)], z_t[:, u // 2, 2 * (u % 2) + k], wsk_t[:], start=False, stop=(k == 1))
                        last.then_inc(S["skipped"], 1)

                    def up(g, q, chunks):
                        pe.wait_ge(S["z2_copied"], 2 * g + q + 1)
                        for c in chunks:
                            at_least(pe, S["f1_copied"], 8 * g + 4 * q + c - 1)
                            t_.matmul(p_f1[c % 2][:, :], w1_t[:, c * P:(c + 1) * P], z2_t[:, q].rearrange("p a b -> p (a b)"),
                                      start=True, stop=True).then_inc(S["f1_done"], 1)

                    def down(g, q):
                        at_least(pe, S["y_ready"], 2 * (g - 1) + q + 1)
                        pe.wait_ge(S["f1_copied"], 8 * g + 4 * q + 4)
                        hold(pe, held)
                        t_.matmul(p_f2[q][:, :], ones3[:], b2_parts[:], start=True, stop=False)
                        for k in range(4):
                            for c in range(4):
                                last = t_.matmul(p_f2[q][:, k * D:(k + 1) * D], act1[:, q, c, k * P:(k + 1) * P], w2_t[:, c], start=False, stop=(k == 3 and c == 3))
                        last.then_inc(S["f2_done"], 1)

                    def half(load, prep, gating, mlp, ending, last):
                        if gating:
                            skips(gating[0], 0)
                            skips(gating[0], 1)
                        if mlp:
                            turn_z2(mlp[0], mlp[1], 0)
                        if gating:
                            skips(gating[0], 2)
                            skips(gating[0], 3)
                        if mlp:
                            up(mlp[0], 0, (0, 1))
                            turn_z2(mlp[0], mlp[1], 1)
                            up(mlp[0], 0, (2, 3))
                            up(mlp[0], 1, range(4))
                            down(mlp[0], 0)
                        if prep:
                            turn_z(prep[0], prep[1], 0)
                        if mlp:
                            down(mlp[0], 1)
                        if prep:
                            turn_z(prep[0], prep[1], 1)
                    flow(pe, half)

                @block.scalar
                def _(act):
                    a = nc.scalar

                    def h_of(g, slot, use, x_slot, x_use, q):
                        if q == 0:
                            act.wait_ge(x_in[x_slot], 16 * (x_use + 1))
                            act.wait_ge(S["tab_ready"], g + 1)
                            at_least(act, S["hat_ready"], g - 1)
                            at_least(act, S["z_ready"], 2 * (g - 1))
                        for k in range(4 * q, 4 * q + 4):
                            last = a.activation(h_sb[:, slot, k], x_sb[:, x_slot, k], ACT.Relu, bias=norm[:, slot, 1, k:k + 1], scale=norm[:, slot, 0, k:k + 1])
                        last.then_inc(S["h_ready"], 1)

                    def z2_of(g, slot, q):
                        act.wait_ge(S["norm2_ready"], g + 1)
                        at_least(act, S["z2_turned"], 2 * (g - 1) + q + 1)
                        for k in range(4 * q, 4 * q + 4):
                            last = a.activation(z2[:, k], x_l[:, slot, k], ACT.Identity, bias=norm2[:, slot, 1, k:k + 1], scale=norm2[:, slot, 0, k:k + 1])
                        last.then_inc(S["z2_ready"], 1)

                    def copy_z2(g, q):
                        act.wait_ge(S["z2_turned"], 2 * g + q + 1)
                        at_least(act, S["f1_done"], 8 * (g - 1) + 4 * q + 4)
                        a.activation(z2_t[:, q].rearrange("p a b -> p (a b)"), p_z2t[:, :], ACT.Copy).then_inc(S["z2_copied"], 1)

                    def copy_z(g, q):
                        act.wait_ge(S["zt_turned"], 2 * g + q + 1)
                        at_least(act, S["skipped"], 4 * (g - 1) + 2 * q + 2)
                        a.activation(z_t[:, q].rearrange("p a b -> p (a b)"), p_zt[:, :], ACT.Copy).then_inc(S["zt_copied"], 1)

                    def relus(g, q, chunks):
                        at_least(act, S["f2_done"], 2 * (g - 1) + q + 1)
                        for c in chunks:
                            act.wait_ge(S["f1_done"], 8 * g + 4 * q + c + 1)
                            a.activation(act1[:, q, c], p_f1[c % 2][:, :], ACT.Relu, bias=b1_col[:, c:c + 1]).then_inc(S["f1_copied"], 1)

                    def half(load, prep, gating, mlp, ending, last):
                        if mlp:
                            copy_z2(mlp[0], 0)
                            z2_of(mlp[0], mlp[1], 1)
                        if gating:
                            act.wait_ge(S["skip_ready"], 4 * gating[0] + 4)
                            a.activation(gate_e[:], logit[:], ACT.Exp, scale=-1.0).then_inc(S["gate_exp"], 1)
                        if mlp:
                            relus(mlp[0], 0, (0, 1))
                            copy_z2(mlp[0], 1)
                            relus(mlp[0], 0, (2, 3))
                        if mlp:
                            relus(mlp[0], 1, range(4))
                        if last:
                            g, slot, use, *_ = last
                            act.wait_ge(S["norm3_ready"], g + 1)
                            at_least(act, h2_out[slot], 16 * use)
                            for k in range(G):
                                a.activation(h2_sb[:, slot, k, 0:D], x1_sb[:, slot, k], ACT.Relu, bias=norm3[:, slot, 3, k:k + 1], scale=norm3[:, slot, 2, k:k + 1])
                            a.activation(h2_sb[:, slot, :, D], norm3[:, slot, 4], ACT.Copy).then_inc(S["h2_ready"], 1)
                        if prep:
                            copy_z(prep[0], 0)
                        if gating:
                            z2_of(gating[0], gating[1], 0)
                        if load:
                            h_of(*load, 0)
                            h_of(*load, 1)
                        if prep:
                            copy_z(prep[0], 1)
                    flow(act, half)

                @block.vector
                def _(dve):
                    v = nc.vector

                    def half(load, prep, gating, mlp, ending, last):
                        if load:
                            g, slot, use, x_slot, x_use = load
                            v.tensor_copy(norm[:, slot], stats[:, bass.ds(g, 1)].rearrange("p a b c -> p (a b) c")).then_inc(S["tab_ready"], 1)
                        if ending:
                            g, slot, use, *_ = ending
                            dve.wait_ge(S["xxl_ready"], g + 1)
                            at_least(dve, x1_out[slot], 16 * use)
                            at_least(dve, S["h2_ready"], g - 1)
                            for q in range(2):
                                dve.wait_ge(S["f2_done"], 2 * g + q + 1)
                                v.tensor_tensor(x1_sb[:, slot, 4 * q:4 * q + 4].rearrange("p a b -> p (a b)"), p_f2[q][:, :],
                                                x_xl[:, slot, 4 * q:4 * q + 4].rearrange("p a b -> p (a b)"), ALU.add).then_inc(S["y_ready"], 1)
                        if gating:
                            g, slot, use, *_ = gating
                            dve.wait_ge(S["wa_ready"], 2 * g + 2)
                            for u in range(4):
                                dve.wait_ge(S["skipped"], 4 * g + u + 1)
                                both = p_skip[u % 2][:, 0:2 * (D + 1)].rearrange("p (t c) -> p t c", t=2)
                                v.tensor_tensor(diff[:, 2 * u:2 * u + 2], both[:, :, 0:D], attn[:, slot, 2 * u:2 * u + 2], ALU.subtract)
                                v.tensor_tensor(logit[:, 2 * u:2 * u + 2], both[:, :, D], wa_sum[:, slot, 2 * u:2 * u + 2], ALU.add).then_inc(S["skip_ready"], 1)
                        if prep:
                            g, slot, use, *_ = prep
                            dve.wait_ge(agg_in[slot], 16 * G * (use + 1))
                            v.tensor_scalar(den[:], agg[:, slot, :, D:MSG], 1e-16, None, ALU.add).then_inc(S["recips"], 1)
                            dve.wait_ge(S["recips"], 2 * g + 1)
                            v.reciprocal(recip[:], den[:]).then_inc(S["recips"], 1)
                            dve.wait_ge(S["recips"], 2 * g + 2)
                            v.tensor_tensor(attn[:, slot].rearrange("p t (h c) -> p t h c", h=H), agg[:, slot, :, 0:D].rearrange("p t (h c) -> p t h c", h=H),
                                            recip[:].unsqueeze(3).broadcast_to([P, G, H, C]), ALU.mult).then_inc(S["attn_ready"], 1)
                        if gating:
                            g, slot, use, *_ = gating
                            dve.wait_ge(S["gate_exp"], g + 1)
                            v.tensor_scalar(gate_1[:], gate_e[:], 1.0, None, ALU.add).then_inc(S["gates"], 1)
                            dve.wait_ge(S["gates"], 2 * g + 1)
                            v.reciprocal(gate[:], gate_1[:]).then_inc(S["gates"], 1)
                            dve.wait_ge(S["gates"], 2 * g + 2)
                            dve.wait_ge(S["skip_ready"], 4 * g + 4)
                            dve.wait_ge(S["hat_ready"], g + 1)
                            for k in range(G):
                                last = v.scalar_tensor_tensor(x_l[:, slot, k], diff[:, k], gate[:, k:k + 1], hat[:, slot, k], ALU.mult, ALU.add)
                            last.then_inc(S["xl_ready"], 1)
                            dve.wait_ge(S["xl_ready"], g + 1)
                            for k in range(G):
                                last = v.bn_stats(six2[:, k], x_l[:, slot, k])
                            last.then_inc(S["bn2"], 1)
                            dve.wait_ge(S["bn2"], 2 * g + 1)
                            hold(dve, held)
                            for k in range(G):
                                last = v.bn_aggr(mv2[:, k], six2[:, k])
                            last.then_inc(S["bn2"], 1)
                            dve.wait_ge(S["bn2"], 2 * g + 2)
                            at_least(dve, S["rstd2"], g)
                            v.tensor_scalar(var2[:], mv2[:, :, 1], EPS, None, ALU.add).then_inc(S["var2"], 1)
                        if ending:
                            g, slot, use, *_ = ending
                            dve.wait_ge(S["y_ready"], 2 * g + 2)
                            for k in range(G):
                                last = v.bn_stats(six3[:, k], x1_sb[:, slot, k])
                            last.then_inc(S["bn3"], 1)
                            dve.wait_ge(S["bn3"], 2 * g + 1)
                            hold(dve, held)
                            for k in range(G):
                                last = v.bn_aggr(mv3[:, k], six3[:, k])
                            last.then_inc(S["bn3"], 1)
                            dve.wait_ge(S["bn3"], 2 * g + 2)
                            at_least(dve, S["rstd3"], g)
                            v.tensor_scalar(var3[:], mv3[:, :, 1], EPS, None, ALU.add).then_inc(S["var3"], 1)
                        if gating:
                            g, slot, use, *_ = gating
                            dve.wait_ge(S["rstd2"], g + 1)
                            v.scalar_tensor_tensor(norm2[:, slot, 1], mv2[:, :, 0], -1.0, norm2[:, slot, 0], ALU.mult, ALU.mult).then_inc(S["norm2_ready"], 1)
                        if prep:
                            g, slot, use, *_ = prep
                            dve.wait_ge(S["tab_ready"], g + 1)
                            for q in range(2):
                                dve.wait_ge(S["h_ready"], 2 * g + q + 1)
                                at_least(dve, S["zt_turned"], 2 * (g - 1) + q + 1)
                                for k in range(4 * q, 4 * q + 4):
                                    last = v.tensor_scalar(z_sb[:, k], h_sb[:, slot, k], norm[:, slot, 2, k:k + 1], norm[:, slot, 3, k:k + 1], ALU.mult, ALU.add)
                                last.then_inc(S["z_ready"], 1)
                            dve.wait_ge(S["attn_ready"], g + 1)
                            v.tensor_tensor(wa_prod[:], attn[:, slot], wa_row[:].unsqueeze(1).broadcast_to([P, G, D]), ALU.mult).then_inc(S["wa_ready"], 1)
                            dve.wait_ge(S["wa_ready"], 2 * g + 1)
                            v.tensor_reduce(wa_sum[:, slot], wa_prod[:], AX.X, ALU.add).then_inc(S["wa_ready"], 1)
                        if ending:
                            g, slot, use, *_ = ending
                            dve.wait_ge(S["rstd3"], g + 1)
                            at_least(dve, S["h2_ready"], g - 1)
                            v.scalar_tensor_tensor(norm3[:, slot, 1], mv3[:, :, 0], -1.0, norm3[:, slot, 0], ALU.mult, ALU.mult).then_inc(S["norm3s"], 1)
                            v.tensor_copy(norm3[:, slot, 4], dinv[:, bass.ds(g, 1)].rearrange("p a t -> p (a t)")).then_inc(S["norm3s"], 1)
                            dve.wait_ge(S["norm3s"], 2 * g + 2)
                            v.tensor_copy(stats2[:, bass.ds(g, 1)].rearrange("p a b c -> p (a b) c"), norm3[:, slot, 0:2])
                            v.tensor_tensor(norm3[:, slot, 2:4], norm3[:, slot, 0:2], norm3[:, slot, 4].unsqueeze(1).broadcast_to([P, 2, G]), ALU.mult).then_inc(S["norm3_ready"], 1)
                    flow(dve, half)

        with phase() as (ctx, t, s):
            h2s = t("h2s", [P, 2, G, ROW1])
            at_s = t("at_s1", [P, 2, G], I32)
            dst_sb, dst_g = t("dst_sb1", [P, 2, GR], U16), t("dst_g", [P, 2, G])
            same = t("same1", [P, 2, G, P])
            rows_sb = t("rows_sb1", [P, 2, G, ROW1])
            p_sum = [ctx.enter_context(nc.psum_tensor(f"p_sum1{n}", [P, 512], F32)) for n in range(4)]
            gathered = [[s(f"e1_gathered{a}{b}") for b in range(4)] for a in range(2)]
            dst_in, stored = ([s(f"e1_{n}{a}") for a in range(2)] for n in ("dst_in", "stored"))
            at_ready, dst_ready, same_ready, summed, sums_copied = (s("e1_" + n) for n in ("at_ready", "dst_ready", "same_ready", "summed", "sums_copied"))
            block = nc.Block()
            with block:
                @block.gpsimd
                def _(pool):
                    def gather(new):
                        g, slot, use = new
                        for u in range(4):
                            at_least(pool, gathered[slot][u], 32 * use)
                        nc.gpsimd.tensor_copy(at_s[:, slot], src_col[:, bass.ds(g * G, G)]).then_inc(at_ready, 1)
                        for u in range(4):
                            at_least(pool, summed, 4 * g + u - 7)
                            pool.wait_ge(at_ready, g + 1)
                            hold(pool, held)
                            for k in (2 * u, 2 * u + 1):
                                pool.indirect_dma_start(out=h2s[:, slot, k], out_offset=None, in_=h2_table,
                                                        in_offset=bass.IndirectOffsetOnAxis(ap=at_s[:, slot, k:k + 1], axis=0)
                                                        ).then_inc(gathered[slot][u], 16)
                    pipeline(pool, NGE, 1, gather)

                @block.sync
                def _(sp):
                    def half(new, old):
                        if new:
                            g, slot, use = new
                            at_least(sp, same_ready, 4 * (g - 1))
                            hold(sp, held)
                            sp.dma_start(dst_sb[:, slot], dst16[bass.ds(g * GR, GR)].unsqueeze(0).broadcast_to([P, GR])).then_inc(dst_in[slot], 16)
                        if old:
                            g, slot, use = old
                            sp.wait_ge(sums_copied, 4 * g + 4)
                            hold(sp, held)
                            sp.dma_start(rows1[bass.ds(g * GR, GR), :].rearrange("(t p) c -> p t c", p=P), rows_sb[:, slot]).then_inc(stored[slot], 16)
                    pipeline(sp, NGE, 2, half)
                    for n in range(2):
                        sp.wait_ge(stored[n], 16 * ((NGE - n + 1) // 2))

                @block.vector
                def _(dve):
                    def half(new):
                        g, slot, use = new
                        nc.vector.tensor_copy(dst_g[:, slot], meta[:, bass.ds(g * G, G), META - 1]).then_inc(dst_ready, 1)
                        dve.wait_ge(dst_ready, g + 1)
                        dve.wait_ge(dst_in[slot], 16 * (use + 1))
                        for u in range(4):
                            at_least(dve, summed, 4 * g + u - 7)
                            for k in (2 * u, 2 * u + 1):
                                last = nc.vector.tensor_scalar(same[:, slot, k], dst_sb[:, slot, k * P:(k + 1) * P], dst_g[:, slot, k:k + 1], None, ALU.is_equal)
                            last.then_inc(same_ready, 1)
                    pipeline(dve, NGE, 1, half)

                @block.tensor
                def _(pe):
                    def half(new):
                        g, slot, use = new
                        for u in range(4):
                            pe.wait_ge(same_ready, 4 * g + u + 1)
                            pe.wait_ge(gathered[slot][u], 32 * (use + 1))
                            at_least(pe, sums_copied, 4 * g + u - 3)
                            for j in range(2):
                                last = nc.tensor.matmul(p_sum[u][:, j * ROW1:(j + 1) * ROW1], same[:, slot, 2 * u + j], h2s[:, slot, 2 * u + j], start=True, stop=True)
                            last.then_inc(summed, 1)
                    pipeline(pe, NGE, 1, half)

                @block.scalar
                def _(act):
                    def half(new):
                        g, slot, use = new
                        at_least(act, stored[slot], 16 * use)
                        for u in range(4):
                            act.wait_ge(summed, 4 * g + u + 1)
                            nc.scalar.activation(rows_sb[:, slot, 2 * u:2 * u + 2], p_sum[u][:, 0:2 * ROW1].rearrange("p (t c) -> p t c", t=2), ACT.Copy).then_inc(sums_copied, 1)
                    pipeline(act, NGE, 1, half)

        with phase() as (ctx, t, s):
            pbank = [ctx.enter_context(nc.psum_tensor(f"pn{n}", [P, 512], F32)) for n in range(4)]
            first_r, last_r, joined = t("first1", [RB, NB, ROW1]), t("last1", [RB, NB, ROW1]), t("joined1", [RB, NB, ROW1])
            sum_t, one_t = t("sum_t", [D, TE]), t("one_t", [1, TE])
            sum_c, one_c = t("sum_c", [D, TE + 1]), t("one_c", [1, TE + 1])
            ends_in, turned, copied, chained, back, joined_s, fixed = (s("n_" + n) for n in ("ends_in", "turned", "copied", "chained", "back", "joined", "fixed"))
            block = nc.Block()
            with block:
                @block.sync
                def _(sp):
                    ends = rows1[0:EP, :].rearrange("(b r e) c -> r b e c", b=NB, r=RB)
                    sp.dma_start(first_r[:], ends[:, :, 0, :]).then_inc(ends_in, 16)
                    sp.dma_start(last_r[:], ends[:, :, P - 1, :]).then_inc(ends_in, 16)

                @block.tensor
                def _(pe):
                    t_ = nc.tensor
                    pe.wait_ge(ends_in, 32)
                    for b in range(NB):
                        cols = slice(b * RB, (b + 1) * RB)
                        t_.transpose(pbank[0][:, cols], last_r[:, b, 0:D], ident[0:RB, 0:RB])
                        last = t_.transpose(pbank[1][0:1, cols], last_r[:, b, D:ROW1], ident[0:RB, 0:RB])
                    last.then_inc(turned, 1)
                    pe.wait_ge(chained, 2)
                    for b in range(NB):
                        cols, at = slice(b * RB, (b + 1) * RB), b % 3 * ROW1
                        t_.transpose(pbank[2 + b // 3][0:RB, at:at + D], sum_c[:, cols], ident[:])
                        last = t_.transpose(pbank[2 + b // 3][0:RB, at + D:at + ROW1], one_c[:, cols], ident[0:1, 0:1])
                    last.then_inc(back, 1)

                @block.vector
                def _(dve):
                    v = nc.vector
                    dve.wait_ge(turned, 1)
                    v.memset(sum_c[:, 0:1], 0.0)
                    v.memset(one_c[:, 0:1], 0.0)
                    v.tensor_copy(sum_t[:], pbank[0][:, 0:TE])
                    v.tensor_copy(one_t[:], pbank[1][0:1, 0:TE]).then_inc(copied, 1)
                    dve.wait_ge(copied, 1)
                    v.tensor_tensor_scan(sum_c[:, 1:TE + 1], through[:], sum_t[:], 0.0, ALU.mult, ALU.add).then_inc(chained, 1)
                    v.tensor_tensor_scan(one_c[:, 1:TE + 1], through[0:1, :], one_t[:], 0.0, ALU.mult, ALU.add).then_inc(chained, 1)
                    dve.wait_ge(back, 1)
                    for b in range(NB):
                        at = b % 3 * ROW1
                        last = v.tensor_tensor(joined[:, b, :], pbank[2 + b // 3][0:RB, at:at + ROW1], first_r[:, b, :], ALU.add)
                    last.then_inc(joined_s, 1)

                @block.gpsimd
                def _(pool):
                    pool.wait_ge(joined_s, 1)
                    for b in range(NB):
                        pool.indirect_dma_start(out=rows1, out_offset=bass.IndirectOffsetOnAxis(ap=fix_at[:, b:b + 1], axis=0),
                                                in_=joined[:, b, :], in_offset=None, bounds_check=EP - 1, oob_is_err=False).then_inc(fixed, 16)
                    pool.wait_ge(fixed, 16 * NB)

        with phase() as (ctx, t, s):
            WAYS = 4
            x1_sb, agg = t("x1c", [P, WAYS, G, D]), t("aggc", [P, WAYS, G, ROW1])
            at_n = t("at_nc", [P, WAYS, G], I32)
            norm, dinv_g = t("normc", [P, WAYS, 2, G]), t("dinv_g", [P, WAYS, G])
            h2 = t("h2c", [P, 2, G, D])
            mixed, base = t("mixed", [P, G, D]), t("basec", [P, 2, G, D])
            m_t = t("m_t", [P, 2, 4, P])
            total, leaky = t("total", [P, G, D]), t("leaky", [P, G, D])
            out_sb = t("out_sb", [P, 2, G, D])
            p_mt = [ctx.enter_context(nc.psum_tensor(f"p_mt{n}", [P, 512], F32)) for n in range(2)]
            p_w = [ctx.enter_context(nc.psum_tensor(f"p_w{n}", [P, 512], F32)) for n in range(2)]
            S = {n: s("c_" + n) for n in (
                "at_ready tab_ready h2_ready mixed_ready hb_ready base_ready turned copied multiplied total_ready leaky_ready out_ready").split()}
            x1_in, agg_in = ([s(f"c_{n}{a}") for a in range(WAYS)] for n in ("x1_in", "agg_in"))
            out_out = [s(f"c_out_out{a}") for a in range(2)]
            block = nc.Block()
            with block:
                @block.sync
                def _(sp):
                    def half(new, old):
                        if new:
                            g, slot, use = new
                            at_least(sp, S["out_ready"], g - WAYS + 1)
                            hold(sp, held)
                            sp.dma_start(x1_sb[:, slot], x1_table[bass.ds(first_row(g), GR), :].rearrange("(p t) d -> p t d", t=G)).then_inc(x1_in[slot], 16)
                        if old:
                            g, slot, use = old
                            if isinstance(g, int) and g == NGN - 1:
                                sp.wait_ge(out_out[(g - 1) % 2], 16 * ((g - 1) // 2 + 1))
                            sp.wait_ge(S["out_ready"], g + 1)
                            hold(sp, held)
                            sp.dma_start(out[bass.ds(first_row(g), GR), :].rearrange("(p t) d -> p t d", t=G), out_sb[:, slot % 2]).then_inc(out_out[slot % 2], 16)
                    pipeline(sp, NGN, WAYS + 1, lambda new, a, b, c, old: half(new, old), WAYS)
                    for n in range(2):
                        sp.wait_ge(out_out[n], 16 * ((NGN - n + 1) // 2))

                @block.gpsimd
                def _(pool):
                    def gather(new):
                        g, slot, use = new
                        at_least(pool, agg_in[slot], 16 * G * use)
                        nc.gpsimd.tensor_copy(at_n[:, slot], node_row[:, bass.ds(g, 1), :].rearrange("p a t -> p (a t)")).then_inc(S["at_ready"], 1)
                        at_least(pool, S["base_ready"], g - WAYS + 1)
                        at_least(pool, S["mixed_ready"], g - WAYS + 1)
                        pool.wait_ge(S["at_ready"], g + 1)
                        hold(pool, held)
                        for k in range(G):
                            pool.indirect_dma_start(out=agg[:, slot, k], out_offset=None, in_=rows1,
                                                    in_offset=bass.IndirectOffsetOnAxis(ap=at_n[:, slot, k:k + 1], axis=0)).then_inc(agg_in[slot], 16)
                    pipeline(pool, NGN, 1, gather, WAYS)

                @block.scalar
                def _(act):
                    a = nc.scalar

                    def half(ahead, new):
                        if ahead:
                            g, slot, use = ahead
                            act.wait_ge(S["tab_ready"], 2 * g + 2)
                            act.wait_ge(x1_in[slot], 16 * (use + 1))
                            at_least(act, S["hb_ready"], g - 1)
                            at_least(act, S["mixed_ready"], g - 1)
                            for k in range(G):
                                last = a.activation(h2[:, slot % 2, k], x1_sb[:, slot, k], ACT.Relu, bias=norm[:, slot, 1, k:k + 1], scale=norm[:, slot, 0, k:k + 1])
                            last.then_inc(S["h2_ready"], 1)
                        if new:
                            g, slot, use = new
                            for q in range(2):
                                act.wait_ge(S["turned"], 2 * g + q + 1)
                                at_least(act, S["multiplied"], 2 * (g - 1) + q + 1)
                                a.activation(m_t[:, q].rearrange("p a b -> p (a b)"), p_mt[q][:, :], ACT.Copy).then_inc(S["copied"], 1)
                    pipeline(act, NGN, 2, half, WAYS)

                @block.tensor
                def _(pe):
                    t_ = nc.tensor

                    def half(new):
                        g, slot, use = new
                        pe.wait_ge(S["mixed_ready"], g + 1)
                        for q in range(2):
                            at_least(pe, S["copied"], 2 * (g - 1) + q + 1)
                            for k in range(4):
                                last = t_.transpose(p_mt[q][:, k * P:(k + 1) * P], mixed[:, 4 * q + k], ident[:])
                            last.then_inc(S["turned"], 1)
                        for q in range(2):
                            pe.wait_ge(S["copied"], 2 * g + q + 1)
                            at_least(pe, S["total_ready"], 2 * (g - 1) + q + 1)
                            for k in range(4):
                                last = t_.matmul(p_w[q][:, k * D:(k + 1) * D], m_t[:, q, k], wl_t[:], start=True, stop=True)
                            last.then_inc(S["multiplied"], 1)
                    pipeline(pe, NGN, 1, half, WAYS)

                @block.vector
                def _(dve):
                    v = nc.vector

                    def half(ahead, new, old):
                        if ahead:
                            g, slot, use = ahead
                            at_least(dve, S["out_ready"], g - WAYS + 1)
                            at_least(dve, S["h2_ready"], g - WAYS + 1)
                            v.tensor_copy(norm[:, slot], stats2[:, bass.ds(g, 1)].rearrange("p a b c -> p (a b) c")).then_inc(S["tab_ready"], 1)
                            v.tensor_copy(dinv_g[:, slot], dinv[:, bass.ds(g, 1)].rearrange("p a t -> p (a t)")).then_inc(S["tab_ready"], 1)
                        if new:
                            g, slot, use = new
                            dve.wait_ge(S["h2_ready"], g + 1)
                            dve.wait_ge(agg_in[slot], 16 * G * (use + 1))
                            at_least(dve, S["turned"], 2 * g)
                            v.tensor_tensor(mixed[:], h2[:, slot % 2], agg[:, slot, :, 0:D], ALU.mult).then_inc(S["mixed_ready"], 1)
                            v.tensor_tensor(base[:, slot % 2], h2[:, slot % 2], bl_row[:].unsqueeze(1).broadcast_to([P, G, D]), ALU.add).then_inc(S["hb_ready"], 1)
                            dve.wait_ge(S["hb_ready"], g + 1)
                            v.tensor_tensor(base[:, slot % 2], base[:, slot % 2], agg[:, slot, :, D:ROW1].broadcast_to([P, G, D]), ALU.mult).then_inc(S["base_ready"], 1)
                        if old:
                            g, slot, use = old
                            dve.wait_ge(S["base_ready"], g + 1)
                            for q in range(2):
                                dve.wait_ge(S["multiplied"], 2 * g + q + 1)
                                v.tensor_tensor(total[:, 4 * q:4 * q + 4].rearrange("p a b -> p (a b)"), p_w[q][:, :],
                                                base[:, slot % 2, 4 * q:4 * q + 4].rearrange("p a b -> p (a b)"), ALU.add).then_inc(S["total_ready"], 1)
                            dve.wait_ge(S["total_ready"], 2 * g + 2)
                            v.scalar_tensor_tensor(leaky[:], total[:], 0.01, total[:], ALU.mult, ALU.max).then_inc(S["leaky_ready"], 1)
                            dve.wait_ge(S["leaky_ready"], g + 1)
                            at_least(dve, out_out[slot % 2], 16 * (2 * use + slot // 2))
                            for k in range(G):
                                last = v.scalar_tensor_tensor(out_sb[:, slot % 2, k], leaky[:, k], dinv_g[:, slot, k:k + 1], x1_sb[:, slot, k], ALU.mult, ALU.add)
                            last.then_inc(S["out_ready"], 1)
                    pipeline(dve, NGN, 3, half, WAYS)


_INS = ["x", "src", "dst", "edge_attr_4", "L0_gnn_ln1_g", "L0_gnn_ln1_b", "L0_gnn_Wq", "L0_gnn_bq", "L0_gnn_Wk", "L0_gnn_bk",
        "L0_gnn_Wv", "L0_gnn_bv", "L0_gnn_We", "L0_gnn_Wskip", "L0_gnn_bskip", "L0_gnn_Wbeta", "L0_gnn_ln2_g", "L0_gnn_ln2_b",
        "L0_gnn_W1", "L0_gnn_b1", "L0_gnn_W2", "L0_gnn_b2", "L1_gnn_W1_w", "L1_gnn_W1_b"]


def kernel(**inputs):
    import numpy as _np
    import concourse.bacc as _bacc
    from concourse import mybir as _mybir
    from concourse.bass_utils import run_bass_kernel_spmd as _run

    nc = _bacc.Bacc("TRN2", target_bir_lowering=False, num_devices=1)
    arrays, args = {}, []
    for name in _INS:
        a = _np.ascontiguousarray(inputs[name])
        arrays[f"in_{name}_dram"] = a
        args.append(nc.dram_tensor(f"in_{name}_dram", a.shape, _mybir.dt.from_np(a.dtype), kind="ExternalInput").ap())
    shape = arrays["in_x_dram"].shape
    args.append(nc.dram_tensor("out_0_dram", shape, _mybir.dt.float32, kind="ExternalOutput").ap())
    build(nc, *args)
    r = _run(nc, [arrays], core_ids=[0])
    return r.results[0]["out_0_dram"]
```
